# Optimizing a Trainium2 kernel written in Bass

```python
import numpy as np
import jax
import jax.numpy as jnp

def _softmax(x, axis=-1):
    return jax.nn.softmax(x, axis=axis)

def _gelu(x):
    return jax.nn.gelu(x, approximate=True)

def _silu(x):
    return jax.nn.silu(x)

def _sigmoid(x):
    return jax.nn.sigmoid(x)

def _layernorm(x, axis=-1, eps=1e-05):
    m = jnp.mean(x, axis=axis, keepdims=True)
    v = jnp.var(x, axis=axis, keepdims=True)
    return (x - m) / jnp.sqrt(v + eps)

def _scatter_add(tgt, idx, src, axis=0):
    return tgt.at[idx].add(src)

def _segment_sum(src, seg, n):
    return jax.ops.segment_sum(src, seg, n)
kernel_name = 'mk_gnn_ffn_d2_gnn_r16_41ebc5'

def setup_inputs(seed: int=0):
    np.random.seed(seed)
    _w = jnp.asarray

    def _rec_inputs():
        import jax
        import jax.numpy as jnp
        _gk = jax.random.key(seed)
        x = -0.0002117 + 1 * jax.random.normal(jax.random.fold_in(_gk, 1), (6250, 256), jnp.float32)
        src = jax.random.randint(jax.random.fold_in(_gk, 2), (100000,), 0, 6250, jnp.int32)
        dst = jax.random.randint(jax.random.fold_in(_gk, 3), (100000,), 0, 6250, jnp.int32)
        _o = jnp.argsort(dst, stable=True)
        src = src[_o]
        dst = dst[_o]
        edge_weight = jax.random.uniform(jax.random.fold_in(_gk, 12), (100000,), jnp.float32, 0.0, 1)
        return (x, src, dst, edge_weight)
    x, src, dst, edge_weight = _rec_inputs()

    def _L0_gnn_setup():
        import jax, jax.numpy as jnp
        import numpy as np
        N = 6250
        E = 200000
        D_IN = 256
        D_OUT = 256
        key = jax.random.key(seed)
        k = jax.random.split(key, 8)
        stdv = 1.0 / np.sqrt(D_OUT)
        x = jax.random.normal(k[0], (N, D_IN), dtype=jnp.float32)
        edge_row = jax.random.randint(k[1], (E,), 0, N, dtype=jnp.int32)
        edge_col = jax.random.randint(k[2], (E,), 0, N, dtype=jnp.int32)
        edge_val = jax.random.uniform(k[3], (E,), dtype=jnp.float32)
        weight_l = jax.random.uniform(k[4], (D_IN, D_OUT), minval=-stdv, maxval=stdv, dtype=jnp.float32)
        bias_l = jax.random.uniform(k[5], (D_OUT,), minval=-stdv, maxval=stdv, dtype=jnp.float32)
        weight_r = jax.random.uniform(k[6], (D_IN, D_OUT), minval=-stdv, maxval=stdv, dtype=jnp.float32)
        bias_r = jax.random.uniform(k[7], (D_OUT,), minval=-stdv, maxval=stdv, dtype=jnp.float32)
        return {'x': x, 'edge_row': edge_row, 'edge_col': edge_col, 'edge_val': edge_val, 'weight_l': weight_l, 'bias_l': bias_l, 'weight_r': weight_r, 'bias_r': bias_r}
    _L0_gnn_all = _L0_gnn_setup()
    _L0_gnn_in = {k: v for k, v in _L0_gnn_all.items() if k in ('weight_l', 'bias_l', 'weight_r', 'bias_r')}
    del _L0_gnn_all

    def _L0_ffn_setup():
        import jax, jax.numpy as jnp
        import numpy as np
        BN_EPS = 0.001

        def _bn(h, g, b, m, v):
            return g * (h - m) * jax.lax.rsqrt(v + BN_EPS) + b
        key = jax.random.key(seed)
        ks = jax.random.split(key, 8)
        B, F, Df = (256, 64, 256)
        E, H, D = (8, 256, 256)
        s1 = 1.0 / np.sqrt(Df)
        s2 = 1.0 / np.sqrt(H)
        return {'x': jax.random.normal(ks[0], (B, F, Df), jnp.float32), 'Wr': jax.random.normal(ks[1], (Df, E), jnp.float32) * s1, 'br': jnp.zeros((E,), jnp.float32), 'W1': jax.random.normal(ks[2], (E, Df, H), jnp.float32) * s1, 'b1': jnp.zeros((E, H), jnp.float32), 'g1': jnp.ones((E, H), jnp.float32), 'be1': jnp.zeros((E, H), jnp.float32), 'm1': jnp.zeros((E, H), jnp.float32), 'v1': jnp.ones((E, H), jnp.float32), 'W2': jax.random.normal(ks[3], (E, H, H), jnp.float32) * s2, 'b2': jnp.zeros((E, H), jnp.float32), 'g2': jnp.ones((E, H), jnp.float32), 'be2': jnp.zeros((E, H), jnp.float32), 'm2': jnp.zeros((E, H), jnp.float32), 'v2': jnp.ones((E, H), jnp.float32), 'Wo': jax.random.normal(ks[4], (E, H, D), jnp.float32) * s2, 'bo': jnp.zeros((E, D), jnp.float32)}
    _L0_ffn_all = _L0_ffn_setup()
    _L0_ffn_in = {k: v for k, v in _L0_ffn_all.items() if k in ('Wr', 'br', 'W1', 'b1', 'g1', 'be1', 'm1', 'v1', 'W2', 'b2', 'g2', 'be2', 'm2', 'v2', 'Wo', 'bo')}
    del _L0_ffn_all

    def _L1_gnn_setup():
        import jax, jax.numpy as jnp
        import numpy as np
        N_NODES = 6250
        N_EDGES = 200000
        IN_DIM = 256
        OUT_DIM = 256
        key = jax.random.key(seed)
        k1, k2, k3, k4, k5 = jax.random.split(key, 5)
        x = jax.random.normal(k1, (N_NODES, IN_DIM), dtype=jnp.float32)
        edge_src = jax.random.randint(k2, (N_EDGES,), 0, N_NODES, dtype=jnp.int32)
        edge_dst = jax.random.randint(k3, (N_EDGES,), 0, N_NODES, dtype=jnp.int32)
        edge_val = jax.random.uniform(k4, (N_EDGES,), dtype=jnp.float32)
        weight = jax.random.uniform(k5, (IN_DIM, OUT_DIM), dtype=jnp.float32)
        bias = jnp.full((OUT_DIM,), 0.3, dtype=jnp.float32)
        return {'x': x, 'edge_src': edge_src, 'edge_dst': edge_dst, 'edge_val': edge_val, 'weight': weight, 'bias': bias}
    _L1_gnn_all = _L1_gnn_setup()
    _L1_gnn_in = {k: v for k, v in _L1_gnn_all.items() if k in ('weight', 'bias')}
    del _L1_gnn_all

    def _L1_ffn_setup():
        import jax, jax.numpy as jnp
        import numpy as np
        B, K, D = (512, 16, 256)
        E = 32
        H = int(D * 0.25)
        key = jax.random.key(seed)
        ks = jax.random.split(key, 7)
        d_rs = D ** (-0.5)
        h_rs = H ** (-0.5)
        x = jax.random.normal(ks[0], (B, K, D), dtype=jnp.float32)
        router_w = jax.random.uniform(ks[1], (E, D), jnp.float32, -d_rs, d_rs)
        router_b = jax.random.uniform(ks[2], (E,), jnp.float32, -d_rs, d_rs)
        W1 = jax.random.uniform(ks[3], (E, D, H), jnp.float32, -h_rs, h_rs)
        b1 = jax.random.uniform(ks[4], (E, H), jnp.float32, -h_rs, h_rs)
        W2 = jax.random.uniform(ks[5], (E, H, D), jnp.float32, -d_rs, d_rs)
        b2 = jax.random.uniform(ks[6], (E, D), jnp.float32, -d_rs, d_rs)
        return {'x': x, 'router_w': router_w, 'router_b': router_b, 'W1': W1, 'b1': b1, 'W2': W2, 'b2': b2}
    _L1_ffn_all = _L1_ffn_setup()
    _L1_ffn_in = {k: v for k, v in _L1_ffn_all.items() if k in ('router_w', 'router_b', 'W1', 'b1', 'W2', 'b2')}
    del _L1_ffn_all
    return {'x': x, 'src': src, 'dst': dst, 'edge_weight': edge_weight, 'L0_gnn_weight_l': _L0_gnn_in['weight_l'], 'L0_gnn_bias_l': _L0_gnn_in['bias_l'], 'L0_gnn_weight_r': _L0_gnn_in['weight_r'], 'L0_gnn_bias_r': _L0_gnn_in['bias_r'], 'L0_ffn_Wr': _L0_ffn_in['Wr'], 'L0_ffn_br': _L0_ffn_in['br'], 'L0_ffn_W1': _L0_ffn_in['W1'], 'L0_ffn_b1': _L0_ffn_in['b1'], 'L0_ffn_g1': _L0_ffn_in['g1'], 'L0_ffn_be1': _L0_ffn_in['be1'], 'L0_ffn_m1': _L0_ffn_in['m1'], 'L0_ffn_v1': _L0_ffn_in['v1'], 'L0_ffn_W2': _L0_ffn_in['W2'], 'L0_ffn_b2': _L0_ffn_in['b2'], 'L0_ffn_g2': _L0_ffn_in['g2'], 'L0_ffn_be2': _L0_ffn_in['be2'], 'L0_ffn_m2': _L0_ffn_in['m2'], 'L0_ffn_v2': _L0_ffn_in['v2'], 'L0_ffn_Wo': _L0_ffn_in['Wo'], 'L0_ffn_bo': _L0_ffn_in['bo'], 'L1_gnn_weight': _L1_gnn_in['weight'], 'L1_gnn_bias': _L1_gnn_in['bias'], 'L1_ffn_router_w': _L1_ffn_in['router_w'], 'L1_ffn_router_b': _L1_ffn_in['router_b'], 'L1_ffn_W1': _L1_ffn_in['W1'], 'L1_ffn_b1': _L1_ffn_in['b1'], 'L1_ffn_W2': _L1_ffn_in['W2'], 'L1_ffn_b2': _L1_ffn_in['b2']}

def reference(x, src, dst, edge_weight, L0_gnn_weight_l, L0_gnn_bias_l, L0_gnn_weight_r, L0_gnn_bias_r, L0_ffn_Wr, L0_ffn_br, L0_ffn_W1, L0_ffn_b1, L0_ffn_g1, L0_ffn_be1, L0_ffn_m1, L0_ffn_v1, L0_ffn_W2, L0_ffn_b2, L0_ffn_g2, L0_ffn_be2, L0_ffn_m2, L0_ffn_v2, L0_ffn_Wo, L0_ffn_bo, L1_gnn_weight, L1_gnn_bias, L1_ffn_router_w, L1_ffn_router_b, L1_ffn_W1, L1_ffn_b1, L1_ffn_W2, L1_ffn_b2):
    import jax
    import jax.numpy as jnp

    def _L0_gnn_ref(x, edge_row, edge_col, edge_val, weight_l, bias_l, weight_r, bias_r):
        import jax, jax.numpy as jnp
        import numpy as np
        N = 6250
        E = 200000
        D_IN = 256
        D_OUT = 256
        h = x @ weight_l
        msgs = edge_val[:, None] * h[edge_col]
        agg = jax.ops.segment_sum(msgs, edge_row, num_segments=N)
        out = agg + bias_l
        out = out + x @ weight_r + bias_r
        return out

    def _L0_ffn_ref(x, Wr, br, W1, b1, g1, be1, m1, v1, W2, b2, g2, be2, m2, v2, Wo, bo):
        import jax, jax.numpy as jnp
        import numpy as np
        BN_EPS = 0.001

        def _bn(h, g, b, m, v):
            return g * (h - m) * jax.lax.rsqrt(v + BN_EPS) + b
        feat = jnp.mean(x, axis=0)
        w = jax.nn.softmax(feat @ Wr + br, axis=-1)
        h = jnp.einsum('bfd,edh->bfeh', x, W1) + b1
        h = jax.nn.relu(_bn(h, g1, be1, m1, v1))
        h = jnp.einsum('bfeh,ehk->bfek', h, W2) + b2
        h = jax.nn.relu(_bn(h, g2, be2, m2, v2))
        y = jnp.einsum('bfeh,ehd->bfed', h, Wo) + bo
        return jnp.einsum('bfed,fe->bfd', y, w)

    def _L1_gnn_ref(x, edge_src, edge_dst, edge_val, weight, bias):
        import jax, jax.numpy as jnp
        import numpy as np
        N_NODES = 6250
        N_EDGES = 200000
        IN_DIM = 256
        OUT_DIM = 256
        h = x @ weight
        msgs = edge_val[:, None] * h[edge_src]
        agg = jax.ops.segment_sum(msgs, edge_dst, num_segments=N_NODES)
        return agg + bias

    def _L1_ffn_ref(x, router_w, router_b, W1, b1, W2, b2):
        import jax, jax.numpy as jnp
        import numpy as np
        B, K, D = (512, 16, 256)
        E = 32
        H = int(D * 0.25)
        xf = x.reshape(-1, D)
        logits = xf @ router_w.T + router_b
        idx = jnp.argmax(logits, axis=-1)
        w1t = jnp.take(W1, idx, axis=0)
        h = jnp.einsum('nd,ndh->nh', xf, w1t) + jnp.take(b1, idx, axis=0)
        h = jax.nn.relu(h)
        w2t = jnp.take(W2, idx, axis=0)
        out = jnp.einsum('nh,nhd->nd', h, w2t) + jnp.take(b2, idx, axis=0)
        out = jax.nn.relu(out)
        return out.reshape(x.shape)
    x = x + _L0_gnn_ref(_layernorm(x, axis=-1), src, dst, edge_weight, L0_gnn_weight_l, L0_gnn_bias_l, L0_gnn_weight_r, L0_gnn_bias_r)
    x = x + _L0_ffn_ref(_layernorm(x, axis=-1)[None], L0_ffn_Wr, L0_ffn_br, L0_ffn_W1, L0_ffn_b1, L0_ffn_g1, L0_ffn_be1, L0_ffn_m1, L0_ffn_v1, L0_ffn_W2, L0_ffn_b2, L0_ffn_g2, L0_ffn_be2, L0_ffn_m2, L0_ffn_v2, L0_ffn_Wo, L0_ffn_bo)[0]
    x = x + _L1_gnn_ref(_layernorm(x, axis=-1), src, dst, edge_weight, L1_gnn_weight, L1_gnn_bias)
    x = x + _L1_ffn_ref(_layernorm(x, axis=-1)[None], L1_ffn_router_w, L1_ffn_router_b, L1_ffn_W1, L1_ffn_b1, L1_ffn_W2, L1_ffn_b2)[0]
    return x

_drawn_inputs = setup_inputs


def setup_inputs(seed=0):
    import zlib

    import numpy as np

    out = dict(_drawn_inputs(seed))
    spreads = {'L0_ffn_br': (0.0, 0.1),
     'L0_ffn_b1': (0.0, 0.408),
     'L0_ffn_g1': (1.0, 0.2),
     'L0_ffn_be1': (0.0, 0.403),
     'L0_ffn_m1': (0.0, 0.394),
     'L0_ffn_v1': (1.0, 0.6),
     'L0_ffn_b2': (0.0, 0.1),
     'L0_ffn_g2': (1.0, 0.2),
     'L0_ffn_be2': (0.0, 0.1),
     'L0_ffn_m2': (0.0, 0.1),
     'L0_ffn_v2': (1.0, 0.588),
     'L0_ffn_bo': (0.0, 0.1),
     'L1_gnn_bias': (0.30000001192092896, 0.6)}
    factors = {'L1_ffn_router_w': 5.711,
     'L1_ffn_router_b': 8.0,
     'L1_ffn_W1': 6.647,
     'L1_ffn_b1': 8.0,
     'L1_ffn_W2': 5.75,
     'L1_ffn_b2': 35.474}
    for name, (base, spread) in spreads.items():
        noise = np.random.default_rng([zlib.crc32(name.encode()), seed]).standard_normal(out[name].shape)
        drawn = base * np.exp(spread * noise) if base else spread * noise
        out[name] = jnp.asarray(drawn.astype(out[name].dtype))
    for name, factor in factors.items():
        out[name] = (out[name] * factor).astype(out[name].dtype)
    return out
```

```python
from contextlib import ExitStack

import numpy as np
import concourse.bass as bass
from concourse import mybir

F32 = mybir.dt.float32
F32R = mybir.dt.float32r
BF16 = mybir.dt.bfloat16
I32 = mybir.dt.int32
U32 = mybir.dt.uint32
ALU = mybir.AluOpType
ACT = mybir.ActivationFunctionType
AX = mybir.AxisListType

P = 128
N_NODES = 6250
D = 256
F = D // P
E_EDGES = 100000
EXPERTS0 = 8
EXPERTS1 = 32
HID1 = 64
PAIRS = EXPERTS1 * HID1 // P

GT = 7
GROUPS = 7
ROWS = GROUPS * GT * P
SUBS = ((0, 4), (4, 3))
W4 = 4 * P

U = 4
EDGE_TILES = 784
E_PAD = EDGE_TILES * P
EGROUPS = EDGE_TILES // U
TR = EDGE_TILES // GT
TABLE_ROWS = ROWS + P
LN_EPS = 1e-5
BN_EPS = 1e-3


def build(nc, x, src, dst, wgt, wl, wr, bl, br, gw, gbr, w1, b1, g1, be1, m1, v1,
          w2, b2, g2, be2, m2, v2, wo, bo, lw, lb, rw, rb, mw1, mb1, mw2, mb2, out):
    ctx = ExitStack()
    with ctx:
        def sb(name, shape, dt=F32):
            return ctx.enter_context(nc.sbuf_tensor(name, shape, dt))

        def sem(name):
            return ctx.enter_context(nc.semaphore(name))

        h_tab = [nc.dram_tensor(f"h_tab{i}", (ROWS, D), F32, kind="Internal").ap() for i in range(2)]
        acc_tab = [[nc.dram_tensor(f"acc_tab{i}_{u}", (TABLE_ROWS, D), F32, kind="Internal").ap()
                    for u in range(U)] for i in range(2)]

        ident = sb("ident", [P, P])
        lower = sb("lower", [P, P])
        dump_row = sb("dump_row", [P, 1])
        src_f = sb("src_f", [P, EDGE_TILES])
        dst_f = sb("dst_f", [P, EDGE_TILES])
        wgt_f = sb("wgt_f", [P, EDGE_TILES])

        bank = [ctx.enter_context(nc.psum_tensor(f"bank{i}", [P, 512], F32)) for i in range(8)]

        acc = sb("acc", [P, GT, D])
        part = sb("part", [P, GT, D])
        xn = sb("xn", [P, GT, D])
        stat = sb("stat", [P, GT, 6])
        mv = sb("mv", [P, GT, 2])
        ve = sb("ve", [P, GT])
        rstd = sb("rstd", [P, GT])
        tmp7 = sb("tmp7", [P, GT])

        s_apart = sem("s_apart")

        def wait_apart(eng, semaphore, value):
            eng.wait_ge(semaphore, value)
            eng.sem_inc(s_apart, 1)

        def node_rows(table, g):
            return table[bass.ds(g * (GT * P), GT * P), :].rearrange("(k p) d -> p k d", p=P)

        class LN:
            def __init__(s, n):
                s.stats = sem(f"{n}_stats")
                s.aggr = sem(f"{n}_aggr")
                s.var = sem(f"{n}_var")
                s.sd = sem(f"{n}_sd")
                s.newton = sem(f"{n}_newton")
                s.xn = sem(f"{n}_xn")
                s.tr = sem(f"{n}_tr")
                s.xt = sem(f"{n}_xt")

        def ln_vector(dve, g, s):
            for k in range(GT):
                last = nc.vector.bn_stats(stat[:, k, :], acc[:, k, :])
            last.then_inc(s.stats, 1)
            wait_apart(dve, s.stats, g + 1)
            for k in range(GT):
                last = nc.vector.bn_aggr(mv[:, k, :], stat[:, k, :])
            last.then_inc(s.aggr, 1)
            dve.wait_ge(s.aggr, g + 1)
            nc.vector.tensor_scalar(ve[:, :], mv[:, :, 1], LN_EPS, None, ALU.add).then_inc(s.var, 1)
            dve.wait_ge(s.sd, g + 1)
            nc.vector.reciprocal(rstd[:, :], rstd[:, :]).then_inc(s.newton, 1)
            dve.wait_ge(s.newton, g * 5 + 1)
            nc.vector.tensor_tensor(tmp7[:, :], rstd[:, :], rstd[:, :], ALU.mult).then_inc(s.newton, 1)
            dve.wait_ge(s.newton, g * 5 + 2)
            nc.vector.tensor_tensor(tmp7[:, :], tmp7[:, :], ve[:, :], ALU.mult).then_inc(s.newton, 1)
            dve.wait_ge(s.newton, g * 5 + 3)
            nc.vector.tensor_scalar(tmp7[:, :], tmp7[:, :], -0.5, 1.5, ALU.mult, ALU.add).then_inc(s.newton, 1)
            dve.wait_ge(s.newton, g * 5 + 4)
            nc.vector.tensor_tensor(rstd[:, :], rstd[:, :], tmp7[:, :], ALU.mult).then_inc(s.newton, 1)
            dve.wait_ge(s.newton, g * 5 + 5)
            dve.wait_ge(s.tr, g * GT)
            for k in range(GT):
                nc.vector.tensor_scalar(xn[:, k, :], acc[:, k, :], mv[:, k, 0:1], rstd[:, k:k + 1],
                                        ALU.subtract, ALU.mult).then_inc(s.xn, 1)

        def ln_root(act, g, s):
            act.wait_ge(s.var, g + 1)
            act.wait_ge(s.xn, g * GT)
            nc.scalar.activation(rstd[:, :], ve[:, :], ACT.Sqrt).then_inc(s.sd, 1)

        def ln_transpose(pe, g, s):
            for k in range(GT):
                pe.wait_ge(s.xn, g * GT + k + 1)
                pe.wait_ge(s.xt, g * GT + (k - 1 if k >= 2 else 0))
                for f in range(F):
                    last = nc.tensor.transpose(bank[k % 2][:, f * P:(f + 1) * P],
                                               xn[:, k, f * P:(f + 1) * P], ident[:, :])
                last.then_inc(s.tr, 1)

        def transposed(k):
            return bank[k % 2][:, 0:D].rearrange("p (f t) -> p f t", f=F)

        with ExitStack() as c1:
            def sb1(name, shape, dt=F32):
                return c1.enter_context(nc.sbuf_tensor(name, shape, dt))

            s_const = sem("s_const")
            s_zero = sem("s_zero")
            s_ezero = sem("s_ezero")
            s_eload = sem("s_eload")
            s_econv = sem("s_econv")
            s_etr = sem("s_etr")
            s_ecol = sem("s_ecol")
            s_w1 = sem("s_w1")
            s_bsum = sem("s_bsum")
            s_xin = sem("s_xin")
            s_mm = sem("s_mm")
            s_hcopy = sem("s_hcopy")
            s_hst = sem("s_hst")
            s_add1 = sem("s_add1")
            s_add2 = sem("s_add2")
            s_bst = sem("s_bst")
            s_idx = sem("s_idx")
            ln1 = LN("ln1")

            with ExitStack() as cc, nc.Block() as block:
                erow_i = sb1("erow_i", [TR, 3, GT, P], I32)
                erow_f = sb1("erow_f", [TR, 2, GT, P])
                wlr = sb1("wlr", [P, F, 2, D])
                biases = sb1("biases", [P, 2, D])
                xnt = sb1("xnt", [P, F, GT * P])
                hbuf = sb1("hbuf", [P, GT, D])
                base = sb1("base", [P, GT, D])
                zeros = sb1("zeros", [P, 2560])
                idx_p = sb1("idx_p", [P, 1], I32)
                idx_q = sb1("idx_q", [P, P], I32)

                @block.gpsimd
                def _(pool):
                    nc.gpsimd.memset(ident[:, :], 0.0).then_inc(s_idx, 1)
                    nc.gpsimd.memset(lower[:, :], 1.0).then_inc(s_idx, 1)
                    pool.wait_ge(s_idx, 2)
                    nc.gpsimd.affine_select(out=ident[:, :], in_=ident[:, :], compare_op=ALU.not_equal,
                                            fill=1.0, base=0, pattern=[[-1, P]],
                                            channel_multiplier=1).then_inc(s_const, 1)
                    nc.gpsimd.affine_select(out=lower[:, :], in_=lower[:, :], compare_op=ALU.is_gt,
                                            fill=0.0, base=0, pattern=[[-1, P]],
                                            channel_multiplier=1).then_inc(s_const, 1)
                    nc.gpsimd.iota(idx_p[:, :], pattern=[[0, 1]], base=ROWS,
                                   channel_multiplier=1).then_inc(s_const, 1)
                    nc.gpsimd.memset(zeros[:, :], 0.0).then_inc(s_zero, 1)

                @block.sync
                def _(sp):
                    for n, a in enumerate((src, dst, wgt)):
                        to = erow_i[:, n] if n < 2 else erow_i[:, n].bitcast(F32)
                        sp.dma_start(to, a.rearrange("(j r p) -> r j p", r=TR, p=P)).then_inc(s_eload, 16)
                    sp.dma_start(wlr[:, :, 0, :], wl.rearrange("(f p) d -> p f d", p=P)).then_inc(s_w1, 16)
                    sp.dma_start(wlr[:, :, 1, :], wr.rearrange("(f p) d -> p f d", p=P)).then_inc(s_w1, 16)
                    sp.dma_start(biases[:, 0, :], bl.partition_broadcast(P)).then_inc(s_w1, 16)
                    sp.dma_start(biases[:, 1, :], br.partition_broadcast(P)).then_inc(s_w1, 16)
                    with sp.Fori(0, GROUPS) as g:
                        wait_apart(sp, s_add1, g * GT)
                        sp.dma_start(acc[:, :, :], node_rows(x, g)).then_inc(s_xin, 16)
                        wait_apart(sp, s_hcopy, g * GT + GT)
                        sp.dma_start(node_rows(h_tab[0], g), hbuf[:, :, :]).then_inc(s_hst, 16)
                        wait_apart(sp, s_add2, g + 1)
                        sp.dma_start(node_rows(acc_tab[0][0], g), base[:, :, :]).then_inc(s_bst, 16)
                    sp.wait_ge(s_hst, 16 * GROUPS)
                    sp.wait_ge(s_bst, 16 * GROUPS)
                    sp.wait_ge(s_ezero, 16 * 32)

                @block.scalar
                def _(act):
                    act.wait_ge(s_zero, 1)
                    for i in range(2):
                        for u in range(U):
                            if u:
                                flat = acc_tab[i][u].rearrange("(p r) d -> p (r d)", p=P)
                                for c in range(5):
                                    act.dma_start(flat[:, c * 2560:(c + 1) * 2560], zeros[:, :]).then_inc(s_ezero, 16)
                            else:
                                act.dma_start(acc_tab[i][0][ROWS:TABLE_ROWS, :], zeros[:, 0:D]).then_inc(s_ezero, 16)
                    for n, col in enumerate((src_f, dst_f, wgt_f)):
                        for j in range(GT):
                            act.wait_ge(s_etr, n * GT + j + 1)
                            nc.scalar.activation(col[:, j * TR:(j + 1) * TR],
                                                 bank[(n * GT + j) % 2][:, 0:TR], ACT.Copy).then_inc(s_ecol, 1)
                    with act.Fori(0, GROUPS) as g:
                        ln_root(act, g, ln1)
                        for k in range(GT):
                            act.wait_ge(ln1.tr, g * GT + k + 1)
                            act.wait_ge(s_mm, g * GT)
                            nc.scalar.activation(xnt[:, :, k * P:(k + 1) * P], transposed(k),
                                                 ACT.Copy).then_inc(ln1.xt, 1)
                        act.wait_ge(s_hst, g * 16)
                        for k in range(GT):
                            act.wait_ge(s_mm, g * GT + k + 1)
                            nc.scalar.activation(hbuf[:, k, :], bank[2 + k % 2][:, 0:D],
                                                 ACT.Copy).then_inc(s_hcopy, 1)

                @block.tensor
                def _(pe):
                    pe.wait_ge(s_const, 1)
                    for n in range(3):
                        for j in range(GT):
                            i = n * GT + j
                            if n < 2:
                                pe.wait_ge(s_econv, n + 1)
                                rows = erow_f[:, n, j, :]
                            else:
                                pe.wait_ge(s_eload, 48)
                                rows = erow_i[:, 2, j, :].bitcast(F32)
                            if i >= 2:
                                pe.wait_ge(s_ecol, i - 1)
                            nc.tensor.transpose(bank[i % 2][:, 0:TR], rows,
                                                ident[0:TR, 0:TR]).then_inc(s_etr, 1)
                    pe.wait_ge(s_ecol, 3 * GT)
                    pe.wait_ge(s_w1, 64)
                    with pe.Fori(0, GROUPS) as g:
                        ln_transpose(pe, g, ln1)
                        for k in range(GT):
                            pe.wait_ge(ln1.xt, g * GT + k + 1)
                            done = g * GT + (k - 1 if k >= 2 else 0)
                            pe.wait_ge(s_hcopy, done)
                            pe.wait_ge(s_add1, done)
                            for w in range(2):
                                for f in range(F):
                                    last = nc.tensor.matmul(bank[2 + 2 * w + k % 2][:, 0:D],
                                                            xnt[:, f, k * P:(k + 1) * P], wlr[:, f, w, :],
                                                            start=(f == 0), stop=(f == F - 1))
                            last.then_inc(s_mm, 1)

                @block.vector
                def _(dve):
                    dve.wait_ge(s_const, 3)
                    nc.vector.tensor_copy(dump_row[:, :], idx_p[:, :]).then_inc(s_bsum, 1)
                    dve.wait_ge(s_eload, 48)
                    for n in range(2):
                        nc.vector.tensor_copy(erow_f[:, n], erow_i[:, n]).then_inc(s_econv, 1)
                    dve.wait_ge(s_w1, 64)
                    nc.vector.tensor_tensor(biases[:, 0, :], biases[:, 0, :], biases[:, 1, :],
                                            ALU.add).then_inc(s_bsum, 1)
                    dve.wait_ge(s_bsum, 2)
                    with dve.Fori(0, GROUPS) as g:
                        dve.wait_ge(s_xin, g * 16 + 16)
                        ln_vector(dve, g, ln1)
                        dve.wait_ge(s_bst, g * 16)
                        for k in range(GT):
                            dve.wait_ge(s_mm, g * GT + k + 1)
                            nc.vector.tensor_tensor(base[:, k, :], bank[4 + k % 2][:, 0:D], acc[:, k, :],
                                                    ALU.add).then_inc(s_add1, 1)
                        dve.wait_ge(s_add1, g * GT + GT)
                        nc.vector.tensor_tensor(base[:, :, :], base[:, :, :],
                                                biases[:, 0, :].unsqueeze(1).broadcast_to([P, GT, D]),
                                                ALU.add).then_inc(s_add2, 1)

        def edge_block(layer, gather_f, scatter_f, scatter_rows):
            n = f"e{layer}"
            s_row = [sem(f"{n}_row{b}") for b in range(2)]
            s_weights = sem(f"{n}_weights")
            s_count = sem(f"{n}_count")
            s_stage = sem(f"{n}_stage")
            s_gather = [[sem(f"{n}_gather{b}{u}") for u in range(U)] for b in range(2)]
            s_sum = sem(f"{n}_sum")
            s_copy = sem(f"{n}_copy")
            s_scatter = [sem(f"{n}_scatter{u}") for u in range(U)]
            with ExitStack() as c2, nc.Block() as block:
                def sb2(name, shape, dt=F32):
                    return c2.enter_context(nc.sbuf_tensor(f"{n}_{name}", shape, dt))
                row = [sb2(f"row{b}", [P, U * P], I32) for b in range(2)]
                wmat = sb2("wmat", [P, 2, U, P])
                junk = sb2("junk", [P, U, P])
                count = sb2("count", [P, 2, U])
                t_idx = sb2("t_idx", [P, U])
                gidx = [sb2(f"gidx{b}", [P, U], I32) for b in range(2)]
                sidx = [sb2(f"sidx{b}", [P, U], I32) for b in range(2)]
                got = sb2("got", [P, 2, U, D])
                summed = sb2("summed", [P, 2, U, D])
                h = h_tab[layer]
                tabs = acc_tab[layer]

                def later(i):
                    return not isinstance(i, int)

                def pairs_of(eng, body):
                    body(0)
                    with eng.Fori(1, EGROUPS // 2) as i:
                        body(i)

                @block.sync
                def _(sp):
                    def body(i):
                        for b in range(2):
                            if later(i):
                                wait_apart(sp, s_count, i * (2 * U) + (b - 1) * U)
                            sp.dma_start(row[b][:, :], scatter_rows[bass.ds((i * 2 + b) * (U * P), U * P)]
                                         .partition_broadcast(P)).then_inc(s_row[b], 16)
                    pairs_of(sp, body)

                @block.vector
                def _(dve):
                    def body(i):
                        for b in range(2):
                            g = i * 2 + b
                            dve.wait_ge(s_row[b], i * 16 + 16)
                            if later(i):
                                dve.wait_ge(s_sum, g * U - U)
                            for u in range(U):
                                col = g * U + u
                                nc.vector.tensor_scalar(wmat[:, b, u, :], row[b][:, u * P:(u + 1) * P],
                                                        scatter_f[:, bass.ds(col, 1)], wgt_f[:, bass.ds(col, 1)],
                                                        ALU.is_equal, ALU.mult).then_inc(s_weights, 1)
                            dve.wait_ge(s_count, g * U)
                            for u in range(U):
                                col = g * U + u
                                nc.vector.scalar_tensor_tensor(
                                    junk[:, u, :], row[b][:, u * P:(u + 1) * P], scatter_f[:, bass.ds(col, 1)],
                                    lower[:, :], ALU.is_equal, ALU.mult,
                                    accum_out=count[:, b, u:u + 1]).then_inc(s_count, 1)
                            cols = scatter_f[:, bass.ds(g * U, U)]
                            dve.wait_ge(s_stage, g * 4)
                            nc.vector.tensor_scalar(t_idx[:, :], cols, -1.0, dump_row[:, 0:1],
                                                    ALU.mult, ALU.add).then_inc(s_stage, 1)
                            dve.wait_ge(s_count, g * U + U)
                            dve.wait_ge(s_stage, g * 4 + 1)
                            nc.vector.scalar_tensor_tensor(t_idx[:, :], count[:, b, :], 0.0, t_idx[:, :],
                                                           ALU.is_gt, ALU.mult).then_inc(s_stage, 1)
                            dve.wait_ge(s_stage, g * 4 + 2)
                            if later(i):
                                for u in range(U):
                                    dve.wait_ge(s_scatter[u], g * 16 - 16)
                            nc.vector.tensor_tensor(sidx[b][:, :], t_idx[:, :], cols, ALU.add).then_inc(s_stage, 1)
                            nc.vector.tensor_copy(gidx[b][:, :], gather_f[:, bass.ds(g * U, U)]).then_inc(s_stage, 1)
                    pairs_of(dve, body)

                @block.gpsimd
                def _(pool):
                    def gather(i, b, u):
                        g = i * 2 + b
                        if u == 0:
                            pool.wait_ge(s_stage, g * 4 + 4)
                        if later(i):
                            wait_apart(pool, s_sum, g * U - 2 * U + u + 1)
                        nc.gpsimd.indirect_dma_start(
                            got[:, b, u, :], None, h, bass.IndirectOffsetOnAxis(gidx[b][:, u:u + 1], 0),
                            bounds_check=ROWS - 1, oob_is_err=True).then_inc(s_gather[b][u], 16)

                    def scatter(g, b, u, first=False):
                        pool.wait_ge(s_copy, g * U + u + 1)
                        if not first:
                            wait_apart(pool, s_scatter[u], g * 16)
                        nc.gpsimd.indirect_dma_start(
                            tabs[u], bass.IndirectOffsetOnAxis(sidx[b][:, u:u + 1], 0), summed[:, b, u, :],
                            None, bounds_check=TABLE_ROWS - 1, oob_is_err=True,
                            compute_op=ALU.add).then_inc(s_scatter[u], 16)

                    for u in range(U):
                        gather(0, 0, u)
                    for u in range(U):
                        gather(0, 1, u)
                        scatter(0, 0, u, first=True)
                    with pool.Fori(1, EGROUPS // 2) as i:
                        for u in range(U):
                            gather(i, 0, u)
                            scatter(i * 2 - 1, 1, u)
                        for u in range(U):
                            gather(i, 1, u)
                            scatter(i * 2, 0, u)
                    for u in range(U):
                        scatter(EGROUPS - 1, 1, u)
                    for u in range(U):
                        pool.wait_ge(s_scatter[u], EGROUPS * 16)

                @block.tensor
                def _(pe):
                    def body(i):
                        for b in range(2):
                            g = i * 2 + b
                            for u in range(U):
                                pe.wait_ge(s_weights, g * U + u + 1)
                                pe.wait_ge(s_gather[b][u], i * 16 + 16)
                                if later(i):
                                    pe.wait_ge(s_copy, g * U - 2 * U + u + 1)
                                nc.tensor.matmul(bank[b * U + u][:, 0:D], wmat[:, b, u, :], got[:, b, u, :],
                                                 start=True, stop=True).then_inc(s_sum, 1)
                    pairs_of(pe, body)

                @block.scalar
                def _(act):
                    def body(i):
                        for b in range(2):
                            g = i * 2 + b
                            for u in range(U):
                                act.wait_ge(s_sum, g * U + u + 1)
                                if later(i):
                                    act.wait_ge(s_scatter[u], g * 16 - 16)
                                nc.scalar.activation(summed[:, b, u, :], bank[b * U + u][:, 0:D],
                                                     ACT.Copy).then_inc(s_copy, 1)
                    pairs_of(act, body)

        edge_block(0, dst_f, src_f, src)

        class Tables:
            def __init__(s, n):
                s.load = sem(f"{n}_tload")
                s.used = sem(f"{n}_tused")

        def tables_load(sp, g, s, layer, acc_free):
            acc_free()
            sp.dma_start(acc[:, :, :], node_rows(acc_tab[layer][0], g)).then_inc(s.load, 16)
            for u in range(1, U):
                wait_apart(sp, s.load, g * (16 * U) + 16 * u)
                wait_apart(sp, s.used, g * (U - 1) + u - 1)
                sp.dma_start(part[:, :, :], node_rows(acc_tab[layer][u], g)).then_inc(s.load, 16)

        def tables_add(dve, g, s):
            for u in range(1, U):
                dve.wait_ge(s.load, g * (16 * U) + 16 * u + 16)
                if u > 1:
                    dve.wait_ge(s.used, g * (U - 1) + u - 1)
                nc.vector.tensor_tensor(acc[:, :, :], acc[:, :, :], part[:, :, :], ALU.add).then_inc(s.used, 1)
            dve.wait_ge(s.used, g * (U - 1) + U - 1)

        with ExitStack() as c3, nc.Block() as block:
            def sb3(name, shape, dt=F32):
                return c3.enter_context(nc.sbuf_tensor(name, shape, dt))
            s_wraw = sem("f_wraw")
            s_whi = sem("f_whi")
            s_wlo = sem("f_wlo")
            s_small = sem("f_small")
            s_bn = sem("f_bn")
            s_bnroot = sem("f_bnroot")
            ln3 = LN("ln3")
            ln4 = LN("ln4")
            tb3 = Tables("f")
            s_glog = sem("f_glog")
            s_gate = sem("f_gate")
            s_gexp = sem("f_gexp")
            s_gtr = sem("f_gtr")
            s_gt = sem("f_gt")
            s_gbo = sem("f_gbo")
            s_acc0 = sem("f_acc0")
            s_xhi = sem("f_xhi")
            s_xlo = sem("f_xlo")
            s_mm = [sem(f"f_mm{i}") for i in range(3)]
            s_relu = [sem(f"f_relu{i}") for i in range(2)]
            s_hi = [sem(f"f_hi{i}") for i in range(2)]
            s_lo = [sem(f"f_lo{i}") for i in range(2)]
            s_out = sem("f_out")
            s_hmm = sem("f_hmm")
            s_hcopy = sem("f_hcopy")
            s_hst = sem("f_hst")
            s_base = sem("f_base")
            s_bst = sem("f_bst")

            raw = sb3("raw", [P, F, D])
            wsrc = (w1, w2, wo)
            whi = [sb3(f"whi{l}", [P, EXPERTS0, F, D], F32R) for l in range(3)]
            wlo = [sb3(f"wlo{l}", [P, EXPERTS0, F, D], F32R) for l in range(3)]
            bnp = sb3("bnp", [P, 2, 5, EXPERTS0, F])
            scl = sb3("scl", [P, 2, EXPERTS0, F])
            shf = sb3("shf", [P, 2, EXPERTS0, F])
            bnt = sb3("bnt", [P, 2, EXPERTS0, F])
            gws = sb3("gws", [P, F, EXPERTS0])
            gbs = sb3("gbs", [P, EXPERTS0])
            bos = sb3("bos", [EXPERTS0, D])
            lws = sb3("lws", [P, F, D])
            lbs = sb3("lbs", [P, D])
            glog = sb3("glog", [P, GT, EXPERTS0])
            gate = sb3("gate", [P, GT, EXPERTS0])
            gm = sb3("gm", [P, GT])
            gateT = sb3("gateT", [EXPERTS0, GT * P])
            xhi = sb3("xhi", [P, F, GT * P], F32R)
            xlo = sb3("xlo", [P, F, GT * P], F32R)
            xraw = sb3("xraw", [P, F, GT * P])
            rl = sb3("rl", [P, 2, F, W4])
            hhi = [sb3(f"hhi{i}", [P, F, W4], F32R) for i in range(2)]
            hlo = [sb3(f"hlo{i}", [P, F, W4], F32R) for i in range(2)]
            NPIECE = 3 * EXPERTS0
            STEPS = [(si, e) for si in range(len(SUBS)) for e in range(EXPERTS0)]
            NS = len(STEPS)
            OUTS = sum(w for _, w in SUBS) * EXPERTS0

            def tiles_before(j):
                return sum(SUBS[si][1] for si, _ in STEPS[:j])

            def three(pe, outp, hi_l, lo_l, hi_r, lo_r, first, last):
                nc.tensor.matmul(outp, hi_l, hi_r, start=first, stop=False)
                nc.tensor.matmul(outp, lo_l, hi_r, start=False, stop=False)
                return nc.tensor.matmul(outp, hi_l, lo_r, start=False, stop=last)

            @block.sync
            def _(sp):
                for l in range(3):
                    for e in range(EXPERTS0):
                        i = l * EXPERTS0 + e
                        if i:
                            sp.wait_ge(s_wlo, i)
                        sp.dma_start(raw[:, :, :], wsrc[l][e].rearrange("(f p) d -> p f d", p=P)).then_inc(s_wraw, 16)
                with sp.Fori(0, GROUPS) as g:
                    def acc_free():
                        wait_apart(sp, s_bst, g * 16)
                    tables_load(sp, g, tb3, 0, acc_free)
                    wait_apart(sp, s_hcopy, g * GT + GT)
                    sp.dma_start(node_rows(h_tab[1], g), part[:, :, :]).then_inc(s_hst, 16)
                    wait_apart(sp, s_base, g + 1)
                    sp.dma_start(node_rows(acc_tab[1][0], g), acc[:, :, :]).then_inc(s_bst, 16)
                    wait_apart(sp, s_hst, g * 16 + 16)
                sp.wait_ge(s_bst, 16 * GROUPS)

            @block.gpsimd
            def _(pool):
                for l, arrs in enumerate(((b1, g1, be1, m1, v1), (b2, g2, be2, m2, v2))):
                    for a, arr in enumerate(arrs):
                        pool.dma_start(bnp[:, l, a], arr).then_inc(s_small, 16)
                pool.dma_start(gws[:, :, :], gw.rearrange("(f p) e -> p f e", p=P)).then_inc(s_small, 16)
                pool.dma_start(gbs[:, :], gbr.partition_broadcast(P)).then_inc(s_small, 16)
                pool.dma_start(bos[:, :], bo).then_inc(s_small, 16)
                pool.dma_start(lws[:, :, :], lw.rearrange("(f p) d -> p f d", p=P)).then_inc(s_small, 16)
                pool.dma_start(lbs[:, :], lb.partition_broadcast(P)).then_inc(s_small, 16)

            @block.scalar
            def _(act):
                act.wait_ge(s_bn, 1)
                nc.scalar.activation(scl[:, :, :, :], bnt[:, :, :, :], ACT.Sqrt).then_inc(s_bnroot, 1)
                for i in range(NPIECE):
                    act.wait_ge(s_wraw, i * 16 + 16)
                    nc.scalar.activation(whi[i // EXPERTS0][:, i % EXPERTS0], raw[:, :, :], ACT.Copy).then_inc(s_whi, 1)
                act.wait_ge(s_bn, 10)
                with act.Fori(0, GROUPS) as g:
                    ln_root(act, g, ln3)
                    for k in range(GT):
                        act.wait_ge(ln3.tr, g * GT + k + 1)
                        act.wait_ge(s_hmm, g * GT)
                        nc.scalar.activation(xraw[:, :, k * P:(k + 1) * P], transposed(k), ACT.Copy).then_inc(ln3.xt, 1)
                    act.wait_ge(s_mm[0], g * (NS * F))
                    for k in range(GT):
                        act.wait_ge(ln3.xt, g * GT + k + 1)
                        nc.scalar.activation(xhi[:, :, k * P:(k + 1) * P], xraw[:, :, k * P:(k + 1) * P],
                                             ACT.Copy).then_inc(s_xhi, 1)
                    act.wait_ge(s_gate, g * 7 + 3)
                    nc.scalar.activation(gate[:, :, :], glog[:, :, :], ACT.Exp).then_inc(s_gexp, 1)
                    for k in range(GT):
                        act.wait_ge(s_gtr, g * GT + k + 1)
                        act.wait_ge(s_gbo, g * GT)
                        nc.scalar.activation(gateT[:, k * P:(k + 1) * P], bank[k % 2][0:EXPERTS0, 0:P],
                                             ACT.Copy).then_inc(s_gt, 1)

                    def relus(l, j):
                        si, e = STEPS[j]
                        n = SUBS[si][1] * P
                        for m in range(F):
                            act.wait_ge(s_mm[l], g * (NS * F) + j * F + m + 1)
                            if j:
                                act.wait_ge(s_lo[l], g * NS + j)
                            nc.scalar.activation(rl[:, l, m, 0:n], bank[2 + 2 * l + m][:, 0:n], ACT.Relu,
                                                 bias=shf[:, l, e, m:m + 1],
                                                 scale=scl[:, l, e, m:m + 1]).then_inc(s_relu[l], 1)
                        act.wait_ge(s_relu[l], g * (NS * F) + j * F + F)
                        if j:
                            if l == 0:
                                act.wait_ge(s_mm[1], g * (NS * F) + j * F)
                            else:
                                act.wait_ge(s_mm[2], g * OUTS + tiles_before(j))
                        nc.scalar.activation(hhi[l][:, :, 0:n], rl[:, l, :, 0:n], ACT.Copy).then_inc(s_hi[l], 1)

                    for j in range(NS + 1):
                        if j < NS:
                            relus(0, j)
                        if j >= 1:
                            relus(1, j - 1)
                    ln_root(act, g, ln4)
                    for k in range(GT):
                        act.wait_ge(ln4.tr, g * GT + k + 1)
                        nc.scalar.activation(xraw[:, :, k * P:(k + 1) * P], transposed(k), ACT.Copy).then_inc(ln4.xt, 1)
                    for k in range(GT):
                        act.wait_ge(s_hmm, g * GT + k + 1)
                        nc.scalar.activation(part[:, k, :], bank[2 + k % 2][:, 0:D], ACT.Copy).then_inc(s_hcopy, 1)

            @block.tensor
            def _(pe):
                pe.wait_ge(s_small, 16 * 15)
                pe.wait_ge(s_wlo, NPIECE)
                with pe.Fori(0, GROUPS) as g:
                    pe.wait_ge(s_hcopy, g * GT)
                    ln_transpose(pe, g, ln3)
                    pe.wait_ge(ln3.xt, g * GT + GT)
                    for k in range(GT):
                        for f in range(F):
                            last = nc.tensor.matmul(bank[6][:, k * EXPERTS0:(k + 1) * EXPERTS0],
                                                    xraw[:, f, k * P:(k + 1) * P], gws[:, f, :],
                                                    start=(f == 0), stop=(f == F - 1))
                    last.then_inc(s_glog, 1)
                    for k in range(GT):
                        if k == 0:
                            pe.wait_ge(s_gate, g * 7 + 7)
                        else:
                            if k >= 2:
                                pe.wait_ge(s_gt, g * GT + k - 1)
                        nc.tensor.transpose(bank[k % 2][0:EXPERTS0, 0:P], gate[:, k, :], ident[:, :]).then_inc(s_gtr, 1)
                    for k in range(GT):
                        pe.wait_ge(s_gt, g * GT + k + 1)
                        if k >= 2:
                            pe.wait_ge(s_acc0, g * GT + k - 1)
                        nc.tensor.matmul(bank[6 + k % 2][:, 0:D], gateT[:, k * P:(k + 1) * P], bos[:, :],
                                         start=True, stop=True).then_inc(s_gbo, 1)
                    pe.wait_ge(s_xhi, g * GT + GT)
                    pe.wait_ge(s_xlo, g * GT + GT)

                    def layer(l, j):
                        si, e = STEPS[j]
                        k0, w = SUBS[si]
                        n = w * P
                        if l == 0:
                            rh, rlo = (xhi[:, :, k0 * P:k0 * P + n], xlo[:, :, k0 * P:k0 * P + n])
                        else:
                            pe.wait_ge(s_hi[0], g * NS + j + 1)
                            pe.wait_ge(s_lo[0], g * NS + j + 1)
                            rh, rlo = hhi[0][:, :, 0:n], hlo[0][:, :, 0:n]
                        for m in range(F):
                            if j:
                                pe.wait_ge(s_relu[l], g * (NS * F) + (j - 1) * F + m + 1)
                            for f in range(F):
                                last = three(pe, bank[2 + 2 * l + m][:, 0:n],
                                             whi[l][:, e, f, m * P:(m + 1) * P], wlo[l][:, e, f, m * P:(m + 1) * P],
                                             rh[:, f, :], rlo[:, f, :], f == 0, f == F - 1)
                            last.then_inc(s_mm[l], 1)

                    def output(j):
                        si, e = STEPS[j]
                        w = SUBS[si][1]
                        pe.wait_ge(s_hi[1], g * NS + j + 1)
                        pe.wait_ge(s_lo[1], g * NS + j + 1)
                        for k in range(w):
                            i = tiles_before(j) + k
                            if i >= 2:
                                pe.wait_ge(s_out, g * OUTS + i - 1)
                            elif i < 2:
                                pe.wait_ge(s_acc0, g * GT + GT)
                            for f in range(F):
                                last = three(pe, bank[6 + i % 2][:, 0:D],
                                             hhi[1][:, f, k * P:(k + 1) * P], hlo[1][:, f, k * P:(k + 1) * P],
                                             whi[2][:, e, f, :], wlo[2][:, e, f, :], f == 0, f == F - 1)
                            last.then_inc(s_mm[2], 1)

                    for j in range(NS + 2):
                        if j < NS:
                            layer(0, j)
                        if 1 <= j <= NS:
                            layer(1, j - 1)
                        if j >= 2:
                            output(j - 2)
                    ln_transpose(pe, g, ln4)
                    for k in range(GT):
                        pe.wait_ge(ln4.xt, g * GT + k + 1)
                        if k >= 2:
                            pe.wait_ge(s_hcopy, g * GT + k - 1)
                        for f in range(F):
                            last = nc.tensor.matmul(bank[2 + k % 2][:, 0:D], xraw[:, f, k * P:(k + 1) * P],
                                                    lws[:, f, :], start=(f == 0), stop=(f == F - 1))
                        last.then_inc(s_hmm, 1)

            @block.vector
            def _(dve):
                dve.wait_ge(s_small, 16 * 15)
                nc.vector.tensor_scalar(bnt[:, :, :, :], bnp[:, :, 4], BN_EPS, None, ALU.add).then_inc(s_bn, 1)
                dve.wait_ge(s_bnroot, 1)
                steps = [
                    lambda: nc.vector.reciprocal(scl[:, :, :, :], scl[:, :, :, :]),
                    lambda: nc.vector.tensor_tensor(shf[:, :, :, :], scl[:, :, :, :], scl[:, :, :, :], ALU.mult),
                    lambda: nc.vector.tensor_tensor(shf[:, :, :, :], shf[:, :, :, :], bnt[:, :, :, :], ALU.mult),
                    lambda: nc.vector.tensor_scalar(shf[:, :, :, :], shf[:, :, :, :], -0.5, 1.5, ALU.mult, ALU.add),
                    lambda: nc.vector.tensor_tensor(scl[:, :, :, :], scl[:, :, :, :], shf[:, :, :, :], ALU.mult),
                    lambda: nc.vector.tensor_tensor(scl[:, :, :, :], scl[:, :, :, :], bnp[:, :, 1], ALU.mult),
                    lambda: nc.vector.tensor_tensor(shf[:, :, :, :], bnp[:, :, 0], bnp[:, :, 3], ALU.subtract),
                    lambda: nc.vector.tensor_tensor(shf[:, :, :, :], shf[:, :, :, :], scl[:, :, :, :], ALU.mult),
                    lambda: nc.vector.tensor_tensor(shf[:, :, :, :], shf[:, :, :, :], bnp[:, :, 2], ALU.add),
                ]
                for n, step in enumerate(steps):
                    step().then_inc(s_bn, 1)
                    dve.wait_ge(s_bn, n + 2)
                for i in range(NPIECE):
                    dve.wait_ge(s_whi, i + 1)
                    nc.vector.tensor_tensor(wlo[i // EXPERTS0][:, i % EXPERTS0], raw[:, :, :],
                                            whi[i // EXPERTS0][:, i % EXPERTS0].bitcast(F32),
                                            ALU.subtract).then_inc(s_wlo, 1)
                with dve.Fori(0, GROUPS) as g:
                    tables_add(dve, g, tb3)
                    ln_vector(dve, g, ln3)
                    dve.wait_ge(s_glog, g + 1)
                    base = g * 7
                    nc.vector.tensor_tensor(glog[:, :, :], bank[6][:, 0:GT * EXPERTS0].rearrange("p (k e) -> p k e", k=GT),
                                            gbs[:, :].unsqueeze(1).broadcast_to([P, GT, EXPERTS0]),
                                            ALU.add).then_inc(s_gate, 1)
                    dve.wait_ge(s_gate, base + 1)
                    nc.vector.tensor_reduce(gm[:, :], glog[:, :, :], AX.X, ALU.max).then_inc(s_gate, 1)
                    dve.wait_ge(s_gate, base + 2)
                    nc.vector.tensor_tensor(glog[:, :, :], glog[:, :, :],
                                            gm[:, :].unsqueeze(2).broadcast_to([P, GT, EXPERTS0]),
                                            ALU.subtract).then_inc(s_gate, 1)
                    for k in range(GT):
                        dve.wait_ge(s_xhi, g * GT + k + 1)
                        nc.vector.tensor_tensor(xlo[:, :, k * P:(k + 1) * P], xraw[:, :, k * P:(k + 1) * P],
                                                xhi[:, :, k * P:(k + 1) * P].bitcast(F32), ALU.subtract).then_inc(s_xlo, 1)
                    dve.wait_ge(s_gexp, g + 1)
                    nc.vector.tensor_reduce(gm[:, :], gate[:, :, :], AX.X, ALU.add).then_inc(s_gate, 1)
                    dve.wait_ge(s_gate, base + 4)
                    nc.vector.reciprocal(gm[:, :], gm[:, :]).then_inc(s_gate, 1)
                    dve.wait_ge(s_gate, base + 5)
                    nc.vector.tensor_tensor(glog[:, :, :], gate[:, :, :],
                                            gm[:, :].unsqueeze(2).broadcast_to([P, GT, EXPERTS0]),
                                            ALU.mult).then_inc(s_gate, 1)
                    dve.wait_ge(s_gate, base + 6)
                    nc.vector.tensor_copy(gate[:, :, :], glog[:, :, :]).then_inc(s_gate, 1)
                    for k in range(GT):
                        dve.wait_ge(s_gbo, g * GT + k + 1)
                        nc.vector.tensor_tensor(acc[:, k, :], bank[6 + k % 2][:, 0:D], acc[:, k, :],
                                                ALU.add).then_inc(s_acc0, 1)
                    dve.wait_ge(s_acc0, g * GT + GT)
                    dve.wait_ge(s_gate, base + 7)

                    def lower_half(l, j):
                        n = SUBS[STEPS[j][0]][1] * P
                        dve.wait_ge(s_hi[l], g * NS + j + 1)
                        nc.vector.tensor_tensor(hlo[l][:, :, 0:n], rl[:, l, :, 0:n], hhi[l][:, :, 0:n].bitcast(F32),
                                                ALU.subtract).then_inc(s_lo[l], 1)

                    def add_out(j):
                        si, e = STEPS[j]
                        k0, w = SUBS[si]
                        for k in range(w):
                            i = tiles_before(j) + k
                            dve.wait_ge(s_mm[2], g * OUTS + i + 1)
                            if e:
                                dve.wait_ge(s_out, g * OUTS + i - w + 1)
                            nc.vector.scalar_tensor_tensor(acc[:, k0 + k, :], bank[6 + i % 2][:, 0:D],
                                                           gate[:, k0 + k, e:e + 1], acc[:, k0 + k, :],
                                                           ALU.mult, ALU.add).then_inc(s_out, 1)

                    for j in range(NS + 2):
                        if j < NS:
                            lower_half(0, j)
                        if j >= 2:
                            add_out(j - 2)
                        if 1 <= j <= NS:
                            lower_half(1, j - 1)
                    dve.wait_ge(s_out, g * OUTS + OUTS)
                    ln_vector(dve, g, ln4)
                    dve.wait_ge(ln4.xn, g * GT + GT)
                    nc.vector.tensor_tensor(acc[:, :, :], acc[:, :, :],
                                            lbs[:, :].unsqueeze(1).broadcast_to([P, GT, D]), ALU.add).then_inc(s_base, 1)

        edge_block(1, src_f, dst_f, dst)

        with ExitStack() as c5, nc.Block() as block:
            def sb5(name, shape, dt=F32):
                return c5.enter_context(nc.sbuf_tensor(name, shape, dt))
            ln5 = LN("ln5")
            tb5 = Tables("m")
            s_wt = sem("m_wt")
            s_sel = sem("m_sel")
            s_selc = sem("m_selc")
            s_log = sem("m_log")
            s_lg = sem("m_lg")
            s_mx = sem("m_mx")
            s_mi = sem("m_mi")
            s_mf = sem("m_mf")
            s_oh = sem("m_oh")
            s_ohtr = sem("m_ohtr")
            s_oht = sem("m_oht")
            s_h = sem("m_h")
            s_m = sem("m_m")
            s_r = sem("m_r")
            s_hm = sem("m_hm")
            s_used = sem("m_used")
            s_y = sem("m_y")
            s_st = sem("m_st")
            w1s = sb5("w1s", [P, F, EXPERTS1 * HID1])
            w2s = sb5("w2s", [P, PAIRS, D])
            b1s = sb5("b1s", [P, PAIRS])
            b2s = sb5("b2s", [EXPERTS1, D])
            b2u = sb5("b2u", [EXPERTS1, D])
            rws = sb5("rws", [P, F, EXPERTS1])
            rbs = sb5("rbs", [P, EXPERTS1])
            io_i = sb5("io_i", [P, EXPERTS1], I32)
            io_f = sb5("io_f", [P, EXPERTS1])
            sel_f = sb5("sel_f", [EXPERTS1, PAIRS * P])
            sel = sb5("sel", [EXPERTS1, PAIRS * P], BF16)
            xnt = sb5("xnt5", [P, F, GT * P])
            lg = sb5("lg", [P, GT, EXPERTS1])
            mx = sb5("mx", [P, GT, 8])
            mi = sb5("mi", [P, GT, 8], U32)
            mf = sb5("mf", [P, GT])
            oh = sb5("oh", [P, GT, EXPERTS1])
            ohT = sb5("ohT", [EXPERTS1, GT * P])
            ohTb = sb5("ohTb", [EXPERTS1, GT * P], BF16)
            hr = sb5("hr", [P, 2, W4])
            hm = [sb5(f"hm{i}", [P, W4]) for i in range(2)]
            yb = sb5("yb", [P, GT, D])
            STEPS5 = [(si, q) for si in range(len(SUBS)) for q in range(PAIRS)]
            NS5 = len(STEPS5)

            @block.gpsimd
            def _(pool):
                nc.gpsimd.iota(io_i[:, :], pattern=[[1, EXPERTS1]], base=0, channel_multiplier=0).then_inc(s_sel, 1)
                nc.gpsimd.memset(sel_f[:, :], 0.0).then_inc(s_sel, 1)
                pool.wait_ge(s_sel, 2)
                v = sel_f[:, :].rearrange("e (x h) -> e x h", h=HID1)
                nc.gpsimd.affine_select(out=v, in_=v, compare_op=ALU.not_equal, fill=1.0, base=0,
                                        pattern=[[-1, EXPERTS1], [0, HID1]], channel_multiplier=1).then_inc(s_sel, 1)

            @block.sync
            def _(sp):
                sp.dma_start(w1s[:, :, :], mw1.rearrange("(f p) n -> p f n", p=P)).then_inc(s_wt, 16)
                sp.dma_start(w2s[:, :, :], mw2.rearrange("(q p) d -> p q d", p=P)).then_inc(s_wt, 16)
                sp.dma_start(b1s[:, :], mb1).then_inc(s_wt, 16)
                sp.dma_start(b2s[:, :], mb2).then_inc(s_wt, 16)
                sp.dma_start(rws[:, :, :], rw.rearrange("(f p) e -> p f e", p=P)).then_inc(s_wt, 16)
                sp.dma_start(rbs[:, :], rb.partition_broadcast(P)).then_inc(s_wt, 16)
                with sp.Fori(0, GROUPS) as g:
                    def acc_free():
                        wait_apart(sp, s_y, g * GT)
                    tables_load(sp, g, tb5, 1, acc_free)
                    wait_apart(sp, s_y, g * GT + GT)
                    sp.dma_start(node_rows(out, g), yb[:, :, :]).then_inc(s_st, 16)
                sp.wait_ge(s_st, 16 * GROUPS)

            @block.scalar
            def _(act):
                act.wait_ge(s_wt, 96)
                with act.Fori(0, GROUPS) as g:
                    ln_root(act, g, ln5)
                    act.wait_ge(s_h, g * NS5)
                    for k in range(GT):
                        act.wait_ge(ln5.tr, g * GT + k + 1)
                        nc.scalar.activation(xnt[:, :, k * P:(k + 1) * P], transposed(k), ACT.Copy).then_inc(ln5.xt, 1)
                    act.wait_ge(s_used, g * NS5)
                    for k in range(GT):
                        act.wait_ge(s_ohtr, g * GT + k + 1)
                        nc.scalar.activation(ohT[:, k * P:(k + 1) * P], bank[k % 2][0:EXPERTS1, 0:P],
                                             ACT.Copy)
                        nc.scalar.activation(ohTb[:, k * P:(k + 1) * P], bank[k % 2][0:EXPERTS1, 0:P],
                                             ACT.Copy).then_inc(s_oht, 1)
                    for j, (si, q) in enumerate(STEPS5):
                        n = SUBS[si][1] * P
                        act.wait_ge(s_h, g * NS5 + j + 1)
                        if j >= 2:
                            act.wait_ge(s_hm, g * NS5 + j - 1)
                        nc.scalar.activation(hr[:, j % 2, 0:n], bank[0 + j % 2][:, 0:n], ACT.Relu,
                                             bias=b1s[:, q:q + 1]).then_inc(s_r, 1)

            @block.tensor
            def _(pe):
                pe.wait_ge(s_wt, 96)
                pe.wait_ge(s_selc, 2)
                with pe.Fori(0, GROUPS) as g:
                    pe.wait_ge(s_r, g * NS5)
                    ln_transpose(pe, g, ln5)
                    pe.wait_ge(s_hm, g * NS5)
                    for k in range(GT):
                        pe.wait_ge(ln5.xt, g * GT + k + 1)
                        for f in range(F):
                            last = nc.tensor.matmul(bank[2][:, k * EXPERTS1:(k + 1) * EXPERTS1],
                                                    xnt[:, f, k * P:(k + 1) * P], rws[:, f, :],
                                                    start=(f == 0), stop=(f == F - 1))
                    last.then_inc(s_log, 1)
                    for k in range(GT):
                        pe.wait_ge(s_oh, g * GT + k + 1)
                        if k >= 2:
                            pe.wait_ge(s_oht, g * GT + k - 1)
                        nc.tensor.transpose(bank[k % 2][0:EXPERTS1, 0:P], oh[:, k, :], ident[:, :]).then_inc(s_ohtr, 1)
                    pe.wait_ge(s_oht, g * GT + GT)

                    def hidden(j):
                        si, q = STEPS5[j]
                        k0, w = SUBS[si]
                        n = w * P
                        if j >= 2:
                            pe.wait_ge(s_r, g * NS5 + j - 1)
                        for f in range(F):
                            last = nc.tensor.matmul(bank[j % 2][:, 0:n], w1s[:, f, q * P:(q + 1) * P],
                                                    xnt[:, f, k0 * P:k0 * P + n], start=(f == 0), stop=(f == F - 1))
                        last.then_inc(s_h, 1)
                        if j >= 2:
                            pe.wait_ge(s_hm, g * NS5 + j - 1)
                        nc.tensor.matmul(bank[2 + j % 2][:, 0:n], sel[:, q * P:(q + 1) * P],
                                         ohTb[:, k0 * P:k0 * P + n], start=True, stop=True).then_inc(s_m, 1)

                    def outputs(j):
                        si, q = STEPS5[j]
                        k0, w = SUBS[si]
                        if q == 0:
                            pe.wait_ge(s_y, g * GT + k0)
                            for k in range(w):
                                nc.tensor.matmul(bank[4 + k][:, 0:D], ohT[:, (k0 + k) * P:(k0 + k + 1) * P], b2s[:, :],
                                                 start=True, stop=False)
                        pe.wait_ge(s_hm, g * NS5 + j + 1)
                        for k in range(w):
                            last = nc.tensor.matmul(bank[4 + k][:, 0:D], hm[j % 2][:, k * P:(k + 1) * P], w2s[:, q, :],
                                                    start=False, stop=(q == PAIRS - 1))
                        last.then_inc(s_used, 1)

                    hidden(0)
                    for j in range(NS5):
                        if j + 1 < NS5:
                            hidden(j + 1)
                        outputs(j)

            @block.vector
            def _(dve):
                dve.wait_ge(s_wt, 96)
                dve.wait_ge(s_sel, 3)
                nc.vector.tensor_copy(sel[:, :], sel_f[:, :]).then_inc(s_selc, 1)
                nc.vector.tensor_copy(io_f[:, :], io_i[:, :]).then_inc(s_selc, 1)
                dve.wait_ge(s_selc, 2)
                with dve.Fori(0, GROUPS) as g:
                    tables_add(dve, g, tb5)
                    ln_vector(dve, g, ln5)
                    dve.wait_ge(s_log, g + 1)
                    nc.vector.tensor_tensor(lg[:, :, :], bank[2][:, 0:GT * EXPERTS1].rearrange("p (k e) -> p k e", k=GT),
                                            rbs[:, :].unsqueeze(1).broadcast_to([P, GT, EXPERTS1]),
                                            ALU.add).then_inc(s_lg, 1)
                    wait_apart(dve, s_lg, g + 1)
                    for k in range(GT):
                        nc.vector.max(mx[:, k, :], lg[:, k, :]).then_inc(s_mx, 1)
                    for k in range(GT):
                        wait_apart(dve, s_mx, g * GT + k + 1)
                        nc.vector.max_index(mi[:, k, :], mx[:, k, :], lg[:, k, :]).then_inc(s_mi, 1)
                    dve.wait_ge(s_mi, g * GT + GT)
                    nc.vector.tensor_copy(mf[:, :], mi[:, :, 0]).then_inc(s_mf, 1)
                    dve.wait_ge(s_mf, g + 1)
                    for k in range(GT):
                        nc.vector.tensor_scalar(oh[:, k, :], io_f[:, :], mf[:, k:k + 1], None,
                                                ALU.is_equal).then_inc(s_oh, 1)

                    def finish(si):
                        k0, w = SUBS[si]
                        for k in range(w):
                            if k == 0:
                                dve.wait_ge(s_used, g * NS5 + PAIRS * (si + 1))
                            nc.vector.scalar_tensor_tensor(yb[:, k0 + k, :], bank[4 + k][:, 0:D], 0.0,
                                                           acc[:, k0 + k, :], ALU.max, ALU.add).then_inc(s_y, 1)

                    dve.wait_ge(s_st, g * 16)
                    for j, (si, q) in enumerate(STEPS5):
                        if q == 1 and si:
                            finish(si - 1)
                        n = SUBS[si][1] * P
                        dve.wait_ge(s_r, g * NS5 + j + 1)
                        dve.wait_ge(s_m, g * NS5 + j + 1)
                        if j >= 2:
                            dve.wait_ge(s_used, g * NS5 + j - 1)
                        nc.vector.tensor_tensor(hm[j % 2][:, 0:n], bank[2 + j % 2][:, 0:n], hr[:, j % 2, 0:n],
                                                ALU.mult).then_inc(s_hm, 1)
                    finish(len(SUBS) - 1)


INS = ["x", "src", "dst", "wgt", "wl", "wr", "bl", "br", "gw", "gbr",
       "w1", "b1", "g1", "be1", "m1", "v1", "w2", "b2", "g2", "be2", "m2", "v2", "wo", "bo",
       "lw", "lb", "rw", "rb", "mw1", "mb1", "mw2", "mb2"]


def kernel(x, src, dst, edge_weight, L0_gnn_weight_l, L0_gnn_bias_l, L0_gnn_weight_r, L0_gnn_bias_r,
           L0_ffn_Wr, L0_ffn_br, L0_ffn_W1, L0_ffn_b1, L0_ffn_g1, L0_ffn_be1, L0_ffn_m1, L0_ffn_v1,
           L0_ffn_W2, L0_ffn_b2, L0_ffn_g2, L0_ffn_be2, L0_ffn_m2, L0_ffn_v2, L0_ffn_Wo, L0_ffn_bo,
           L1_gnn_weight, L1_gnn_bias, L1_ffn_router_w, L1_ffn_router_b, L1_ffn_W1, L1_ffn_b1,
           L1_ffn_W2, L1_ffn_b2):
    import concourse.bacc as bacc
    from concourse.bass_utils import run_bass_kernel_spmd

    def padded(a, rows):
        a = np.asarray(a)
        return np.concatenate([a, np.zeros((rows - a.shape[0],) + a.shape[1:], a.dtype)])

    def features_first(a):
        return np.asarray(a).reshape(EXPERTS0, F, P).transpose(2, 0, 1)

    arrays = [
        padded(x, ROWS), padded(src, E_PAD), padded(dst, E_PAD), padded(edge_weight, E_PAD),
        L0_gnn_weight_l, L0_gnn_weight_r, L0_gnn_bias_l, L0_gnn_bias_r, L0_ffn_Wr, L0_ffn_br,
        L0_ffn_W1, *(features_first(a) for a in (L0_ffn_b1, L0_ffn_g1, L0_ffn_be1, L0_ffn_m1, L0_ffn_v1)),
        L0_ffn_W2, *(features_first(a) for a in (L0_ffn_b2, L0_ffn_g2, L0_ffn_be2, L0_ffn_m2, L0_ffn_v2)),
        L0_ffn_Wo, L0_ffn_bo, L1_gnn_weight, L1_gnn_bias,
        np.asarray(L1_ffn_router_w).transpose(1, 0), L1_ffn_router_b,
        np.asarray(L1_ffn_W1).transpose(1, 0, 2).reshape(D, EXPERTS1 * HID1),
        np.asarray(L1_ffn_b1).reshape(PAIRS, P).transpose(1, 0),
        np.asarray(L1_ffn_W2).reshape(EXPERTS1 * HID1, D), L1_ffn_b2,
    ]
    nc = bacc.Bacc("TRN2", target_bir_lowering=False, num_devices=1)
    feeds, args = {}, []
    for name, a in zip(INS, arrays):
        a = np.ascontiguousarray(a)
        feeds[f"in_{name}"] = a
        args.append(nc.dram_tensor(f"in_{name}", a.shape, mybir.dt.from_np(a.dtype), kind="ExternalInput").ap())
    out = nc.dram_tensor("out_rows", (ROWS, D), F32, kind="ExternalOutput").ap()
    build(nc, *args, out)
    r = run_bass_kernel_spmd(nc, [feeds], core_ids=[0])
    return r.results[0]["out_rows"][:N_NODES]
```

```python
from contextlib import ExitStack, contextmanager

import numpy as np
import concourse.bass as bass
from concourse import mybir

F32 = mybir.dt.float32
F32R = mybir.dt.float32r
BF16 = mybir.dt.bfloat16
I32 = mybir.dt.int32
U32 = mybir.dt.uint32
ALU = mybir.AluOpType
ACT = mybir.ActivationFunctionType
AX = mybir.AxisListType

P = 128
N_NODES = 6250
D = 256
F = D // P
E_EDGES = 100000
EXPERTS0 = 8
EXPERTS1 = 32
HID1 = 64
PAIRS = EXPERTS1 * HID1 // P

GT = 7
GROUPS = 7
ROWS = GROUPS * GT * P
SUBS = ((0, 4), (4, 3))
W4 = 4 * P

U = 4
TABLES = (2 * U, U)
EDGE_TILES = 784
E_PAD = EDGE_TILES * P
EGROUPS = EDGE_TILES // U
TR = EDGE_TILES // GT
SPAN = 64
PHASE = EGROUPS // GROUPS
SLACK = 3
HALF = PHASE * U // 2
RING = 4
H_ROWS = ROWS + SPAN
TABLE_ROWS = ROWS + P
LN_EPS = 1e-5
BN_EPS = 1e-3


def build(nc, x, src, dst, wgt, wl, wr, bl, br, gw, gbr, w1, b1, g1, be1, m1, v1,
          w2, b2, g2, be2, m2, v2, wo, bo, lw, lb, rw, rb, mw1, mb1, mw2, mb2, out):
    ctx = ExitStack()
    with ctx:
        def sb(name, shape, dt=F32):
            return ctx.enter_context(nc.sbuf_tensor(name, shape, dt))

        lent = [None]

        def sem(name):
            if lent[0]:
                return lent[0].pop(0)
            return ctx.enter_context(nc.semaphore(name))

        @contextmanager
        def borrowed(handles):
            lent[0] = list(handles)
            yield
            lent[0] = None

        h_tab = [nc.dram_tensor(f"h_tab{i}", ((H_ROWS, ROWS)[i], D), F32, kind="Internal").ap() for i in range(2)]
        acc_tab = [[nc.dram_tensor(f"acc_tab{i}_{u}", (TABLE_ROWS, D), F32, kind="Internal").ap()
                    for u in range(TABLES[i])] for i in range(2)]

        ident = sb("ident", [P, P])
        lower = sb("lower", [P, P])
        dump_row = sb("dump_row", [P, 1])
        src_f = sb("src_f", [P, EDGE_TILES + HALF])
        dst_f = sb("dst_f", [P, EDGE_TILES])
        wgt_f = sb("wgt_f", [P, EDGE_TILES])

        win_i = sb("win_i", [1, EGROUPS], I32)
        rel_f = sb("rel_f", [P, EDGE_TILES])
        iota_w = sb("iota_w", [P, SPAN])
        apart = sb("apart", [1, 1], I32)

        bank = [ctx.enter_context(nc.psum_tensor(f"bank{i}", [P, 512], F32)) for i in range(8)]

        acc = sb("acc", [P, GT, D])
        part = sb("part", [P, GT, D])
        xn = sb("xn", [P, GT, D])
        stat = sb("stat", [P, GT, 6])
        mv = sb("mv", [P, GT, 2])
        ve = sb("ve", [P, GT])
        rstd = sb("rstd", [P, GT])
        tmp7 = sb("tmp7", [P, GT])

        s_apart = sem("s_apart")

        def wait_apart(eng, semaphore, value):
            eng.wait_ge(semaphore, value)
            eng.sem_inc(s_apart, 1)

        def node_rows(table, g):
            return table[bass.ds(g * (GT * P), GT * P), :].rearrange("(k p) d -> p k d", p=P)

        class LN:
            def __init__(s, n):
                s.stats = sem(f"{n}_stats")
                s.aggr = sem(f"{n}_aggr")
                s.var = sem(f"{n}_var")
                s.sd = sem(f"{n}_sd")
                s.newton = sem(f"{n}_newton")
                s.xn = sem(f"{n}_xn")
                s.tr = sem(f"{n}_tr")
                s.xt = sem(f"{n}_xt")

        def ln_vector(dve, g, s):
            for k in range(GT):
                last = nc.vector.bn_stats(stat[:, k, :], acc[:, k, :])
            last.then_inc(s.stats, 1)
            wait_apart(dve, s.stats, g + 1)
            for k in range(GT):
                last = nc.vector.bn_aggr(mv[:, k, :], stat[:, k, :])
            last.then_inc(s.aggr, 1)
            dve.wait_ge(s.aggr, g + 1)
            nc.vector.tensor_scalar(ve[:, :], mv[:, :, 1], LN_EPS, None, ALU.add).then_inc(s.var, 1)
            dve.wait_ge(s.sd, g + 1)
            nc.vector.reciprocal(rstd[:, :], rstd[:, :]).then_inc(s.newton, 1)
            dve.wait_ge(s.newton, g * 5 + 1)
            nc.vector.tensor_tensor(tmp7[:, :], rstd[:, :], rstd[:, :], ALU.mult).then_inc(s.newton, 1)
            dve.wait_ge(s.newton, g * 5 + 2)
            nc.vector.tensor_tensor(tmp7[:, :], tmp7[:, :], ve[:, :], ALU.mult).then_inc(s.newton, 1)
            dve.wait_ge(s.newton, g * 5 + 3)
            nc.vector.tensor_scalar(tmp7[:, :], tmp7[:, :], -0.5, 1.5, ALU.mult, ALU.add).then_inc(s.newton, 1)
            dve.wait_ge(s.newton, g * 5 + 4)
            nc.vector.tensor_tensor(rstd[:, :], rstd[:, :], tmp7[:, :], ALU.mult).then_inc(s.newton, 1)
            dve.wait_ge(s.newton, g * 5 + 5)
            dve.wait_ge(s.tr, g * GT)
            for k in range(GT):
                nc.vector.tensor_scalar(xn[:, k, :], acc[:, k, :], mv[:, k, 0:1], rstd[:, k:k + 1],
                                        ALU.subtract, ALU.mult).then_inc(s.xn, 1)

        def ln_root(act, g, s):
            act.wait_ge(s.var, g + 1)
            act.wait_ge(s.xn, g * GT)
            nc.scalar.activation(rstd[:, :], ve[:, :], ACT.Sqrt).then_inc(s.sd, 1)

        def ln_transpose(pe, g, s):
            for k in range(GT):
                pe.wait_ge(s.xn, g * GT + k + 1)
                pe.wait_ge(s.xt, g * GT + (k - 1 if k >= 2 else 0))
                for f in range(F):
                    last = nc.tensor.transpose(bank[k % 2][:, f * P:(f + 1) * P],
                                               xn[:, k, f * P:(f + 1) * P], ident[:, :])
                last.then_inc(s.tr, 1)

        def transposed(k):
            return bank[k % 2][:, 0:D].rearrange("p (f t) -> p f t", f=F)

        with ExitStack() as c1:
            def sb1(name, shape, dt=F32):
                return c1.enter_context(nc.sbuf_tensor(name, shape, dt))

            s_const = sem("s_const")
            s_zero = sem("s_zero")
            s_ezero = sem("s_ezero")
            s_eload = sem("s_eload")
            s_econv = sem("s_econv")
            s_etr = sem("s_etr")
            s_ecol = sem("s_ecol")
            s_w1 = sem("s_w1")
            s_bsum = sem("s_bsum")
            s_xin = sem("s_xin")
            s_mm = sem("s_mm")
            s_hcopy = sem("s_hcopy")
            s_hst = sem("s_hst")
            s_add1 = sem("s_add1")
            s_add2 = sem("s_add2")
            s_bst = sem("s_bst")
            s_idx = sem("s_idx")
            s_win = sem("s_win")
            s_winb = sem("s_winb")
            s_far = sem("s_far")
            s_farsum = sem("s_farsum")
            ln1 = LN("ln1")

            with ExitStack() as cc, nc.Block() as block:
                erow_i = sb1("erow_i", [TR, 3, GT, P], I32)
                erow_f = sb1("erow_f", [TR, 2, GT, P])
                wlr = sb1("wlr", [P, F, 2, D])
                biases = sb1("biases", [P, 2, D])
                xnt = sb1("xnt", [P, F, GT * P])
                hbuf = sb1("hbuf", [P, GT, D])
                base = sb1("base", [P, GT, D])
                zeros = sb1("zeros", [P, 2560])
                idx_p = sb1("idx_p", [P, 1], I32)
                iota_i = sb1("iota_i", [P, SPAN], I32)
                low_i = sb1("low_i", [1, EGROUPS], I32)
                win_f = sb1("win_f", [1, EGROUPS])
                low_f = sb1("low_f", [1, EGROUPS])
                ones = sb1("ones", [P, P])
                far = sb1("far", [P, EDGE_TILES])
                far_n = sb1("far_n", [P, 1])
                late_n = sb1("late_n", [1, 1])

                @block.gpsimd
                def _(pool):
                    nc.gpsimd.memset(ident[:, :], 0.0).then_inc(s_idx, 1)
                    nc.gpsimd.memset(lower[:, :], 1.0).then_inc(s_idx, 1)
                    pool.wait_ge(s_idx, 2)
                    nc.gpsimd.affine_select(out=ident[:, :], in_=ident[:, :], compare_op=ALU.not_equal,
                                            fill=1.0, base=0, pattern=[[-1, P]],
                                            channel_multiplier=1).then_inc(s_const, 1)
                    nc.gpsimd.affine_select(out=lower[:, :], in_=lower[:, :], compare_op=ALU.is_gt,
                                            fill=0.0, base=0, pattern=[[-1, P]],
                                            channel_multiplier=1).then_inc(s_const, 1)
                    nc.gpsimd.iota(idx_p[:, :], pattern=[[0, 1]], base=ROWS,
                                   channel_multiplier=1).then_inc(s_const, 1)
                    nc.gpsimd.iota(iota_i[:, :], pattern=[[1, SPAN]], base=0,
                                   channel_multiplier=0).then_inc(s_const, 1)
                    low = low_i[:, :].rearrange("o (k i) -> o k i", i=PHASE)
                    nc.gpsimd.iota(low[:, :, 0:SLACK], pattern=[[GT * P, GROUPS], [0, SLACK]], base=-GT * P,
                                   channel_multiplier=0).then_inc(s_const, 1)
                    nc.gpsimd.iota(low[:, :, SLACK:PHASE], pattern=[[GT * P, GROUPS], [0, PHASE - SLACK]], base=0,
                                   channel_multiplier=0).then_inc(s_const, 1)
                    nc.gpsimd.memset(ones[:, :], 1.0).then_inc(s_const, 1)
                    nc.gpsimd.memset(src_f[:, EDGE_TILES:], 0.0)
                    nc.gpsimd.memset(zeros[:, :], 0.0).then_inc(s_zero, 1)

                @block.sync
                def _(sp):
                    for n, a in enumerate((src, dst, wgt)):
                        to = erow_i[:, n] if n < 2 else erow_i[:, n].bitcast(F32)
                        sp.dma_start(to, a.rearrange("(j r p) -> r j p", r=TR, p=P)).then_inc(s_eload, 16)
                    sp.dma_start(win_i[:, :], dst.rearrange("(g e) -> e g", e=U * P)[0:1, :],
                                 allow_slow_non_contiguous=True).then_inc(s_win, 16)
                    sp.dma_start(wlr[:, :, 0, :], wl.rearrange("(f p) d -> p f d", p=P)).then_inc(s_w1, 16)
                    sp.dma_start(wlr[:, :, 1, :], wr.rearrange("(f p) d -> p f d", p=P)).then_inc(s_w1, 16)
                    sp.dma_start(biases[:, 0, :], bl.partition_broadcast(P)).then_inc(s_w1, 16)
                    sp.dma_start(biases[:, 1, :], br.partition_broadcast(P)).then_inc(s_w1, 16)
                    with sp.Fori(0, GROUPS) as g:
                        wait_apart(sp, s_add1, g * GT)
                        sp.dma_start(acc[:, :, :], node_rows(x, g)).then_inc(s_xin, 16)
                        wait_apart(sp, s_hcopy, g * GT + GT)
                        sp.dma_start(node_rows(h_tab[0], g), hbuf[:, :, :]).then_inc(s_hst, 16)
                        wait_apart(sp, s_add2, g + 1)
                        sp.dma_start(node_rows(acc_tab[0][0], g), base[:, :, :]).then_inc(s_bst, 16)
                    sp.wait_ge(s_hst, 16 * GROUPS)
                    sp.wait_ge(s_bst, 16 * GROUPS)
                    sp.wait_ge(s_ezero, 16 * (5 * (sum(TABLES) - 2) + 3))

                @block.scalar
                def _(act):
                    act.wait_ge(s_zero, 1)
                    for i in range(2):
                        for u in range(TABLES[i]):
                            if u:
                                flat = acc_tab[i][u].rearrange("(p r) d -> p (r d)", p=P)
                                for c in range(5):
                                    act.dma_start(flat[:, c * 2560:(c + 1) * 2560], zeros[:, :]).then_inc(s_ezero, 16)
                            else:
                                act.dma_start(acc_tab[i][0][ROWS:TABLE_ROWS, :], zeros[:, 0:D]).then_inc(s_ezero, 16)
                    act.dma_start(h_tab[0][ROWS:H_ROWS, :], zeros[0:SPAN, 0:D]).then_inc(s_ezero, 16)
                    for n, col in enumerate((src_f, dst_f, wgt_f)):
                        for j in range(GT):
                            act.wait_ge(s_etr, n * GT + j + 1)
                            nc.scalar.activation(col[:, j * TR:(j + 1) * TR],
                                                 bank[(n * GT + j) % 2][:, 0:TR], ACT.Copy).then_inc(s_ecol, 1)
                    with act.Fori(0, GROUPS) as g:
                        ln_root(act, g, ln1)
                        for k in range(GT):
                            act.wait_ge(ln1.tr, g * GT + k + 1)
                            act.wait_ge(s_mm, g * GT)
                            nc.scalar.activation(xnt[:, :, k * P:(k + 1) * P], transposed(k),
                                                 ACT.Copy).then_inc(ln1.xt, 1)
                        act.wait_ge(s_hst, g * 16)
                        for k in range(GT):
                            act.wait_ge(s_mm, g * GT + k + 1)
                            nc.scalar.activation(hbuf[:, k, :], bank[2 + k % 2][:, 0:D],
                                                 ACT.Copy).then_inc(s_hcopy, 1)

                @block.tensor
                def _(pe):
                    pe.wait_ge(s_const, 1)
                    for n in range(3):
                        for j in range(GT):
                            i = n * GT + j
                            if n < 2:
                                pe.wait_ge(s_econv, n + 1)
                                rows = erow_f[:, n, j, :]
                            else:
                                pe.wait_ge(s_eload, 48)
                                rows = erow_i[:, 2, j, :].bitcast(F32)
                            if i >= 2:
                                pe.wait_ge(s_ecol, i - 1)
                            nc.tensor.transpose(bank[i % 2][:, 0:TR], rows,
                                                ident[0:TR, 0:TR]).then_inc(s_etr, 1)
                    pe.wait_ge(s_const, 7)
                    pe.wait_ge(s_winb, 2)
                    nc.tensor.matmul(bank[7][:, 0:EGROUPS], ones[0:1, :], win_f[:, :],
                                     start=True, stop=True).then_inc(s_winb, 1)
                    pe.wait_ge(s_far, 3)
                    nc.tensor.matmul(bank[6][0:1, 0:1], far_n[:, :], ones[:, 0:1],
                                     start=True, stop=True).then_inc(s_farsum, 1)
                    pe.wait_ge(s_ecol, 3 * GT)
                    pe.wait_ge(s_w1, 64)
                    with pe.Fori(0, GROUPS) as g:
                        ln_transpose(pe, g, ln1)
                        for k in range(GT):
                            pe.wait_ge(ln1.xt, g * GT + k + 1)
                            done = g * GT + (k - 1 if k >= 2 else 0)
                            pe.wait_ge(s_hcopy, done)
                            pe.wait_ge(s_add1, done)
                            for w in range(2):
                                for f in range(F):
                                    last = nc.tensor.matmul(bank[2 + 2 * w + k % 2][:, 0:D],
                                                            xnt[:, f, k * P:(k + 1) * P], wlr[:, f, w, :],
                                                            start=(f == 0), stop=(f == F - 1))
                            last.then_inc(s_mm, 1)

                @block.vector
                def _(dve):
                    dve.wait_ge(s_const, 6)
                    nc.vector.tensor_copy(dump_row[:, :], idx_p[:, :])
                    nc.vector.tensor_copy(iota_w[:, :], iota_i[:, :])
                    nc.vector.tensor_copy(low_f[:, :], low_i[:, :]).then_inc(s_bsum, 1)
                    dve.wait_ge(s_win, 16)
                    nc.vector.tensor_copy(win_f[:, :], win_i[:, :]).then_inc(s_winb, 2)
                    dve.wait_ge(s_eload, 48)
                    for n in range(2):
                        nc.vector.tensor_copy(erow_f[:, n], erow_i[:, n]).then_inc(s_econv, 1)
                    dve.wait_ge(s_winb, 3)
                    dve.wait_ge(s_ecol, 2 * GT)
                    nc.vector.tensor_tensor(rel_f[:, :].rearrange("p (g u) -> p g u", u=U),
                                            dst_f[:, :].rearrange("p (g u) -> p g u", u=U),
                                            bank[7][:, 0:EGROUPS].unsqueeze(2).broadcast_to([P, EGROUPS, U]),
                                            ALU.subtract).then_inc(s_far, 1)
                    dve.wait_ge(s_far, 1)
                    nc.vector.tensor_scalar(far[:, :], rel_f[:, :], float(SPAN), None, ALU.is_ge).then_inc(s_far, 1)
                    dve.wait_ge(s_far, 2)
                    nc.vector.scalar_tensor_tensor(far[:, :], rel_f[:, :], 0.0, far[:, :], ALU.is_lt, ALU.add,
                                                   accum_out=far_n[:, :]).then_inc(s_far, 1)
                    dve.wait_ge(s_bsum, 1)
                    nc.vector.tensor_tensor(low_f[:, :], low_f[:, :], win_f[:, :], ALU.is_gt).then_inc(s_far, 1)
                    dve.wait_ge(s_far, 4)
                    nc.vector.tensor_reduce(late_n[:, :], low_f[:, :], AX.X, ALU.add).then_inc(s_far, 1)
                    dve.wait_ge(s_far, 5)
                    dve.wait_ge(s_farsum, 1)
                    nc.vector.tensor_tensor(late_n[:, :], bank[6][0:1, 0:1], late_n[:, :], ALU.add).then_inc(s_far, 1)
                    dve.wait_ge(s_far, 6)
                    nc.vector.tensor_scalar(apart[:, :], late_n[:, :], 1.0, None, ALU.min).then_inc(s_far, 1)
                    dve.wait_ge(s_w1, 64)
                    nc.vector.tensor_tensor(biases[:, 0, :], biases[:, 0, :], biases[:, 1, :],
                                            ALU.add).then_inc(s_bsum, 1)
                    dve.wait_ge(s_bsum, 2)
                    with dve.Fori(0, GROUPS) as g:
                        dve.wait_ge(s_xin, g * 16 + 16)
                        ln_vector(dve, g, ln1)
                        dve.wait_ge(s_bst, g * 16)
                        for k in range(GT):
                            dve.wait_ge(s_mm, g * GT + k + 1)
                            nc.vector.tensor_tensor(base[:, k, :], bank[4 + k % 2][:, 0:D], acc[:, k, :],
                                                    ALU.add).then_inc(s_add1, 1)
                        dve.wait_ge(s_add1, g * GT + GT)
                        nc.vector.tensor_tensor(base[:, :, :], base[:, :, :],
                                                biases[:, 0, :].unsqueeze(1).broadcast_to([P, GT, D]),
                                                ALU.add).then_inc(s_add2, 1)

        def edge_block(layer, gather_f, scatter_f, scatter_rows):
            n = f"e{layer}"
            s_row = [sem(f"{n}_row{b}") for b in range(2)]
            s_weights = sem(f"{n}_weights")
            s_count = sem(f"{n}_count")
            s_stage = sem(f"{n}_stage")
            s_gather = [[sem(f"{n}_gather{b}{u}") for u in range(U)] for b in range(2)]
            s_sum = sem(f"{n}_sum")
            s_copy = sem(f"{n}_copy")
            s_scatter = [sem(f"{n}_scatter{u}") for u in range(U)]
            with ExitStack() as c2, nc.Block() as block:
                def sb2(name, shape, dt=F32):
                    return c2.enter_context(nc.sbuf_tensor(f"{n}_{name}", shape, dt))
                row = [sb2(f"row{b}", [P, U * P], I32) for b in range(2)]
                wmat = sb2("wmat", [P, 2, U, P])
                junk = sb2("junk", [P, U, P])
                count = sb2("count", [P, 2, U])
                t_idx = sb2("t_idx", [P, U])
                gidx = [sb2(f"gidx{b}", [P, U], I32) for b in range(2)]
                sidx = [sb2(f"sidx{b}", [P, U], I32) for b in range(2)]
                got = sb2("got", [P, 2, U, D])
                summed = sb2("summed", [P, 2, U, D])
                h = h_tab[layer]
                tabs = acc_tab[layer]

                def later(i):
                    return not isinstance(i, int)

                def pairs_of(eng, body):
                    body(0)
                    with eng.Fori(1, EGROUPS // 2) as i:
                        body(i)

                @block.sync
                def _(sp):
                    with sp.If(sp.value_load(apart[:, :], min_val=0, max_val=1) == 1):
                        def body(i):
                            for b in range(2):
                                if later(i):
                                    wait_apart(sp, s_count, i * (2 * U) + (b - 1) * U)
                                sp.dma_start(row[b][:, :], scatter_rows[bass.ds((i * 2 + b) * (U * P), U * P)]
                                             .partition_broadcast(P)).then_inc(s_row[b], 16)
                        pairs_of(sp, body)

                @block.vector
                def _(dve):
                    with dve.If(dve.value_load(apart[:, :], min_val=0, max_val=1) == 1):
                        def body(i):
                            for b in range(2):
                                g = i * 2 + b
                                dve.wait_ge(s_row[b], i * 16 + 16)
                                if later(i):
                                    dve.wait_ge(s_sum, g * U - U)
                                for u in range(U):
                                    col = g * U + u
                                    nc.vector.tensor_scalar(wmat[:, b, u, :], row[b][:, u * P:(u + 1) * P],
                                                            scatter_f[:, bass.ds(col, 1)], wgt_f[:, bass.ds(col, 1)],
                                                            ALU.is_equal, ALU.mult).then_inc(s_weights, 1)
                                dve.wait_ge(s_count, g * U)
                                for u in range(U):
                                    col = g * U + u
                                    nc.vector.scalar_tensor_tensor(
                                        junk[:, u, :], row[b][:, u * P:(u + 1) * P], scatter_f[:, bass.ds(col, 1)],
                                        lower[:, :], ALU.is_equal, ALU.mult,
                                        accum_out=count[:, b, u:u + 1]).then_inc(s_count, 1)
                                cols = scatter_f[:, bass.ds(g * U, U)]
                                dve.wait_ge(s_stage, g * 4)
                                nc.vector.tensor_scalar(t_idx[:, :], cols, -1.0, dump_row[:, 0:1],
                                                        ALU.mult, ALU.add).then_inc(s_stage, 1)
                                dve.wait_ge(s_count, g * U + U)
                                dve.wait_ge(s_stage, g * 4 + 1)
                                nc.vector.scalar_tensor_tensor(t_idx[:, :], count[:, b, :], 0.0, t_idx[:, :],
                                                               ALU.is_gt, ALU.mult).then_inc(s_stage, 1)
                                dve.wait_ge(s_stage, g * 4 + 2)
                                if later(i):
                                    for u in range(U):
                                        dve.wait_ge(s_scatter[u], g * 16 - 16)
                                nc.vector.tensor_tensor(sidx[b][:, :], t_idx[:, :], cols, ALU.add).then_inc(s_stage, 1)
                                nc.vector.tensor_copy(gidx[b][:, :], gather_f[:, bass.ds(g * U, U)]).then_inc(s_stage, 1)
                        pairs_of(dve, body)

                @block.gpsimd
                def _(pool):
                    with pool.If(pool.value_load(apart[:, :], min_val=0, max_val=1) == 1):
                        def gather(i, b, u):
                            g = i * 2 + b
                            if u == 0:
                                pool.wait_ge(s_stage, g * 4 + 4)
                            if later(i):
                                wait_apart(pool, s_sum, g * U - 2 * U + u + 1)
                            nc.gpsimd.indirect_dma_start(
                                got[:, b, u, :], None, h, bass.IndirectOffsetOnAxis(gidx[b][:, u:u + 1], 0),
                                bounds_check=ROWS - 1, oob_is_err=True).then_inc(s_gather[b][u], 16)

                        def scatter(g, b, u, first=False):
                            pool.wait_ge(s_copy, g * U + u + 1)
                            if not first:
                                wait_apart(pool, s_scatter[u], g * 16)
                            nc.gpsimd.indirect_dma_start(
                                tabs[u], bass.IndirectOffsetOnAxis(sidx[b][:, u:u + 1], 0), summed[:, b, u, :],
                                None, bounds_check=TABLE_ROWS - 1, oob_is_err=True,
                                compute_op=ALU.add).then_inc(s_scatter[u], 16)

                        for u in range(U):
                            gather(0, 0, u)
                        for u in range(U):
                            gather(0, 1, u)
                            scatter(0, 0, u, first=True)
                        with pool.Fori(1, EGROUPS // 2) as i:
                            for u in range(U):
                                gather(i, 0, u)
                                scatter(i * 2 - 1, 1, u)
                            for u in range(U):
                                gather(i, 1, u)
                                scatter(i * 2, 0, u)
                        for u in range(U):
                            scatter(EGROUPS - 1, 1, u)
                        for u in range(U):
                            pool.wait_ge(s_scatter[u], EGROUPS * 16)

                @block.tensor
                def _(pe):
                    with pe.If(pe.value_load(apart[:, :], min_val=0, max_val=1) == 1):
                        def body(i):
                            for b in range(2):
                                g = i * 2 + b
                                for u in range(U):
                                    pe.wait_ge(s_weights, g * U + u + 1)
                                    pe.wait_ge(s_gather[b][u], i * 16 + 16)
                                    if later(i):
                                        pe.wait_ge(s_copy, g * U - 2 * U + u + 1)
                                    nc.tensor.matmul(bank[b * U + u][:, 0:D], wmat[:, b, u, :], got[:, b, u, :],
                                                     start=True, stop=True).then_inc(s_sum, 1)
                        pairs_of(pe, body)

                @block.scalar
                def _(act):
                    with act.If(act.value_load(apart[:, :], min_val=0, max_val=1) == 1):
                        def body(i):
                            for b in range(2):
                                g = i * 2 + b
                                for u in range(U):
                                    act.wait_ge(s_sum, g * U + u + 1)
                                    if later(i):
                                        act.wait_ge(s_scatter[u], g * 16 - 16)
                                    nc.scalar.activation(summed[:, b, u, :], bank[b * U + u][:, 0:D],
                                                         ACT.Copy).then_inc(s_copy, 1)
                        pairs_of(act, body)

        pair0 = [sem(f"pair0_{j}") for j in range(25)]
        with borrowed(pair0), ExitStack() as c2, nc.Block() as block:
            def sbn(name, shape, dt=F32):
                return c2.enter_context(nc.sbuf_tensor(f"n0_{name}", shape, dt))
            s_row = [sem(f"n0_row{b}") for b in range(2)]
            s_hwin = [sem(f"n0_hwin{b}") for b in range(2)]
            s_hot = sem("n0_hot")
            s_weights = sem("n0_weights")
            s_count = sem("n0_count")
            s_stage = sem("n0_stage")
            s_mix = sem("n0_mix")
            s_mixc = sem("n0_mixc")
            s_sum = sem("n0_sum")
            s_copy = sem("n0_copy")
            s_scatter = [[sem(f"n0_scatter{b}{u}") for u in range(U)] for b in range(2)]
            row = [sbn(f"row{b}", [P, U * P], I32) for b in range(2)]
            hwin = [sbn(f"hwin{b}", [SPAN, D]) for b in range(2)]
            hot = sbn("hot", [P, 2, U, SPAN])
            wmat = sbn("wmat", [P, 2, U, P])
            junk = sbn("junk", [P, U, P])
            count = sbn("count", [P, 2, U])
            t_idx = sbn("t_idx", [P, U])
            sidx = [sbn(f"sidx{b}", [P, U], I32) for b in range(2)]
            mix = [sbn(f"mix{b}", [SPAN, U * P]) for b in range(2)]
            summed = sbn("summed", [P, 2, U, D])
            tabs = acc_tab[0]

            def later(i):
                return not isinstance(i, int)

            def pairs_of(eng, body):
                body(0)
                with eng.Fori(1, EGROUPS // 2) as i:
                    body(i)

            @block.sync
            def _(sp):
                with sp.If(sp.value_load(apart[:, :], min_val=0, max_val=1) == 0):
                    def body(i):
                        for b in range(2):
                            g = i * 2 + b
                            if later(i):
                                wait_apart(sp, s_count, g * U - U)
                            sp.dma_start(row[b][:, :], src[bass.ds(g * (U * P), U * P)]
                                         .partition_broadcast(P)).then_inc(s_row[b], 16)
                            start = sp.value_load(win_i[0:1, bass.ds(g, 1)], min_val=0, max_val=N_NODES - 1)
                            if later(i):
                                wait_apart(sp, s_sum, g * U - U)
                            sp.dma_start(hwin[b][:, :], h_tab[0][bass.ds(start, SPAN), :]).then_inc(s_hwin[b], 16)
                    pairs_of(sp, body)

            @block.vector
            def _(dve):
                with dve.If(dve.value_load(apart[:, :], min_val=0, max_val=1) == 0):
                    def body(i):
                        for b in range(2):
                            g = i * 2 + b
                            if later(i):
                                dve.wait_ge(s_mix, g - 1)
                            for u in range(U):
                                nc.vector.tensor_scalar(hot[:, b, u, :], iota_w[:, :], rel_f[:, bass.ds(g * U + u, 1)],
                                                        None, ALU.is_equal).then_inc(s_hot, 1)
                            dve.wait_ge(s_row[b], i * 16 + 16)
                            for u in range(U):
                                col = g * U + u
                                nc.vector.tensor_scalar(wmat[:, b, u, :], row[b][:, u * P:(u + 1) * P],
                                                        src_f[:, bass.ds(col, 1)], wgt_f[:, bass.ds(col, 1)],
                                                        ALU.is_equal, ALU.mult).then_inc(s_weights, 1)
                            dve.wait_ge(s_count, g * U)
                            for u in range(U):
                                nc.vector.scalar_tensor_tensor(
                                    junk[:, u, :], row[b][:, u * P:(u + 1) * P], src_f[:, bass.ds(g * U + u, 1)],
                                    lower[:, :], ALU.is_equal, ALU.mult,
                                    accum_out=count[:, b, u:u + 1]).then_inc(s_count, 1)
                            cols = src_f[:, bass.ds(g * U, U)]
                            dve.wait_ge(s_stage, g * 3)
                            nc.vector.tensor_scalar(t_idx[:, :], cols, -1.0, dump_row[:, 0:1],
                                                    ALU.mult, ALU.add).then_inc(s_stage, 1)
                            dve.wait_ge(s_count, g * U + U)
                            dve.wait_ge(s_stage, g * 3 + 1)
                            nc.vector.scalar_tensor_tensor(t_idx[:, :], count[:, b, :], 0.0, t_idx[:, :],
                                                           ALU.is_gt, ALU.mult).then_inc(s_stage, 1)
                            dve.wait_ge(s_stage, g * 3 + 2)
                            if later(i):
                                for u in range(U):
                                    dve.wait_ge(s_scatter[b][u], i * 16)
                            nc.vector.tensor_tensor(sidx[b][:, :], t_idx[:, :], cols, ALU.add).then_inc(s_stage, 1)
                    pairs_of(dve, body)

            @block.gpsimd
            def _(pool):
                with pool.If(pool.value_load(apart[:, :], min_val=0, max_val=1) == 0):
                    def body(i):
                        for b in range(2):
                            g = i * 2 + b
                            pool.wait_ge(s_stage, g * 3 + 3)
                            for u in range(U):
                                pool.wait_ge(s_copy, g * U + u + 1)
                                wait_apart(pool, s_scatter[b][u], i * 16)
                                nc.gpsimd.indirect_dma_start(
                                    tabs[b * U + u], bass.IndirectOffsetOnAxis(sidx[b][:, u:u + 1], 0), summed[:, b, u, :],
                                    None, bounds_check=TABLE_ROWS - 1, oob_is_err=True,
                                    compute_op=ALU.add).then_inc(s_scatter[b][u], 16)
                    pairs_of(pool, body)
                    for u in range(2 * U):
                        pool.wait_ge(s_scatter[u // U][u % U], EGROUPS // 2 * 16)

            @block.tensor
            def _(pe):
                with pe.If(pe.value_load(apart[:, :], min_val=0, max_val=1) == 0):
                    def mixes(g, b, first=False):
                        if not first:
                            pe.wait_ge(s_mixc, g - 1)
                        for u in range(U):
                            pe.wait_ge(s_hot, g * U + u + 1)
                            pe.wait_ge(s_weights, g * U + u + 1)
                            last = nc.tensor.matmul(bank[b][0:SPAN, u * P:(u + 1) * P], hot[:, b, u, :],
                                                    wmat[:, b, u, :], start=True, stop=True)
                        last.then_inc(s_mix, 1)

                    def sums(g, b, visit, first=False):
                        pe.wait_ge(s_mixc, g + 1)
                        pe.wait_ge(s_hwin[b], visit * 16 + 16)
                        for u in range(U):
                            if not first:
                                pe.wait_ge(s_copy, g * U - U + u + 1)
                            nc.tensor.matmul(bank[2 + u][:, 0:D], mix[b][:, u * P:(u + 1) * P], hwin[b][:, :],
                                             start=True, stop=True).then_inc(s_sum, 1)

                    mixes(0, 0, first=True)
                    mixes(1, 1, first=True)
                    sums(0, 0, 0, first=True)
                    with pe.Fori(1, EGROUPS // 2) as i:
                        mixes(i * 2, 0)
                        sums(i * 2 - 1, 1, i - 1)
                        mixes(i * 2 + 1, 1)
                        sums(i * 2, 0, i)
                    sums(EGROUPS - 1, 1, EGROUPS // 2 - 1)

            @block.scalar
            def _(act):
                with act.If(act.value_load(apart[:, :], min_val=0, max_val=1) == 0):
                    def mix_copy(g, b):
                        act.wait_ge(s_mix, g + 1)
                        nc.scalar.activation(mix[b][:, :], bank[b][0:SPAN, :], ACT.Copy).then_inc(s_mixc, 1)

                    def sum_copy(g, b, visit, early=False):
                        for u in range(U):
                            act.wait_ge(s_sum, g * U + u + 1)
                            if not early:
                                act.wait_ge(s_scatter[b][u], visit * 16)
                            nc.scalar.activation(summed[:, b, u, :], bank[2 + u][:, 0:D], ACT.Copy).then_inc(s_copy, 1)

                    mix_copy(0, 0)
                    mix_copy(1, 1)
                    sum_copy(0, 0, 0, early=True)
                    mix_copy(2, 0)
                    sum_copy(1, 1, 0, early=True)
                    mix_copy(3, 1)
                    sum_copy(2, 0, 1)
                    with act.Fori(2, EGROUPS // 2) as i:
                        mix_copy(i * 2, 0)
                        sum_copy(i * 2 - 1, 1, i - 1)
                        mix_copy(i * 2 + 1, 1)
                        sum_copy(i * 2, 0, i)
                    sum_copy(EGROUPS - 1, 1, EGROUPS // 2 - 1)


        with borrowed(pair0):
            edge_block(0, dst_f, src_f, src)

        class Tables:
            def __init__(s, n):
                s.load = sem(f"{n}_tload")
                s.used = sem(f"{n}_tused")

        def tables_load(sp, g, s, layer, acc_free):
            n = TABLES[layer]
            acc_free()
            sp.dma_start(acc[:, :, :], node_rows(acc_tab[layer][0], g)).then_inc(s.load, 16)
            for u in range(1, n):
                wait_apart(sp, s.load, g * (16 * n) + 16 * u)
                wait_apart(sp, s.used, g * (n - 1) + u - 1)
                sp.dma_start(part[:, :, :], node_rows(acc_tab[layer][u], g)).then_inc(s.load, 16)

        def tables_add(dve, g, s, layer):
            n = TABLES[layer]
            for u in range(1, n):
                dve.wait_ge(s.load, g * (16 * n) + 16 * u + 16)
                if u > 1:
                    dve.wait_ge(s.used, g * (n - 1) + u - 1)
                nc.vector.tensor_tensor(acc[:, :, :], acc[:, :, :], part[:, :, :], ALU.add).then_inc(s.used, 1)
            dve.wait_ge(s.used, g * (n - 1) + n - 1)

        with ExitStack() as c3, nc.Block() as block:
            def sb3(name, shape, dt=F32):
                return c3.enter_context(nc.sbuf_tensor(name, shape, dt))
            s_wraw = sem("f_wraw")
            s_whi = sem("f_whi")
            s_wlo = sem("f_wlo")
            s_small = sem("f_small")
            s_bn = sem("f_bn")
            s_bnroot = sem("f_bnroot")
            ln3 = LN("ln3")
            ln4 = LN("ln4")
            tb3 = Tables("f")
            s_glog = sem("f_glog")
            s_gate = sem("f_gate")
            s_gexp = sem("f_gexp")
            s_gtr = sem("f_gtr")
            s_gt = sem("f_gt")
            s_gbo = sem("f_gbo")
            s_acc0 = sem("f_acc0")
            s_xhi = sem("f_xhi")
            s_xlo = sem("f_xlo")
            s_mm = [sem(f"f_mm{i}") for i in range(3)]
            s_relu = [sem(f"f_relu{i}") for i in range(2)]
            s_hi = [sem(f"f_hi{i}") for i in range(2)]
            s_lo = [sem(f"f_lo{i}") for i in range(2)]
            s_out = sem("f_out")
            s_hmm = sem("f_hmm")
            s_hcopy = sem("f_hcopy")
            s_hst = sem("f_hst")
            s_base = sem("f_base")
            s_bst = sem("f_bst")

            raw = sb3("raw", [P, F, D])
            wsrc = (w1, w2, wo)
            whi = [sb3(f"whi{l}", [P, EXPERTS0, F, D], F32R) for l in range(3)]
            wlo = [sb3(f"wlo{l}", [P, EXPERTS0, F, D], F32R) for l in range(3)]
            bnp = sb3("bnp", [P, 2, 5, EXPERTS0, F])
            scl = sb3("scl", [P, 2, EXPERTS0, F])
            shf = sb3("shf", [P, 2, EXPERTS0, F])
            bnt = sb3("bnt", [P, 2, EXPERTS0, F])
            gws = sb3("gws", [P, F, EXPERTS0])
            gbs = sb3("gbs", [P, EXPERTS0])
            bos = sb3("bos", [EXPERTS0, D])
            lws = sb3("lws", [P, F, D])
            lbs = sb3("lbs", [P, D])
            glog = sb3("glog", [P, GT, EXPERTS0])
            gate = sb3("gate", [P, GT, EXPERTS0])
            gm = sb3("gm", [P, GT])
            gateT = sb3("gateT", [EXPERTS0, GT * P])
            xhi = sb3("xhi", [P, F, GT * P], F32R)
            xlo = sb3("xlo", [P, F, GT * P], F32R)
            xraw = sb3("xraw", [P, F, GT * P])
            rl = sb3("rl", [P, 2, F, W4])
            hhi = [sb3(f"hhi{i}", [P, F, W4], F32R) for i in range(2)]
            hlo = [sb3(f"hlo{i}", [P, F, W4], F32R) for i in range(2)]
            NPIECE = 3 * EXPERTS0
            STEPS = [(si, e) for si in range(len(SUBS)) for e in range(EXPERTS0)]
            NS = len(STEPS)
            OUTS = sum(w for _, w in SUBS) * EXPERTS0

            def tiles_before(j):
                return sum(SUBS[si][1] for si, _ in STEPS[:j])

            def three(pe, outp, hi_l, lo_l, hi_r, lo_r, first, last):
                nc.tensor.matmul(outp, hi_l, hi_r, start=first, stop=False)
                nc.tensor.matmul(outp, lo_l, hi_r, start=False, stop=False)
                return nc.tensor.matmul(outp, hi_l, lo_r, start=False, stop=last)

            @block.sync
            def _(sp):
                for l in range(3):
                    for e in range(EXPERTS0):
                        i = l * EXPERTS0 + e
                        if i:
                            sp.wait_ge(s_wlo, i)
                        sp.dma_start(raw[:, :, :], wsrc[l][e].rearrange("(f p) d -> p f d", p=P)).then_inc(s_wraw, 16)
                with sp.Fori(0, GROUPS) as g:
                    def acc_free():
                        wait_apart(sp, s_bst, g * 16)
                    tables_load(sp, g, tb3, 0, acc_free)
                    wait_apart(sp, s_hcopy, g * GT + GT)
                    sp.dma_start(node_rows(h_tab[1], g), part[:, :, :]).then_inc(s_hst, 16)
                    wait_apart(sp, s_base, g + 1)
                    sp.dma_start(node_rows(acc_tab[1][0], g), acc[:, :, :]).then_inc(s_bst, 16)
                    wait_apart(sp, s_hst, g * 16 + 16)
                sp.wait_ge(s_bst, 16 * GROUPS)

            @block.gpsimd
            def _(pool):
                for l, arrs in enumerate(((b1, g1, be1, m1, v1), (b2, g2, be2, m2, v2))):
                    for a, arr in enumerate(arrs):
                        pool.dma_start(bnp[:, l, a], arr).then_inc(s_small, 16)
                pool.dma_start(gws[:, :, :], gw.rearrange("(f p) e -> p f e", p=P)).then_inc(s_small, 16)
                pool.dma_start(gbs[:, :], gbr.partition_broadcast(P)).then_inc(s_small, 16)
                pool.dma_start(bos[:, :], bo).then_inc(s_small, 16)
                pool.dma_start(lws[:, :, :], lw.rearrange("(f p) d -> p f d", p=P)).then_inc(s_small, 16)
                pool.dma_start(lbs[:, :], lb.partition_broadcast(P)).then_inc(s_small, 16)

            @block.scalar
            def _(act):
                act.wait_ge(s_bn, 1)
                nc.scalar.activation(scl[:, :, :, :], bnt[:, :, :, :], ACT.Sqrt).then_inc(s_bnroot, 1)
                for i in range(NPIECE):
                    act.wait_ge(s_wraw, i * 16 + 16)
                    nc.scalar.activation(whi[i // EXPERTS0][:, i % EXPERTS0], raw[:, :, :], ACT.Copy).then_inc(s_whi, 1)
                act.wait_ge(s_bn, 10)
                with act.Fori(0, GROUPS) as g:
                    ln_root(act, g, ln3)
                    for k in range(GT):
                        act.wait_ge(ln3.tr, g * GT + k + 1)
                        act.wait_ge(s_hmm, g * GT)
                        nc.scalar.activation(xraw[:, :, k * P:(k + 1) * P], transposed(k), ACT.Copy).then_inc(ln3.xt, 1)
                    act.wait_ge(s_mm[0], g * (NS * F))
                    for k in range(GT):
                        act.wait_ge(ln3.xt, g * GT + k + 1)
                        nc.scalar.activation(xhi[:, :, k * P:(k + 1) * P], xraw[:, :, k * P:(k + 1) * P],
                                             ACT.Copy).then_inc(s_xhi, 1)
                    act.wait_ge(s_gate, g * 7 + 3)
                    nc.scalar.activation(gate[:, :, :], glog[:, :, :], ACT.Exp).then_inc(s_gexp, 1)
                    for k in range(GT):
                        act.wait_ge(s_gtr, g * GT + k + 1)
                        act.wait_ge(s_gbo, g * GT)
                        nc.scalar.activation(gateT[:, k * P:(k + 1) * P], bank[k % 2][0:EXPERTS0, 0:P],
                                             ACT.Copy).then_inc(s_gt, 1)

                    def relus(l, j):
                        si, e = STEPS[j]
                        n = SUBS[si][1] * P
                        for m in range(F):
                            act.wait_ge(s_mm[l], g * (NS * F) + j * F + m + 1)
                            if j:
                                act.wait_ge(s_lo[l], g * NS + j)
                            nc.scalar.activation(rl[:, l, m, 0:n], bank[2 + 2 * l + m][:, 0:n], ACT.Relu,
                                                 bias=shf[:, l, e, m:m + 1],
                                                 scale=scl[:, l, e, m:m + 1]).then_inc(s_relu[l], 1)
                        act.wait_ge(s_relu[l], g * (NS * F) + j * F + F)
                        if j:
                            if l == 0:
                                act.wait_ge(s_mm[1], g * (NS * F) + j * F)
                            else:
                                act.wait_ge(s_mm[2], g * OUTS + tiles_before(j))
                        nc.scalar.activation(hhi[l][:, :, 0:n], rl[:, l, :, 0:n], ACT.Copy).then_inc(s_hi[l], 1)

                    for j in range(NS + 1):
                        if j < NS:
                            relus(0, j)
                        if j >= 1:
                            relus(1, j - 1)
                    ln_root(act, g, ln4)
                    for k in range(GT):
                        act.wait_ge(ln4.tr, g * GT + k + 1)
                        nc.scalar.activation(xraw[:, :, k * P:(k + 1) * P], transposed(k), ACT.Copy).then_inc(ln4.xt, 1)
                    for k in range(GT):
                        act.wait_ge(s_hmm, g * GT + k + 1)
                        nc.scalar.activation(part[:, k, :], bank[2 + k % 2][:, 0:D], ACT.Copy).then_inc(s_hcopy, 1)

            @block.tensor
            def _(pe):
                pe.wait_ge(s_small, 16 * 15)
                pe.wait_ge(s_wlo, NPIECE)
                with pe.Fori(0, GROUPS) as g:
                    pe.wait_ge(s_hcopy, g * GT)
                    ln_transpose(pe, g, ln3)
                    pe.wait_ge(ln3.xt, g * GT + GT)
                    for k in range(GT):
                        for f in range(F):
                            last = nc.tensor.matmul(bank[6][:, k * EXPERTS0:(k + 1) * EXPERTS0],
                                                    xraw[:, f, k * P:(k + 1) * P], gws[:, f, :],
                                                    start=(f == 0), stop=(f == F - 1))
                    last.then_inc(s_glog, 1)
                    for k in range(GT):
                        if k == 0:
                            pe.wait_ge(s_gate, g * 7 + 7)
                        else:
                            if k >= 2:
                                pe.wait_ge(s_gt, g * GT + k - 1)
                        nc.tensor.transpose(bank[k % 2][0:EXPERTS0, 0:P], gate[:, k, :], ident[:, :]).then_inc(s_gtr, 1)
                    for k in range(GT):
                        pe.wait_ge(s_gt, g * GT + k + 1)
                        if k >= 2:
                            pe.wait_ge(s_acc0, g * GT + k - 1)
                        nc.tensor.matmul(bank[6 + k % 2][:, 0:D], gateT[:, k * P:(k + 1) * P], bos[:, :],
                                         start=True, stop=True).then_inc(s_gbo, 1)
                    pe.wait_ge(s_xhi, g * GT + GT)
                    pe.wait_ge(s_xlo, g * GT + GT)

                    def layer(l, j):
                        si, e = STEPS[j]
                        k0, w = SUBS[si]
                        n = w * P
                        if l == 0:
                            rh, rlo = (xhi[:, :, k0 * P:k0 * P + n], xlo[:, :, k0 * P:k0 * P + n])
                        else:
                            pe.wait_ge(s_hi[0], g * NS + j + 1)
                            pe.wait_ge(s_lo[0], g * NS + j + 1)
                            rh, rlo = hhi[0][:, :, 0:n], hlo[0][:, :, 0:n]
                        for m in range(F):
                            if j:
                                pe.wait_ge(s_relu[l], g * (NS * F) + (j - 1) * F + m + 1)
                            for f in range(F):
                                last = three(pe, bank[2 + 2 * l + m][:, 0:n],
                                             whi[l][:, e, f, m * P:(m + 1) * P], wlo[l][:, e, f, m * P:(m + 1) * P],
                                             rh[:, f, :], rlo[:, f, :], f == 0, f == F - 1)
                            last.then_inc(s_mm[l], 1)

                    def output(j):
                        si, e = STEPS[j]
                        w = SUBS[si][1]
                        pe.wait_ge(s_hi[1], g * NS + j + 1)
                        pe.wait_ge(s_lo[1], g * NS + j + 1)
                        for k in range(w):
                            i = tiles_before(j) + k
                            if i >= 2:
                                pe.wait_ge(s_out, g * OUTS + i - 1)
                            elif i < 2:
                                pe.wait_ge(s_acc0, g * GT + GT)
                            for f in range(F):
                                last = three(pe, bank[6 + i % 2][:, 0:D],
                                             hhi[1][:, f, k * P:(k + 1) * P], hlo[1][:, f, k * P:(k + 1) * P],
                                             whi[2][:, e, f, :], wlo[2][:, e, f, :], f == 0, f == F - 1)
                            last.then_inc(s_mm[2], 1)

                    for j in range(NS + 2):
                        if j < NS:
                            layer(0, j)
                        if 1 <= j <= NS:
                            layer(1, j - 1)
                        if j >= 2:
                            output(j - 2)
                    ln_transpose(pe, g, ln4)
                    for k in range(GT):
                        pe.wait_ge(ln4.xt, g * GT + k + 1)
                        if k >= 2:
                            pe.wait_ge(s_hcopy, g * GT + k - 1)
                        for f in range(F):
                            last = nc.tensor.matmul(bank[2 + k % 2][:, 0:D], xraw[:, f, k * P:(k + 1) * P],
                                                    lws[:, f, :], start=(f == 0), stop=(f == F - 1))
                        last.then_inc(s_hmm, 1)

            @block.vector
            def _(dve):
                dve.wait_ge(s_small, 16 * 15)
                nc.vector.tensor_scalar(bnt[:, :, :, :], bnp[:, :, 4], BN_EPS, None, ALU.add).then_inc(s_bn, 1)
                dve.wait_ge(s_bnroot, 1)
                steps = [
                    lambda: nc.vector.reciprocal(scl[:, :, :, :], scl[:, :, :, :]),
                    lambda: nc.vector.tensor_tensor(shf[:, :, :, :], scl[:, :, :, :], scl[:, :, :, :], ALU.mult),
                    lambda: nc.vector.tensor_tensor(shf[:, :, :, :], shf[:, :, :, :], bnt[:, :, :, :], ALU.mult),
                    lambda: nc.vector.tensor_scalar(shf[:, :, :, :], shf[:, :, :, :], -0.5, 1.5, ALU.mult, ALU.add),
                    lambda: nc.vector.tensor_tensor(scl[:, :, :, :], scl[:, :, :, :], shf[:, :, :, :], ALU.mult),
                    lambda: nc.vector.tensor_tensor(scl[:, :, :, :], scl[:, :, :, :], bnp[:, :, 1], ALU.mult),
                    lambda: nc.vector.tensor_tensor(shf[:, :, :, :], bnp[:, :, 0], bnp[:, :, 3], ALU.subtract),
                    lambda: nc.vector.tensor_tensor(shf[:, :, :, :], shf[:, :, :, :], scl[:, :, :, :], ALU.mult),
                    lambda: nc.vector.tensor_tensor(shf[:, :, :, :], shf[:, :, :, :], bnp[:, :, 2], ALU.add),
                ]
                for n, step in enumerate(steps):
                    step().then_inc(s_bn, 1)
                    dve.wait_ge(s_bn, n + 2)
                for i in range(NPIECE):
                    dve.wait_ge(s_whi, i + 1)
                    nc.vector.tensor_tensor(wlo[i // EXPERTS0][:, i % EXPERTS0], raw[:, :, :],
                                            whi[i // EXPERTS0][:, i % EXPERTS0].bitcast(F32),
                                            ALU.subtract).then_inc(s_wlo, 1)
                with dve.Fori(0, GROUPS) as g:
                    tables_add(dve, g, tb3, 0)
                    ln_vector(dve, g, ln3)
                    dve.wait_ge(s_glog, g + 1)
                    base = g * 7
                    nc.vector.tensor_tensor(glog[:, :, :], bank[6][:, 0:GT * EXPERTS0].rearrange("p (k e) -> p k e", k=GT),
                                            gbs[:, :].unsqueeze(1).broadcast_to([P, GT, EXPERTS0]),
                                            ALU.add).then_inc(s_gate, 1)
                    dve.wait_ge(s_gate, base + 1)
                    nc.vector.tensor_reduce(gm[:, :], glog[:, :, :], AX.X, ALU.max).then_inc(s_gate, 1)
                    dve.wait_ge(s_gate, base + 2)
                    nc.vector.tensor_tensor(glog[:, :, :], glog[:, :, :],
                                            gm[:, :].unsqueeze(2).broadcast_to([P, GT, EXPERTS0]),
                                            ALU.subtract).then_inc(s_gate, 1)
                    for k in range(GT):
                        dve.wait_ge(s_xhi, g * GT + k + 1)
                        nc.vector.tensor_tensor(xlo[:, :, k * P:(k + 1) * P], xraw[:, :, k * P:(k + 1) * P],
                                                xhi[:, :, k * P:(k + 1) * P].bitcast(F32), ALU.subtract).then_inc(s_xlo, 1)
                    dve.wait_ge(s_gexp, g + 1)
                    nc.vector.tensor_reduce(gm[:, :], gate[:, :, :], AX.X, ALU.add).then_inc(s_gate, 1)
                    dve.wait_ge(s_gate, base + 4)
                    nc.vector.reciprocal(gm[:, :], gm[:, :]).then_inc(s_gate, 1)
                    dve.wait_ge(s_gate, base + 5)
                    nc.vector.tensor_tensor(glog[:, :, :], gate[:, :, :],
                                            gm[:, :].unsqueeze(2).broadcast_to([P, GT, EXPERTS0]),
                                            ALU.mult).then_inc(s_gate, 1)
                    dve.wait_ge(s_gate, base + 6)
                    nc.vector.tensor_copy(gate[:, :, :], glog[:, :, :]).then_inc(s_gate, 1)
                    for k in range(GT):
                        dve.wait_ge(s_gbo, g * GT + k + 1)
                        nc.vector.tensor_tensor(acc[:, k, :], bank[6 + k % 2][:, 0:D], acc[:, k, :],
                                                ALU.add).then_inc(s_acc0, 1)
                    dve.wait_ge(s_acc0, g * GT + GT)
                    dve.wait_ge(s_gate, base + 7)

                    def lower_half(l, j):
                        n = SUBS[STEPS[j][0]][1] * P
                        dve.wait_ge(s_hi[l], g * NS + j + 1)
                        nc.vector.tensor_tensor(hlo[l][:, :, 0:n], rl[:, l, :, 0:n], hhi[l][:, :, 0:n].bitcast(F32),
                                                ALU.subtract).then_inc(s_lo[l], 1)

                    def add_out(j):
                        si, e = STEPS[j]
                        k0, w = SUBS[si]
                        for k in range(w):
                            i = tiles_before(j) + k
                            dve.wait_ge(s_mm[2], g * OUTS + i + 1)
                            if e:
                                dve.wait_ge(s_out, g * OUTS + i - w + 1)
                            nc.vector.scalar_tensor_tensor(acc[:, k0 + k, :], bank[6 + i % 2][:, 0:D],
                                                           gate[:, k0 + k, e:e + 1], acc[:, k0 + k, :],
                                                           ALU.mult, ALU.add).then_inc(s_out, 1)

                    for j in range(NS + 2):
                        if j < NS:
                            lower_half(0, j)
                        if j >= 2:
                            add_out(j - 2)
                        if 1 <= j <= NS:
                            lower_half(1, j - 1)
                    dve.wait_ge(s_out, g * OUTS + OUTS)
                    ln_vector(dve, g, ln4)
                    dve.wait_ge(ln4.xn, g * GT + GT)
                    nc.vector.tensor_tensor(acc[:, :, :], acc[:, :, :],
                                            lbs[:, :].unsqueeze(1).broadcast_to([P, GT, D]), ALU.add).then_inc(s_base, 1)

        pair1 = [sem(f"pair1_{j}") for j in range(48)]
        with borrowed(pair1), ExitStack() as c4, nc.Block() as block:
            def sb4(name, shape, dt=F32):
                return c4.enter_context(nc.sbuf_tensor(name, shape, dt))
            ln5 = LN("ln5n")
            s_got = [sem(f"n1_got{r}") for r in range(RING)]
            s_gidx = sem("n1_gidx")
            s_sw = sem("n1_sw")
            s_prod = sem("n1_prod")
            s_wadd = sem("n1_wadd")
            s_clear = sem("n1_clear")
            s_accin = sem("n1_accin")
            s_part = sem("n1_part")
            s_ptr = sem("n1_ptr")
            s_acc = sem("n1_acc")
            s_wt = sem("n1_wt")
            s_sel = sem("n1_sel")
            s_selc = sem("n1_selc")
            s_log = sem("n1_log")
            s_lg = sem("n1_lg")
            s_mx = sem("n1_mx")
            s_mi = sem("n1_mi")
            s_mf = sem("n1_mf")
            s_oh = sem("n1_oh")
            s_ohtr = sem("n1_ohtr")
            s_oht = sem("n1_oht")
            s_h = sem("n1_h")
            s_m = sem("n1_m")
            s_r = sem("n1_r")
            s_hm = sem("n1_hm")
            s_used = sem("n1_used")
            s_y = sem("n1_y")
            s_st = sem("n1_st")
            w1s = sb4("n1_w1s", [P, F, EXPERTS1 * HID1])
            w2s = sb4("n1_w2s", [P, PAIRS, D])
            b1s = sb4("n1_b1s", [P, PAIRS])
            b2s = sb4("n1_b2s", [EXPERTS1, D])
            b2u = sb4("n1_b2u", [EXPERTS1, D])
            rws = sb4("n1_rws", [P, F, EXPERTS1])
            rbs = sb4("n1_rbs", [P, EXPERTS1])
            io_i = sb4("n1_io_i", [P, EXPERTS1], I32)
            io_f = sb4("n1_io_f", [P, EXPERTS1])
            sel_f = sb4("n1_sel_f", [EXPERTS1, PAIRS * P])
            sel = sb4("n1_sel", [EXPERTS1, PAIRS * P], BF16)
            xnt = sb4("n1_xnt4", [P, F, GT * P])
            lg = sb4("n1_lg", [P, GT, EXPERTS1])
            mx = sb4("n1_mx", [P, GT, 8])
            mi = sb4("n1_mi", [P, GT, 8], U32)
            mf = sb4("n1_mf", [P, GT])
            oh = sb4("n1_oh", [P, GT, EXPERTS1])
            ohT = sb4("n1_ohT", [EXPERTS1, GT * P])
            ohTb = sb4("n1_ohTb", [EXPERTS1, GT * P], BF16)
            hr = sb4("n1_hr", [P, 2, W4])
            hm = [sb4(f"n1_hm{i}", [P, W4]) for i in range(2)]
            yb = sb4("n1_yb", [P, GT, D])
            sums_t = sb4("n1_sums_t", [P, F, ROWS + SPAN])
            part_t = sb4("n1_part_t", [P, F, GT * P])
            got = sb4("n1_got", [P, RING, U, D])
            sw = sb4("n1_sw", [P, 2, U, SPAN])
            gidx = [sb4(f"n1_gidx{h}", [P, HALF], I32) for h in range(2)]
            PREP = 9
            STEPS5 = [(si, q) for si in range(len(SUBS)) for q in range(PAIRS)]
            NS5 = len(STEPS5)

            def steps_at(i):
                after = lambda x: max(0, x - PREP + 1) * NS5 // (PHASE - PREP)
                return range(after(i - 1), after(i))

            def phases(eng, edges, ffn):
                for i in range(PHASE):
                    edges(0, i)
                with eng.Fori(1, GROUPS) as k:
                    for i in range(PHASE):
                        edges(k, i)
                        ffn(k - 1, k, i)
                for i in range(PHASE):
                    ffn(GROUPS - 1, GROUPS, i)

            def output_tile(k):
                return bank[4 + k // 2][:, (k % 2) * D:(k % 2) * D + D]

            @block.gpsimd
            def _(pool):
                with pool.If(pool.value_load(apart[:, :], min_val=0, max_val=1) == 0):
                    nc.gpsimd.iota(io_i[:, :], pattern=[[1, EXPERTS1]], base=0, channel_multiplier=0).then_inc(s_sel, 1)
                    nc.gpsimd.memset(sel_f[:, :], 0.0).then_inc(s_sel, 1)
                    pool.wait_ge(s_sel, 2)
                    v = sel_f[:, :].rearrange("e (x h) -> e x h", h=HID1)
                    nc.gpsimd.affine_select(out=v, in_=v, compare_op=ALU.not_equal, fill=1.0, base=0,
                                            pattern=[[-1, EXPERTS1], [0, HID1]], channel_multiplier=1).then_inc(s_sel, 1)

                    def edges(k, i):
                        if i in (0, PHASE // 2):
                            pool.wait_ge(s_gidx, k * 2 + (1 if i == 0 else 2))
                        if i >= RING or not isinstance(k, int):
                            wait_apart(pool, s_prod, k * PHASE + (i - RING + 1))
                        half = i // (PHASE // 2)
                        for u in range(U):
                            c = i * U + u - half * HALF
                            nc.gpsimd.indirect_dma_start(
                                got[:, i % RING, u, :], None, h_tab[1],
                                bass.IndirectOffsetOnAxis(gidx[half][:, c:c + 1], 0),
                                bounds_check=ROWS - 1, oob_is_err=True).then_inc(s_got[i % RING], 16)

                    for i in range(PHASE):
                        edges(0, i)
                    with pool.Fori(1, GROUPS) as k:
                        for i in range(PHASE):
                            edges(k, i)

            @block.sync
            def _(sp):
                with sp.If(sp.value_load(apart[:, :], min_val=0, max_val=1) == 0):
                    sp.dma_start(w1s[:, :, :], mw1.rearrange("(f p) n -> p f n", p=P)).then_inc(s_wt, 16)
                    sp.dma_start(w2s[:, :, :], mw2.rearrange("(q p) d -> p q d", p=P)).then_inc(s_wt, 16)
                    sp.dma_start(b1s[:, :], mb1).then_inc(s_wt, 16)
                    sp.dma_start(b2s[:, :], mb2).then_inc(s_wt, 16)
                    sp.dma_start(rws[:, :, :], rw.rearrange("(f p) e -> p f e", p=P)).then_inc(s_wt, 16)
                    sp.dma_start(rbs[:, :], rb.partition_broadcast(P)).then_inc(s_wt, 16)
                    with sp.Fori(0, GROUPS) as g:
                        wait_apart(sp, s_y, g * GT)
                        sp.dma_start(acc[:, :, :], node_rows(acc_tab[1][0], g)).then_inc(s_accin, 16)
                        wait_apart(sp, s_y, g * GT + GT)
                        sp.dma_start(node_rows(out, g), yb[:, :, :]).then_inc(s_st, 16)
                    sp.wait_ge(s_st, 16 * GROUPS)

            @block.scalar
            def _(act):
                with act.If(act.value_load(apart[:, :], min_val=0, max_val=1) == 0):
                    act.wait_ge(s_wt, 96)
                    def ffn(g, k_next, i):
                        if i == SLACK:
                            act.wait_ge(s_wadd, k_next * PHASE + (0 if isinstance(k_next, int) else SLACK))
                            act.wait_ge(s_ptr, g * GT)
                            nc.scalar.activation(part_t[:, :, :], sums_t[:, :, bass.ds(g * (GT * P), GT * P)],
                                                 ACT.Copy).then_inc(s_part, 1)
                        if i == SLACK + 1:
                            ln_root(act, g, ln5)
                            act.wait_ge(s_h, g * NS5)
                            for k in range(GT):
                                act.wait_ge(ln5.tr, g * GT + k + 1)
                                nc.scalar.activation(xnt[:, :, k * P:(k + 1) * P], transposed(k),
                                                     ACT.Copy).then_inc(ln5.xt, 1)
                        if i == SLACK + 4:
                            act.wait_ge(s_used, g * NS5)
                            for k in range(GT):
                                act.wait_ge(s_ohtr, g * GT + k + 1)
                                nc.scalar.activation(ohT[:, k * P:(k + 1) * P], bank[k % 2][0:EXPERTS1, 0:P],
                                                     ACT.Copy)
                                nc.scalar.activation(ohTb[:, k * P:(k + 1) * P], bank[k % 2][0:EXPERTS1, 0:P],
                                                     ACT.Copy).then_inc(s_oht, 1)
                        for j in steps_at(i):
                            si, q = STEPS5[j]
                            n = SUBS[si][1] * P
                            act.wait_ge(s_h, g * NS5 + j + 1)
                            if j >= 2:
                                act.wait_ge(s_hm, g * NS5 + j - 1)
                            nc.scalar.activation(hr[:, j % 2, 0:n], bank[0 + j % 2][:, 0:n], ACT.Relu,
                                                 bias=b1s[:, q:q + 1]).then_inc(s_r, 1)

                    phases(act, lambda k, i: None, ffn)

            @block.tensor
            def _(pe):
                with pe.If(pe.value_load(apart[:, :], min_val=0, max_val=1) == 0):
                    pe.wait_ge(s_wt, 96)
                    pe.wait_ge(s_selc, 2)
                    def edges(k, i):
                        g = k * PHASE + i
                        pe.wait_ge(s_got[i % RING], (k * (PHASE // RING) + i // RING + 1) * (16 * U))
                        pe.wait_ge(s_sw, g * U + U)
                        if i >= 2 or not isinstance(k, int):
                            pe.wait_ge(s_wadd, g - 1)
                        for f in range(F):
                            for u in range(U):
                                last = nc.tensor.matmul(bank[6 + i % 2][:, f * SPAN:(f + 1) * SPAN],
                                                        got[:, i % RING, u, f * P:(f + 1) * P], sw[:, i % 2, u, :],
                                                        start=(u == 0), stop=(u == U - 1))
                        last.then_inc(s_prod, 1)

                    def hidden(g, j):
                        si, q = STEPS5[j]
                        k0, w = SUBS[si]
                        n = w * P
                        if j >= 2:
                            pe.wait_ge(s_r, g * NS5 + j - 1)
                        for f in range(F):
                            last = nc.tensor.matmul(bank[j % 2][:, 0:n], w1s[:, f, q * P:(q + 1) * P],
                                                    xnt[:, f, k0 * P:k0 * P + n], start=(f == 0), stop=(f == F - 1))
                        last.then_inc(s_h, 1)
                        if j >= 2:
                            pe.wait_ge(s_hm, g * NS5 + j - 1)
                        nc.tensor.matmul(bank[2 + j % 2][:, 0:n], sel[:, q * P:(q + 1) * P],
                                         ohTb[:, k0 * P:k0 * P + n], start=True, stop=True).then_inc(s_m, 1)

                    def outputs(g, j):
                        si, q = STEPS5[j]
                        k0, w = SUBS[si]
                        if q == 0:
                            pe.wait_ge(s_y, g * GT + k0)
                            for k in range(w):
                                nc.tensor.matmul(output_tile(k), ohT[:, (k0 + k) * P:(k0 + k + 1) * P], b2s[:, :],
                                                 start=(k % 2 == 0), stop=False, skip_group_check=True)
                        pe.wait_ge(s_hm, g * NS5 + j + 1)
                        for k in range(w):
                            last = nc.tensor.matmul(output_tile(k), hm[j % 2][:, k * P:(k + 1) * P], w2s[:, q, :],
                                                    start=False, stop=(q == PAIRS - 1), skip_group_check=True)
                        last.then_inc(s_used, 1)

                    def ffn(g, k_next, i):
                        if i == SLACK + 1:
                            pe.wait_ge(s_r, g * NS5)
                            pe.wait_ge(s_part, g + 1)
                            for k in range(GT):
                                if k >= 2:
                                    pe.wait_ge(s_acc, g * GT + k - 1)
                                for f in range(F):
                                    last = nc.tensor.transpose(bank[k % 2][:, f * P:(f + 1) * P],
                                                               part_t[:, f, k * P:(k + 1) * P], ident[:, :])
                                last.then_inc(s_ptr, 1)
                        if i == SLACK + 3:
                            pe.wait_ge(s_acc, g * GT + GT)
                            ln_transpose(pe, g, ln5)
                            pe.wait_ge(s_hm, g * NS5)
                            for k in range(GT):
                                pe.wait_ge(ln5.xt, g * GT + k + 1)
                                for f in range(F):
                                    last = nc.tensor.matmul(bank[2][:, k * EXPERTS1:(k + 1) * EXPERTS1],
                                                            xnt[:, f, k * P:(k + 1) * P], rws[:, f, :],
                                                            start=(f == 0), stop=(f == F - 1))
                            last.then_inc(s_log, 1)
                        if i == SLACK + 5:
                            for k in range(GT):
                                pe.wait_ge(s_oh, g * GT + k + 1)
                                if k >= 2:
                                    pe.wait_ge(s_oht, g * GT + k - 1)
                                nc.tensor.transpose(bank[k % 2][0:EXPERTS1, 0:P], oh[:, k, :],
                                                    ident[:, :]).then_inc(s_ohtr, 1)
                            pe.wait_ge(s_oht, g * GT + GT)
                            hidden(g, 0)
                        for j in steps_at(i):
                            if j + 1 < NS5:
                                hidden(g, j + 1)
                            outputs(g, j)

                    phases(pe, edges, ffn)

            @block.vector
            def _(dve):
                with dve.If(dve.value_load(apart[:, :], min_val=0, max_val=1) == 0):
                    dve.wait_ge(s_wt, 96)
                    dve.wait_ge(s_sel, 3)
                    nc.vector.tensor_copy(sel[:, :], sel_f[:, :]).then_inc(s_selc, 1)
                    nc.vector.tensor_copy(io_f[:, :], io_i[:, :]).then_inc(s_selc, 1)
                    dve.wait_ge(s_selc, 2)
                    nc.vector.memset(sums_t[:, :, :], 0.0).then_inc(s_clear, 1)
                    nc.vector.tensor_copy(gidx[0][:, :], src_f[:, 0:HALF]).then_inc(s_gidx, 1)

                    def add_window(g, static_first=False):
                        start = dve.value_load(win_i[0:1, bass.ds(g, 1)], min_val=0, max_val=N_NODES - 1)
                        window = sums_t[:, :, bass.ds(start, SPAN)]
                        if static_first:
                            dve.wait_ge(s_clear, 1)
                        else:
                            dve.wait_ge(s_wadd, g)
                        dve.wait_ge(s_prod, g + 1)
                        nc.vector.tensor_tensor(window, bank[6 + g_parity[0]][:, 0:F * SPAN].rearrange("p (f n) -> p f n", f=F),
                                                window, ALU.add).then_inc(s_wadd, 1)

                    g_parity = [0]

                    def edges(k, i):
                        g = k * PHASE + i
                        if i >= 2 or not isinstance(k, int):
                            dve.wait_ge(s_prod, g - 1)
                        for u in range(U):
                            col = g * U + u
                            nc.vector.tensor_scalar(sw[:, i % 2, u, :], iota_w[:, :], rel_f[:, bass.ds(col, 1)],
                                                    wgt_f[:, bass.ds(col, 1)], ALU.is_equal, ALU.mult).then_inc(s_sw, 1)
                        if i >= 1 or not isinstance(k, int):
                            g_parity[0] = (i - 1) % 2
                            add_window(g - 1, static_first=isinstance(k, int) and i == 1)
                        if i == 2:
                            nc.vector.tensor_copy(gidx[1][:, :], src_f[:, bass.ds(k * (2 * HALF) + HALF, HALF)]).then_inc(s_gidx, 1)
                        if i == PHASE // 2 + 2:
                            nc.vector.tensor_copy(gidx[0][:, :], src_f[:, bass.ds(k * (2 * HALF) + 2 * HALF, HALF)]).then_inc(s_gidx, 1)

                    def finish(g, si):
                        k0, w = SUBS[si]
                        for k in range(w):
                            if k == 0:
                                dve.wait_ge(s_used, g * NS5 + PAIRS * (si + 1))
                            nc.vector.scalar_tensor_tensor(yb[:, k0 + k, :], output_tile(k), 0.0,
                                                           acc[:, k0 + k, :], ALU.max, ALU.add).then_inc(s_y, 1)

                    def ffn(g, k_next, i):
                        if i == 0 and isinstance(g, int):
                            g_parity[0] = 1
                            add_window(EGROUPS - 1)
                        if i == SLACK + 1:
                            dve.wait_ge(s_accin, g * 16 + 16)
                            for k in range(GT):
                                dve.wait_ge(s_ptr, g * GT + k + 1)
                                nc.vector.tensor_tensor(acc[:, k, :], bank[k % 2][:, 0:D], acc[:, k, :],
                                                        ALU.add).then_inc(s_acc, 1)
                        if i == SLACK + 2:
                            dve.wait_ge(s_acc, g * GT + GT)
                            ln_vector(dve, g, ln5)
                        if i == SLACK + 4:
                            dve.wait_ge(s_log, g + 1)
                            nc.vector.tensor_tensor(lg[:, :, :],
                                                    bank[2][:, 0:GT * EXPERTS1].rearrange("p (k e) -> p k e", k=GT),
                                                    rbs[:, :].unsqueeze(1).broadcast_to([P, GT, EXPERTS1]),
                                                    ALU.add).then_inc(s_lg, 1)
                            wait_apart(dve, s_lg, g + 1)
                            for k in range(GT):
                                nc.vector.max(mx[:, k, :], lg[:, k, :]).then_inc(s_mx, 1)
                            for k in range(GT):
                                wait_apart(dve, s_mx, g * GT + k + 1)
                                nc.vector.max_index(mi[:, k, :], mx[:, k, :], lg[:, k, :]).then_inc(s_mi, 1)
                            dve.wait_ge(s_mi, g * GT + GT)
                            nc.vector.tensor_copy(mf[:, :], mi[:, :, 0]).then_inc(s_mf, 1)
                            dve.wait_ge(s_mf, g + 1)
                            for k in range(GT):
                                nc.vector.tensor_scalar(oh[:, k, :], io_f[:, :], mf[:, k:k + 1], None,
                                                        ALU.is_equal).then_inc(s_oh, 1)
                            dve.wait_ge(s_st, g * 16)
                        for j in steps_at(i):
                            si, q = STEPS5[j]
                            if q == 1 and si:
                                finish(g, si - 1)
                            n = SUBS[si][1] * P
                            dve.wait_ge(s_r, g * NS5 + j + 1)
                            dve.wait_ge(s_m, g * NS5 + j + 1)
                            if j >= 2:
                                dve.wait_ge(s_used, g * NS5 + j - 1)
                            nc.vector.tensor_tensor(hm[j % 2][:, 0:n], bank[2 + j % 2][:, 0:n], hr[:, j % 2, 0:n],
                                                    ALU.mult).then_inc(s_hm, 1)
                        if i == PHASE - 1:
                            finish(g, len(SUBS) - 1)

                    phases(dve, edges, ffn)

        both = borrowed(pair1)
        both.__enter__()
        edge_block(1, src_f, dst_f, dst)

        with ExitStack() as c5, nc.Block() as block:
            def sb5(name, shape, dt=F32):
                return c5.enter_context(nc.sbuf_tensor(name, shape, dt))
            ln5 = LN("ln5")
            tb5 = Tables("m")
            s_wt = sem("m_wt")
            s_sel = sem("m_sel")
            s_selc = sem("m_selc")
            s_log = sem("m_log")
            s_lg = sem("m_lg")
            s_mx = sem("m_mx")
            s_mi = sem("m_mi")
            s_mf = sem("m_mf")
            s_oh = sem("m_oh")
            s_ohtr = sem("m_ohtr")
            s_oht = sem("m_oht")
            s_h = sem("m_h")
            s_m = sem("m_m")
            s_r = sem("m_r")
            s_hm = sem("m_hm")
            s_used = sem("m_used")
            s_y = sem("m_y")
            s_st = sem("m_st")
            w1s = sb5("w1s", [P, F, EXPERTS1 * HID1])
            w2s = sb5("w2s", [P, PAIRS, D])
            b1s = sb5("b1s", [P, PAIRS])
            b2s = sb5("b2s", [EXPERTS1, D])
            b2u = sb5("b2u", [EXPERTS1, D])
            rws = sb5("rws", [P, F, EXPERTS1])
            rbs = sb5("rbs", [P, EXPERTS1])
            io_i = sb5("io_i", [P, EXPERTS1], I32)
            io_f = sb5("io_f", [P, EXPERTS1])
            sel_f = sb5("sel_f", [EXPERTS1, PAIRS * P])
            sel = sb5("sel", [EXPERTS1, PAIRS * P], BF16)
            xnt = sb5("xnt5", [P, F, GT * P])
            lg = sb5("lg", [P, GT, EXPERTS1])
            mx = sb5("mx", [P, GT, 8])
            mi = sb5("mi", [P, GT, 8], U32)
            mf = sb5("mf", [P, GT])
            oh = sb5("oh", [P, GT, EXPERTS1])
            ohT = sb5("ohT", [EXPERTS1, GT * P])
            ohTb = sb5("ohTb", [EXPERTS1, GT * P], BF16)
            hr = sb5("hr", [P, 2, W4])
            hm = [sb5(f"hm{i}", [P, W4]) for i in range(2)]
            yb = sb5("yb", [P, GT, D])
            STEPS5 = [(si, q) for si in range(len(SUBS)) for q in range(PAIRS)]
            NS5 = len(STEPS5)

            @block.gpsimd
            def _(pool):
                with pool.If(pool.value_load(apart[:, :], min_val=0, max_val=1) == 1):
                    nc.gpsimd.iota(io_i[:, :], pattern=[[1, EXPERTS1]], base=0, channel_multiplier=0).then_inc(s_sel, 1)
                    nc.gpsimd.memset(sel_f[:, :], 0.0).then_inc(s_sel, 1)
                    pool.wait_ge(s_sel, 2)
                    v = sel_f[:, :].rearrange("e (x h) -> e x h", h=HID1)
                    nc.gpsimd.affine_select(out=v, in_=v, compare_op=ALU.not_equal, fill=1.0, base=0,
                                            pattern=[[-1, EXPERTS1], [0, HID1]], channel_multiplier=1).then_inc(s_sel, 1)

            @block.sync
            def _(sp):
                with sp.If(sp.value_load(apart[:, :], min_val=0, max_val=1) == 1):
                    sp.dma_start(w1s[:, :, :], mw1.rearrange("(f p) n -> p f n", p=P)).then_inc(s_wt, 16)
                    sp.dma_start(w2s[:, :, :], mw2.rearrange("(q p) d -> p q d", p=P)).then_inc(s_wt, 16)
                    sp.dma_start(b1s[:, :], mb1).then_inc(s_wt, 16)
                    sp.dma_start(b2s[:, :], mb2).then_inc(s_wt, 16)
                    sp.dma_start(rws[:, :, :], rw.rearrange("(f p) e -> p f e", p=P)).then_inc(s_wt, 16)
                    sp.dma_start(rbs[:, :], rb.partition_broadcast(P)).then_inc(s_wt, 16)
                    with sp.Fori(0, GROUPS) as g:
                        def acc_free():
                            wait_apart(sp, s_y, g * GT)
                        tables_load(sp, g, tb5, 1, acc_free)
                        wait_apart(sp, s_y, g * GT + GT)
                        sp.dma_start(node_rows(out, g), yb[:, :, :]).then_inc(s_st, 16)
                    sp.wait_ge(s_st, 16 * GROUPS)

            @block.scalar
            def _(act):
                with act.If(act.value_load(apart[:, :], min_val=0, max_val=1) == 1):
                    act.wait_ge(s_wt, 96)
                    with act.Fori(0, GROUPS) as g:
                        ln_root(act, g, ln5)
                        act.wait_ge(s_h, g * NS5)
                        for k in range(GT):
                            act.wait_ge(ln5.tr, g * GT + k + 1)
                            nc.scalar.activation(xnt[:, :, k * P:(k + 1) * P], transposed(k), ACT.Copy).then_inc(ln5.xt, 1)
                        act.wait_ge(s_used, g * NS5)
                        for k in range(GT):
                            act.wait_ge(s_ohtr, g * GT + k + 1)
                            nc.scalar.activation(ohT[:, k * P:(k + 1) * P], bank[k % 2][0:EXPERTS1, 0:P],
                                                 ACT.Copy)
                            nc.scalar.activation(ohTb[:, k * P:(k + 1) * P], bank[k % 2][0:EXPERTS1, 0:P],
                                                 ACT.Copy).then_inc(s_oht, 1)
                        for j, (si, q) in enumerate(STEPS5):
                            n = SUBS[si][1] * P
                            act.wait_ge(s_h, g * NS5 + j + 1)
                            if j >= 2:
                                act.wait_ge(s_hm, g * NS5 + j - 1)
                            nc.scalar.activation(hr[:, j % 2, 0:n], bank[0 + j % 2][:, 0:n], ACT.Relu,
                                                 bias=b1s[:, q:q + 1]).then_inc(s_r, 1)

            @block.tensor
            def _(pe):
                with pe.If(pe.value_load(apart[:, :], min_val=0, max_val=1) == 1):
                    pe.wait_ge(s_wt, 96)
                    pe.wait_ge(s_selc, 2)
                    with pe.Fori(0, GROUPS) as g:
                        pe.wait_ge(s_r, g * NS5)
                        ln_transpose(pe, g, ln5)
                        pe.wait_ge(s_hm, g * NS5)
                        for k in range(GT):
                            pe.wait_ge(ln5.xt, g * GT + k + 1)
                            for f in range(F):
                                last = nc.tensor.matmul(bank[2][:, k * EXPERTS1:(k + 1) * EXPERTS1],
                                                        xnt[:, f, k * P:(k + 1) * P], rws[:, f, :],
                                                        start=(f == 0), stop=(f == F - 1))
                        last.then_inc(s_log, 1)
                        for k in range(GT):
                            pe.wait_ge(s_oh, g * GT + k + 1)
                            if k >= 2:
                                pe.wait_ge(s_oht, g * GT + k - 1)
                            nc.tensor.transpose(bank[k % 2][0:EXPERTS1, 0:P], oh[:, k, :], ident[:, :]).then_inc(s_ohtr, 1)
                        pe.wait_ge(s_oht, g * GT + GT)

                        def hidden(j):
                            si, q = STEPS5[j]
                            k0, w = SUBS[si]
                            n = w * P
                            if j >= 2:
                                pe.wait_ge(s_r, g * NS5 + j - 1)
                            for f in range(F):
                                last = nc.tensor.matmul(bank[j % 2][:, 0:n], w1s[:, f, q * P:(q + 1) * P],
                                                        xnt[:, f, k0 * P:k0 * P + n], start=(f == 0), stop=(f == F - 1))
                            last.then_inc(s_h, 1)
                            if j >= 2:
                                pe.wait_ge(s_hm, g * NS5 + j - 1)
                            nc.tensor.matmul(bank[2 + j % 2][:, 0:n], sel[:, q * P:(q + 1) * P],
                                             ohTb[:, k0 * P:k0 * P + n], start=True, stop=True).then_inc(s_m, 1)

                        def outputs(j):
                            si, q = STEPS5[j]
                            k0, w = SUBS[si]
                            if q == 0:
                                pe.wait_ge(s_y, g * GT + k0)
                                for k in range(w):
                                    nc.tensor.matmul(bank[4 + k][:, 0:D], ohT[:, (k0 + k) * P:(k0 + k + 1) * P], b2s[:, :],
                                                     start=True, stop=False)
                            pe.wait_ge(s_hm, g * NS5 + j + 1)
                            for k in range(w):
                                last = nc.tensor.matmul(bank[4 + k][:, 0:D], hm[j % 2][:, k * P:(k + 1) * P], w2s[:, q, :],
                                                        start=False, stop=(q == PAIRS - 1))
                            last.then_inc(s_used, 1)

                        hidden(0)
                        for j in range(NS5):
                            if j + 1 < NS5:
                                hidden(j + 1)
                            outputs(j)

            @block.vector
            def _(dve):
                with dve.If(dve.value_load(apart[:, :], min_val=0, max_val=1) == 1):
                    dve.wait_ge(s_wt, 96)
                    dve.wait_ge(s_sel, 3)
                    nc.vector.tensor_copy(sel[:, :], sel_f[:, :]).then_inc(s_selc, 1)
                    nc.vector.tensor_copy(io_f[:, :], io_i[:, :]).then_inc(s_selc, 1)
                    dve.wait_ge(s_selc, 2)
                    with dve.Fori(0, GROUPS) as g:
                        tables_add(dve, g, tb5, 1)
                        ln_vector(dve, g, ln5)
                        dve.wait_ge(s_log, g + 1)
                        nc.vector.tensor_tensor(lg[:, :, :], bank[2][:, 0:GT * EXPERTS1].rearrange("p (k e) -> p k e", k=GT),
                                                rbs[:, :].unsqueeze(1).broadcast_to([P, GT, EXPERTS1]),
                                                ALU.add).then_inc(s_lg, 1)
                        wait_apart(dve, s_lg, g + 1)
                        for k in range(GT):
                            nc.vector.max(mx[:, k, :], lg[:, k, :]).then_inc(s_mx, 1)
                        for k in range(GT):
                            wait_apart(dve, s_mx, g * GT + k + 1)
                            nc.vector.max_index(mi[:, k, :], mx[:, k, :], lg[:, k, :]).then_inc(s_mi, 1)
                        dve.wait_ge(s_mi, g * GT + GT)
                        nc.vector.tensor_copy(mf[:, :], mi[:, :, 0]).then_inc(s_mf, 1)
                        dve.wait_ge(s_mf, g + 1)
                        for k in range(GT):
                            nc.vector.tensor_scalar(oh[:, k, :], io_f[:, :], mf[:, k:k + 1], None,
                                                    ALU.is_equal).then_inc(s_oh, 1)

                        def finish(si):
                            k0, w = SUBS[si]
                            for k in range(w):
                                if k == 0:
                                    dve.wait_ge(s_used, g * NS5 + PAIRS * (si + 1))
                                nc.vector.scalar_tensor_tensor(yb[:, k0 + k, :], bank[4 + k][:, 0:D], 0.0,
                                                               acc[:, k0 + k, :], ALU.max, ALU.add).then_inc(s_y, 1)

                        dve.wait_ge(s_st, g * 16)
                        for j, (si, q) in enumerate(STEPS5):
                            if q == 1 and si:
                                finish(si - 1)
                            n = SUBS[si][1] * P
                            dve.wait_ge(s_r, g * NS5 + j + 1)
                            dve.wait_ge(s_m, g * NS5 + j + 1)
                            if j >= 2:
                                dve.wait_ge(s_used, g * NS5 + j - 1)
                            nc.vector.tensor_tensor(hm[j % 2][:, 0:n], bank[2 + j % 2][:, 0:n], hr[:, j % 2, 0:n],
                                                    ALU.mult).then_inc(s_hm, 1)
                        finish(len(SUBS) - 1)
        both.__exit__(None, None, None)


INS = ["x", "src", "dst", "wgt", "wl", "wr", "bl", "br", "gw", "gbr",
       "w1", "b1", "g1", "be1", "m1", "v1", "w2", "b2", "g2", "be2", "m2", "v2", "wo", "bo",
       "lw", "lb", "rw", "rb", "mw1", "mb1", "mw2", "mb2"]


def kernel(x, src, dst, edge_weight, L0_gnn_weight_l, L0_gnn_bias_l, L0_gnn_weight_r, L0_gnn_bias_r,
           L0_ffn_Wr, L0_ffn_br, L0_ffn_W1, L0_ffn_b1, L0_ffn_g1, L0_ffn_be1, L0_ffn_m1, L0_ffn_v1,
           L0_ffn_W2, L0_ffn_b2, L0_ffn_g2, L0_ffn_be2, L0_ffn_m2, L0_ffn_v2, L0_ffn_Wo, L0_ffn_bo,
           L1_gnn_weight, L1_gnn_bias, L1_ffn_router_w, L1_ffn_router_b, L1_ffn_W1, L1_ffn_b1,
           L1_ffn_W2, L1_ffn_b2):
    import concourse.bacc as bacc
    from concourse.bass_utils import run_bass_kernel_spmd

    def padded(a, rows):
        a = np.asarray(a)
        return np.concatenate([a, np.zeros((rows - a.shape[0],) + a.shape[1:], a.dtype)])

    def repeated(a, rows):
        a = np.asarray(a)
        return np.concatenate([a, np.repeat(a[-1:], rows - a.shape[0])])

    def features_first(a):
        return np.asarray(a).reshape(EXPERTS0, F, P).transpose(2, 0, 1)

    arrays = [
        padded(x, ROWS), padded(src, E_PAD), repeated(dst, E_PAD), padded(edge_weight, E_PAD),
        L0_gnn_weight_l, L0_gnn_weight_r, L0_gnn_bias_l, L0_gnn_bias_r, L0_ffn_Wr, L0_ffn_br,
        L0_ffn_W1, *(features_first(a) for a in (L0_ffn_b1, L0_ffn_g1, L0_ffn_be1, L0_ffn_m1, L0_ffn_v1)),
        L0_ffn_W2, *(features_first(a) for a in (L0_ffn_b2, L0_ffn_g2, L0_ffn_be2, L0_ffn_m2, L0_ffn_v2)),
        L0_ffn_Wo, L0_ffn_bo, L1_gnn_weight, L1_gnn_bias,
        np.asarray(L1_ffn_router_w).transpose(1, 0), L1_ffn_router_b,
        np.asarray(L1_ffn_W1).transpose(1, 0, 2).reshape(D, EXPERTS1 * HID1),
        np.asarray(L1_ffn_b1).reshape(PAIRS, P).transpose(1, 0),
        np.asarray(L1_ffn_W2).reshape(EXPERTS1 * HID1, D), L1_ffn_b2,
    ]
    nc = bacc.Bacc("TRN2", target_bir_lowering=False, num_devices=1)
    feeds, args = {}, []
    for name, a in zip(INS, arrays):
        a = np.ascontiguousarray(a)
        feeds[f"in_{name}"] = a
        args.append(nc.dram_tensor(f"in_{name}", a.shape, mybir.dt.from_np(a.dtype), kind="ExternalInput").ap())
    out = nc.dram_tensor("out_rows", (ROWS, D), F32, kind="ExternalOutput").ap()
    build(nc, *args, out)
    r = run_bass_kernel_spmd(nc, [feeds], core_ids=[0])
    return r.results[0]["out_rows"][:N_NODES]
```

```python
from contextlib import ExitStack, contextmanager

import numpy as np
import concourse.bass as bass
from concourse import mybir

F32 = mybir.dt.float32
F32R = mybir.dt.float32r
BF16 = mybir.dt.bfloat16
I32 = mybir.dt.int32
U32 = mybir.dt.uint32
ALU = mybir.AluOpType
ACT = mybir.ActivationFunctionType
AX = mybir.AxisListType

P = 128
N_NODES = 6250
D = 256
F = D // P
E_EDGES = 100000
EXPERTS0 = 8
EXPERTS1 = 32
HID1 = 64
PAIRS = EXPERTS1 * HID1 // P

GT = 7
GROUPS = 7
ROWS = GROUPS * GT * P
SUBS = ((0, 4), (4, 3))
W4 = 4 * P

U = 4
TABLES = (U, U)
EDGE_TILES = 784
E_PAD = EDGE_TILES * P
EGROUPS = EDGE_TILES // U
TR = EDGE_TILES // GT
SPAN = 64
PHASE = EGROUPS // GROUPS
SLACK = 2
HALF = PHASE * U // 2
RING = 4
H_ROWS = ROWS + SPAN
TABLE_ROWS = ROWS + P
LN_EPS = 1e-5
BN_EPS = 1e-3


def build(nc, x, src, dst, wgt, wl, wr, bl, br, gw, gbr, w1, b1, g1, be1, m1, v1,
          w2, b2, g2, be2, m2, v2, wo, bo, lw, lb, rw, rb, mw1, mb1, mw2, mb2, out):
    ctx = ExitStack()
    with ctx:
        def sb(name, shape, dt=F32):
            return ctx.enter_context(nc.sbuf_tensor(name, shape, dt))

        lent = [None]

        def sem(name):
            if lent[0]:
                return lent[0].pop(0)
            return ctx.enter_context(nc.semaphore(name))

        @contextmanager
        def borrowed(handles):
            lent[0] = list(handles)
            yield
            lent[0] = None

        h_tab = [nc.dram_tensor(f"h_tab{i}", ((H_ROWS, ROWS)[i], D), F32, kind="Internal").ap() for i in range(2)]
        acc_tab = [[nc.dram_tensor(f"acc_tab{i}_{u}", (TABLE_ROWS, D), F32, kind="Internal").ap()
                    for u in range(TABLES[i])] for i in range(2)]

        ident = sb("ident", [P, P])
        lower = sb("lower", [P, P])
        dump_row = sb("dump_row", [P, 1])
        src_f = sb("src_f", [P, EDGE_TILES + HALF])
        dst_f = sb("dst_f", [P, EDGE_TILES])
        wgt_f = sb("wgt_f", [P, EDGE_TILES])

        win_i = sb("win_i", [1, EGROUPS], I32)
        rel_f = sb("rel_f", [P, EDGE_TILES])
        iota_w = sb("iota_w", [P, SPAN])
        apart = sb("apart", [1, 1], I32)

        bank = [ctx.enter_context(nc.psum_tensor(f"bank{i}", [P, 512], F32)) for i in range(8)]

        acc = sb("acc", [P, GT, D])
        part = sb("part", [P, GT, D])
        xn = sb("xn", [P, GT, D])
        stat = sb("stat", [P, GT, 6])
        mv = sb("mv", [P, GT, 2])
        ve = sb("ve", [P, GT])
        rstd = sb("rstd", [P, GT])
        tmp7 = sb("tmp7", [P, GT])

        s_apart = sem("s_apart")

        def wait_apart(eng, semaphore, value):
            eng.wait_ge(semaphore, value)
            eng.sem_inc(s_apart, 1)

        def node_rows(table, g):
            return table[bass.ds(g * (GT * P), GT * P), :].rearrange("(k p) d -> p k d", p=P)

        class LN:
            def __init__(s, n):
                s.stats = sem(f"{n}_stats")
                s.aggr = sem(f"{n}_aggr")
                s.var = sem(f"{n}_var")
                s.sd = sem(f"{n}_sd")
                s.newton = sem(f"{n}_newton")
                s.xn = sem(f"{n}_xn")
                s.tr = sem(f"{n}_tr")
                s.xt = sem(f"{n}_xt")

        def ln_stats(g, s, acc):
            for k in range(GT):
                last = nc.vector.bn_stats(stat[:, k, :], acc[:, k, :])
            last.then_inc(s.stats, 1)

        def ln_variance(dve, g, s):
            wait_apart(dve, s.stats, g + 1)
            for k in range(GT):
                last = nc.vector.bn_aggr(mv[:, k, :], stat[:, k, :])
            last.then_inc(s.aggr, 1)
            dve.wait_ge(s.aggr, g + 1)
            nc.vector.tensor_scalar(ve[:, :], mv[:, :, 1], LN_EPS, None, ALU.add).then_inc(s.var, 1)

        def ln_newton(dve, g, s):
            dve.wait_ge(s.sd, g + 1)
            nc.vector.reciprocal(rstd[:, :], rstd[:, :]).then_inc(s.newton, 1)
            dve.wait_ge(s.newton, g * 5 + 1)
            nc.vector.tensor_tensor(tmp7[:, :], rstd[:, :], rstd[:, :], ALU.mult).then_inc(s.newton, 1)
            dve.wait_ge(s.newton, g * 5 + 2)
            nc.vector.tensor_tensor(tmp7[:, :], tmp7[:, :], ve[:, :], ALU.mult).then_inc(s.newton, 1)
            dve.wait_ge(s.newton, g * 5 + 3)
            nc.vector.tensor_scalar(tmp7[:, :], tmp7[:, :], -0.5, 1.5, ALU.mult, ALU.add).then_inc(s.newton, 1)
            dve.wait_ge(s.newton, g * 5 + 4)
            nc.vector.tensor_tensor(rstd[:, :], rstd[:, :], tmp7[:, :], ALU.mult).then_inc(s.newton, 1)
            dve.wait_ge(s.newton, g * 5 + 5)
            dve.wait_ge(s.tr, g * GT)

        def ln_normalise(s, acc, xn, tiles):
            for k in tiles:
                nc.vector.tensor_scalar(xn[:, k, :], acc[:, k, :], mv[:, k, 0:1], rstd[:, k:k + 1],
                                        ALU.subtract, ALU.mult).then_inc(s.xn, 1)

        def ln_vector(dve, g, s, acc=acc, xn=xn):
            ln_stats(g, s, acc)
            ln_variance(dve, g, s)
            ln_newton(dve, g, s)
            ln_normalise(s, acc, xn, range(GT))

        def ln_root(act, g, s):
            act.wait_ge(s.var, g + 1)
            act.wait_ge(s.xn, g * GT)
            nc.scalar.activation(rstd[:, :], ve[:, :], ACT.Sqrt).then_inc(s.sd, 1)

        def ln_transpose(pe, g, s, xn=xn):
            for k in range(GT):
                pe.wait_ge(s.xn, g * GT + k + 1)
                pe.wait_ge(s.xt, g * GT + (k - 1 if k >= 2 else 0))
                for f in range(F):
                    last = nc.tensor.transpose(bank[k % 2][:, f * P:(f + 1) * P],
                                               xn[:, k, f * P:(f + 1) * P], ident[:, :])
                last.then_inc(s.tr, 1)

        def transposed(k):
            return bank[k % 2][:, 0:D].rearrange("p (f t) -> p f t", f=F)

        with ExitStack() as c1:
            def sb1(name, shape, dt=F32):
                return c1.enter_context(nc.sbuf_tensor(name, shape, dt))

            s_const = sem("s_const")
            s_zero = sem("s_zero")
            s_ezero = sem("s_ezero")
            s_eload = sem("s_eload")
            s_econv = sem("s_econv")
            s_etr = sem("s_etr")
            s_ecol = sem("s_ecol")
            s_w1 = sem("s_w1")
            s_bsum = sem("s_bsum")
            s_xin = [sem(f"s_xin{b}") for b in range(2)]
            s_mm = sem("s_mm")
            s_hcopy = sem("s_hcopy")
            s_hst = sem("s_hst")
            s_add1 = sem("s_add1")
            s_add2 = sem("s_add2")
            s_bst = sem("s_bst")
            s_idx = sem("s_idx")
            s_win = sem("s_win")
            s_winb = sem("s_winb")
            s_far = sem("s_far")
            s_farsum = sem("s_farsum")
            ln1 = LN("ln1")

            with ExitStack() as cc, nc.Block() as block:
                erow_i = sb1("erow_i", [TR, 3, GT, P], I32)
                erow_f = sb1("erow_f", [TR, 2, GT, P])
                wlr = sb1("wlr", [P, F, 2, D])
                biases = sb1("biases", [P, 2, D])
                xnt = sb1("xnt", [P, F, GT * P])
                hbuf = sb1("hbuf", [P, GT, D])
                base = sb1("base", [P, GT, D])
                zeros = sb1("zeros", [P, 2560])
                xb = (acc, part)
                idx_p = sb1("idx_p", [P, 1], I32)
                iota_i = sb1("iota_i", [P, SPAN], I32)
                low_i = sb1("low_i", [1, EGROUPS], I32)
                win_f = sb1("win_f", [1, EGROUPS])
                low_f = sb1("low_f", [1, EGROUPS])
                ones = sb1("ones", [P, P])
                far = sb1("far", [P, EDGE_TILES])
                far_n = sb1("far_n", [P, 1])
                late_n = sb1("late_n", [1, 1])

                @block.gpsimd
                def _(pool):
                    nc.gpsimd.memset(ident[:, :], 0.0).then_inc(s_idx, 1)
                    nc.gpsimd.memset(lower[:, :], 1.0).then_inc(s_idx, 1)
                    pool.wait_ge(s_idx, 2)
                    nc.gpsimd.affine_select(out=ident[:, :], in_=ident[:, :], compare_op=ALU.not_equal,
                                            fill=1.0, base=0, pattern=[[-1, P]],
                                            channel_multiplier=1).then_inc(s_const, 1)
                    nc.gpsimd.affine_select(out=lower[:, :], in_=lower[:, :], compare_op=ALU.is_gt,
                                            fill=0.0, base=0, pattern=[[-1, P]],
                                            channel_multiplier=1).then_inc(s_const, 1)
                    nc.gpsimd.iota(idx_p[:, :], pattern=[[0, 1]], base=ROWS,
                                   channel_multiplier=1).then_inc(s_const, 1)
                    nc.gpsimd.iota(iota_i[:, :], pattern=[[1, SPAN]], base=0,
                                   channel_multiplier=0).then_inc(s_const, 1)
                    low = low_i[:, :].rearrange("o (k i) -> o k i", i=PHASE)
                    nc.gpsimd.iota(low[:, :, 0:SLACK], pattern=[[GT * P, GROUPS], [0, SLACK]], base=-GT * P,
                                   channel_multiplier=0).then_inc(s_const, 1)
                    nc.gpsimd.iota(low[:, :, SLACK:PHASE], pattern=[[GT * P, GROUPS], [0, PHASE - SLACK]], base=0,
                                   channel_multiplier=0).then_inc(s_const, 1)
                    nc.gpsimd.memset(ones[:, :], 1.0).then_inc(s_const, 1)
                    nc.gpsimd.memset(src_f[:, EDGE_TILES:], 0.0)
                    nc.gpsimd.memset(zeros[:, :], 0.0).then_inc(s_zero, 1)

                @block.sync
                def _(sp):
                    for n, a in enumerate((src, dst, wgt)):
                        to = erow_i[:, n] if n < 2 else erow_i[:, n].bitcast(F32)
                        sp.dma_start(to, a.rearrange("(j r p) -> r j p", r=TR, p=P)).then_inc(s_eload, 16)
                    sp.dma_start(win_i[:, :], dst.rearrange("(g e) -> e g", e=U * P)[0:1, :],
                                 allow_slow_non_contiguous=True).then_inc(s_win, 16)
                    sp.dma_start(wlr[:, :, 0, :], wl.rearrange("(f p) d -> p f d", p=P)).then_inc(s_w1, 16)
                    sp.dma_start(wlr[:, :, 1, :], wr.rearrange("(f p) d -> p f d", p=P)).then_inc(s_w1, 16)
                    sp.dma_start(biases[:, 0, :], bl.partition_broadcast(P)).then_inc(s_w1, 16)
                    sp.dma_start(biases[:, 1, :], br.partition_broadcast(P)).then_inc(s_w1, 16)
                    sp.dma_start(xb[0][:, :, :], node_rows(x, 0)).then_inc(s_xin[0], 16)

                    def group(g, b, last=False):
                        if not last:
                            wait_apart(sp, s_add1, g * GT)
                            sp.dma_start(xb[1 - b][:, :, :], node_rows(x, g + 1)).then_inc(s_xin[1 - b], 16)
                        wait_apart(sp, s_hcopy, g * GT + GT)
                        sp.dma_start(node_rows(h_tab[0], g), hbuf[:, :, :]).then_inc(s_hst, 16)
                        wait_apart(sp, s_add2, g + 1)
                        sp.dma_start(node_rows(acc_tab[0][0], g), base[:, :, :]).then_inc(s_bst, 16)

                    with sp.Fori(0, GROUPS // 2) as i:
                        group(i * 2, 0)
                        group(i * 2 + 1, 1)
                    group(GROUPS - 1, 0, last=True)
                    sp.wait_ge(s_hst, 16 * GROUPS)
                    sp.wait_ge(s_bst, 16 * GROUPS)
                    sp.wait_ge(s_ezero, 16 * (5 * (TABLES[0] - 1) + 2))

                @block.scalar
                def _(act):
                    act.wait_ge(s_zero, 1)
                    act.dma_start(acc_tab[0][0][ROWS:TABLE_ROWS, :], zeros[:, 0:D]).then_inc(s_ezero, 16)
                    for u in range(1, TABLES[0]):
                        flat = acc_tab[0][u].rearrange("(p r) d -> p (r d)", p=P)
                        for c in range(5):
                            act.dma_start(flat[:, c * 2560:(c + 1) * 2560], zeros[:, :]).then_inc(s_ezero, 16)
                    act.dma_start(h_tab[0][ROWS:H_ROWS, :], zeros[0:SPAN, 0:D]).then_inc(s_ezero, 16)
                    for n, col in enumerate((src_f, dst_f, wgt_f)):
                        for j in range(GT):
                            act.wait_ge(s_etr, n * GT + j + 1)
                            nc.scalar.activation(col[:, j * TR:(j + 1) * TR],
                                                 bank[(n * GT + j) % 2][:, 0:TR], ACT.Copy).then_inc(s_ecol, 1)
                    def group(g, last=False):
                        for k in range(GT):
                            act.wait_ge(ln1.tr, g * GT + k + 1)
                            act.wait_ge(s_mm, g * GT)
                            nc.scalar.activation(xnt[:, :, k * P:(k + 1) * P], transposed(k),
                                                 ACT.Copy).then_inc(ln1.xt, 1)
                        if not last:
                            ln_root(act, g + 1, ln1)
                        act.wait_ge(s_hst, g * 16)
                        for k in range(GT):
                            act.wait_ge(s_mm, g * GT + k + 1)
                            nc.scalar.activation(hbuf[:, k, :], bank[2 + k % 2][:, 0:D],
                                                 ACT.Copy).then_inc(s_hcopy, 1)

                    ln_root(act, 0, ln1)
                    with act.Fori(0, GROUPS - 1) as g:
                        group(g)
                    group(GROUPS - 1, last=True)

                @block.tensor
                def _(pe):
                    pe.wait_ge(s_const, 1)
                    for n in range(3):
                        for j in range(GT):
                            i = n * GT + j
                            if n < 2:
                                pe.wait_ge(s_econv, n + 1)
                                rows = erow_f[:, n, j, :]
                            else:
                                pe.wait_ge(s_eload, 48)
                                rows = erow_i[:, 2, j, :].bitcast(F32)
                            if i >= 2:
                                pe.wait_ge(s_ecol, i - 1)
                            nc.tensor.transpose(bank[i % 2][:, 0:TR], rows,
                                                ident[0:TR, 0:TR]).then_inc(s_etr, 1)
                    pe.wait_ge(s_const, 7)
                    pe.wait_ge(s_winb, 2)
                    nc.tensor.matmul(bank[7][:, 0:EGROUPS], ones[0:1, :], win_f[:, :],
                                     start=True, stop=True).then_inc(s_winb, 1)
                    pe.wait_ge(s_far, 3)
                    nc.tensor.matmul(bank[6][0:1, 0:1], far_n[:, :], ones[:, 0:1],
                                     start=True, stop=True).then_inc(s_farsum, 1)
                    pe.wait_ge(s_ecol, 3 * GT)
                    pe.wait_ge(s_w1, 64)
                    with pe.Fori(0, GROUPS) as g:
                        ln_transpose(pe, g, ln1)
                        for k in range(GT):
                            pe.wait_ge(ln1.xt, g * GT + k + 1)
                            done = g * GT + (k - 1 if k >= 2 else 0)
                            pe.wait_ge(s_hcopy, done)
                            pe.wait_ge(s_add1, done)
                            for w in range(2):
                                for f in range(F):
                                    last = nc.tensor.matmul(bank[2 + 2 * w + k % 2][:, 0:D],
                                                            xnt[:, f, k * P:(k + 1) * P], wlr[:, f, w, :],
                                                            start=(f == 0), stop=(f == F - 1))
                            last.then_inc(s_mm, 1)

                @block.vector
                def _(dve):
                    dve.wait_ge(s_const, 6)
                    nc.vector.tensor_copy(dump_row[:, :], idx_p[:, :])
                    nc.vector.tensor_copy(iota_w[:, :], iota_i[:, :])
                    nc.vector.tensor_copy(low_f[:, :], low_i[:, :]).then_inc(s_bsum, 1)
                    dve.wait_ge(s_win, 16)
                    nc.vector.tensor_copy(win_f[:, :], win_i[:, :]).then_inc(s_winb, 2)
                    dve.wait_ge(s_eload, 48)
                    for n in range(2):
                        nc.vector.tensor_copy(erow_f[:, n], erow_i[:, n]).then_inc(s_econv, 1)
                    dve.wait_ge(s_winb, 3)
                    dve.wait_ge(s_ecol, 2 * GT)
                    nc.vector.tensor_tensor(rel_f[:, :].rearrange("p (g u) -> p g u", u=U),
                                            dst_f[:, :].rearrange("p (g u) -> p g u", u=U),
                                            bank[7][:, 0:EGROUPS].unsqueeze(2).broadcast_to([P, EGROUPS, U]),
                                            ALU.subtract).then_inc(s_far, 1)
                    dve.wait_ge(s_far, 1)
                    nc.vector.tensor_scalar(far[:, :], rel_f[:, :], float(SPAN), None, ALU.is_ge).then_inc(s_far, 1)
                    dve.wait_ge(s_far, 2)
                    nc.vector.scalar_tensor_tensor(far[:, :], rel_f[:, :], 0.0, far[:, :], ALU.is_lt, ALU.add,
                                                   accum_out=far_n[:, :]).then_inc(s_far, 1)
                    dve.wait_ge(s_bsum, 1)
                    nc.vector.tensor_tensor(low_f[:, :], low_f[:, :], win_f[:, :], ALU.is_gt).then_inc(s_far, 1)
                    dve.wait_ge(s_far, 4)
                    nc.vector.tensor_reduce(late_n[:, :], low_f[:, :], AX.X, ALU.add).then_inc(s_far, 1)
                    dve.wait_ge(s_far, 5)
                    dve.wait_ge(s_farsum, 1)
                    nc.vector.tensor_tensor(late_n[:, :], bank[6][0:1, 0:1], late_n[:, :], ALU.add).then_inc(s_far, 1)
                    dve.wait_ge(s_far, 6)
                    nc.vector.tensor_scalar(apart[:, :], late_n[:, :], 1.0, None, ALU.min).then_inc(s_far, 1)
                    dve.wait_ge(s_w1, 64)
                    nc.vector.tensor_tensor(biases[:, 0, :], biases[:, 0, :], biases[:, 1, :],
                                            ALU.add).then_inc(s_bsum, 1)
                    dve.wait_ge(s_bsum, 2)

                    def scales(g, b, visit):
                        dve.wait_ge(s_xin[b], visit * 16 + 16)
                        ln_stats(g, ln1, xb[b])
                        ln_variance(dve, g, ln1)
                        ln_newton(dve, g, ln1)

                    def group(g, b, next_visit, last=False):
                        ln_normalise(ln1, xb[b], xn, range(GT))
                        if not last:
                            dve.wait_ge(ln1.xn, g * GT + GT)
                            scales(g + 1, 1 - b, next_visit)
                        dve.wait_ge(s_bst, g * 16)
                        for k in range(GT):
                            dve.wait_ge(s_mm, g * GT + k + 1)
                            nc.vector.tensor_tensor(base[:, k, :], bank[4 + k % 2][:, 0:D], xb[b][:, k, :],
                                                    ALU.add).then_inc(s_add1, 1)
                        dve.wait_ge(s_add1, g * GT + GT)
                        nc.vector.tensor_tensor(base[:, :, :], base[:, :, :],
                                                biases[:, 0, :].unsqueeze(1).broadcast_to([P, GT, D]),
                                                ALU.add).then_inc(s_add2, 1)

                    scales(0, 0, 0)
                    with dve.Fori(0, GROUPS // 2) as i:
                        group(i * 2, 0, i)
                        group(i * 2 + 1, 1, i + 1)
                    group(GROUPS - 1, 0, None, last=True)

        def edge_block(layer, gather_f, scatter_f, scatter_rows):
            n = f"e{layer}"
            s_row = [sem(f"{n}_row{b}") for b in range(2)]
            s_weights = sem(f"{n}_weights")
            s_count = sem(f"{n}_count")
            s_stage = sem(f"{n}_stage")
            s_gather = [[sem(f"{n}_gather{b}{u}") for u in range(U)] for b in range(2)]
            s_sum = sem(f"{n}_sum")
            s_copy = sem(f"{n}_copy")
            s_scatter = [sem(f"{n}_scatter{u}") for u in range(U)]
            s_zero = sem(f"{n}_zero")
            s_clear = sem(f"{n}_clear")
            with ExitStack() as c2, nc.Block() as block:
                def sb2(name, shape, dt=F32):
                    return c2.enter_context(nc.sbuf_tensor(f"{n}_{name}", shape, dt))
                zeros = sb2("zeros", [P, 2560])
                row = [sb2(f"row{b}", [P, U * P], I32) for b in range(2)]
                wmat = sb2("wmat", [P, 2, U, P])
                junk = sb2("junk", [P, U, P])
                count = sb2("count", [P, 2, U])
                t_idx = sb2("t_idx", [P, U])
                gidx = [sb2(f"gidx{b}", [P, U], I32) for b in range(2)]
                sidx = [sb2(f"sidx{b}", [P, U], I32) for b in range(2)]
                got = sb2("got", [P, 2, U, D])
                summed = sb2("summed", [P, 2, U, D])
                h = h_tab[layer]
                tabs = acc_tab[layer]

                def later(i):
                    return not isinstance(i, int)

                def pairs_of(eng, body):
                    body(0)
                    with eng.Fori(1, EGROUPS // 2) as i:
                        body(i)

                @block.sync
                def _(sp):
                    with sp.If(sp.value_load(apart[:, :], min_val=0, max_val=1) == 1):
                        if layer == 1:
                            sp.wait_ge(s_zero, 1)
                            sp.dma_start(tabs[0][ROWS:TABLE_ROWS, :], zeros[:, 0:D]).then_inc(s_clear, 16)
                            for u in range(1, U):
                                flat = tabs[u].rearrange("(p r) d -> p (r d)", p=P)
                                for c in range(5):
                                    sp.dma_start(flat[:, c * 2560:(c + 1) * 2560], zeros[:, :]).then_inc(s_clear, 16)

                        def body(i):
                            for b in range(2):
                                if later(i):
                                    wait_apart(sp, s_count, i * (2 * U) + (b - 1) * U)
                                sp.dma_start(row[b][:, :], scatter_rows[bass.ds((i * 2 + b) * (U * P), U * P)]
                                             .partition_broadcast(P)).then_inc(s_row[b], 16)
                        pairs_of(sp, body)

                @block.vector
                def _(dve):
                    with dve.If(dve.value_load(apart[:, :], min_val=0, max_val=1) == 1):
                        def body(i):
                            for b in range(2):
                                g = i * 2 + b
                                dve.wait_ge(s_row[b], i * 16 + 16)
                                if later(i):
                                    dve.wait_ge(s_sum, g * U - U)
                                for u in range(U):
                                    col = g * U + u
                                    nc.vector.tensor_scalar(wmat[:, b, u, :], row[b][:, u * P:(u + 1) * P],
                                                            scatter_f[:, bass.ds(col, 1)], wgt_f[:, bass.ds(col, 1)],
                                                            ALU.is_equal, ALU.mult).then_inc(s_weights, 1)
                                dve.wait_ge(s_count, g * U)
                                for u in range(U):
                                    col = g * U + u
                                    nc.vector.scalar_tensor_tensor(
                                        junk[:, u, :], row[b][:, u * P:(u + 1) * P], scatter_f[:, bass.ds(col, 1)],
                                        lower[:, :], ALU.is_equal, ALU.mult,
                                        accum_out=count[:, b, u:u + 1]).then_inc(s_count, 1)
                                cols = scatter_f[:, bass.ds(g * U, U)]
                                dve.wait_ge(s_stage, g * 4)
                                nc.vector.tensor_scalar(t_idx[:, :], cols, -1.0, dump_row[:, 0:1],
                                                        ALU.mult, ALU.add).then_inc(s_stage, 1)
                                dve.wait_ge(s_count, g * U + U)
                                dve.wait_ge(s_stage, g * 4 + 1)
                                nc.vector.scalar_tensor_tensor(t_idx[:, :], count[:, b, :], 0.0, t_idx[:, :],
                                                               ALU.is_gt, ALU.mult).then_inc(s_stage, 1)
                                dve.wait_ge(s_stage, g * 4 + 2)
                                if later(i):
                                    for u in range(U):
                                        dve.wait_ge(s_scatter[u], g * 16 - 16)
                                nc.vector.tensor_tensor(sidx[b][:, :], t_idx[:, :], cols, ALU.add).then_inc(s_stage, 1)
                                nc.vector.tensor_copy(gidx[b][:, :], gather_f[:, bass.ds(g * U, U)]).then_inc(s_stage, 1)
                        pairs_of(dve, body)

                @block.gpsimd
                def _(pool):
                    with pool.If(pool.value_load(apart[:, :], min_val=0, max_val=1) == 1):
                        def gather(i, b, u):
                            g = i * 2 + b
                            if u == 0:
                                pool.wait_ge(s_stage, g * 4 + 4)
                            if later(i):
                                wait_apart(pool, s_sum, g * U - 2 * U + u + 1)
                            nc.gpsimd.indirect_dma_start(
                                got[:, b, u, :], None, h, bass.IndirectOffsetOnAxis(gidx[b][:, u:u + 1], 0),
                                bounds_check=ROWS - 1, oob_is_err=True).then_inc(s_gather[b][u], 16)

                        def scatter(g, b, u, first=False):
                            pool.wait_ge(s_copy, g * U + u + 1)
                            if not first:
                                wait_apart(pool, s_scatter[u], g * 16)
                            nc.gpsimd.indirect_dma_start(
                                tabs[u], bass.IndirectOffsetOnAxis(sidx[b][:, u:u + 1], 0), summed[:, b, u, :],
                                None, bounds_check=TABLE_ROWS - 1, oob_is_err=True,
                                compute_op=ALU.add).then_inc(s_scatter[u], 16)

                        if layer == 1:
                            nc.gpsimd.memset(zeros[:, :], 0.0).then_inc(s_zero, 1)
                        for u in range(U):
                            gather(0, 0, u)
                        if layer == 1:
                            pool.wait_ge(s_clear, 16 * (1 + 5 * (U - 1)))
                        for u in range(U):
                            gather(0, 1, u)
                            scatter(0, 0, u, first=True)
                        with pool.Fori(1, EGROUPS // 2) as i:
                            for u in range(U):
                                gather(i, 0, u)
                                scatter(i * 2 - 1, 1, u)
                            for u in range(U):
                                gather(i, 1, u)
                                scatter(i * 2, 0, u)
                        for u in range(U):
                            scatter(EGROUPS - 1, 1, u)
                        for u in range(U):
                            pool.wait_ge(s_scatter[u], EGROUPS * 16)

                @block.tensor
                def _(pe):
                    with pe.If(pe.value_load(apart[:, :], min_val=0, max_val=1) == 1):
                        def body(i):
                            for b in range(2):
                                g = i * 2 + b
                                for u in range(U):
                                    pe.wait_ge(s_weights, g * U + u + 1)
                                    pe.wait_ge(s_gather[b][u], i * 16 + 16)
                                    if later(i):
                                        pe.wait_ge(s_copy, g * U - 2 * U + u + 1)
                                    nc.tensor.matmul(bank[b * U + u][:, 0:D], wmat[:, b, u, :], got[:, b, u, :],
                                                     start=True, stop=True).then_inc(s_sum, 1)
                        pairs_of(pe, body)

                @block.scalar
                def _(act):
                    with act.If(act.value_load(apart[:, :], min_val=0, max_val=1) == 1):
                        def body(i):
                            for b in range(2):
                                g = i * 2 + b
                                for u in range(U):
                                    act.wait_ge(s_sum, g * U + u + 1)
                                    if later(i):
                                        act.wait_ge(s_scatter[u], g * 16 - 16)
                                    nc.scalar.activation(summed[:, b, u, :], bank[b * U + u][:, 0:D],
                                                         ACT.Copy).then_inc(s_copy, 1)
                        pairs_of(act, body)

        pair0 = [sem(f"pair0_{j}") for j in range(25)]
        with borrowed(pair0), ExitStack() as c2, nc.Block() as block:
            def sbn(name, shape, dt=F32):
                return c2.enter_context(nc.sbuf_tensor(f"n0_{name}", shape, dt))
            s_row = [sem(f"n0_row{b}") for b in range(2)]
            s_hwin = [sem(f"n0_hwin{b}") for b in range(2)]
            s_hot = sem("n0_hot")
            s_weights = sem("n0_weights")
            s_count = sem("n0_count")
            s_stage = sem("n0_stage")
            s_mix = sem("n0_mix")
            s_mixc = sem("n0_mixc")
            s_sum = sem("n0_sum")
            s_copy = sem("n0_copy")
            s_scatter = [sem(f"n0_scatter{u}") for u in range(U)]
            row = [sbn(f"row{b}", [P, U * P], I32) for b in range(2)]
            hwin = [sbn(f"hwin{b}", [SPAN, D]) for b in range(2)]
            hot = sbn("hot", [P, 2, U, SPAN])
            wmat = sbn("wmat", [P, 2, U, P])
            junk = sbn("junk", [P, U, P])
            count = sbn("count", [P, 2, U])
            t_idx = sbn("t_idx", [P, U])
            sidx = [sbn(f"sidx{b}", [P, U], I32) for b in range(4)]
            mix = [sbn(f"mix{b}", [SPAN, U * P]) for b in range(2)]
            summed = sbn("summed", [P, 2, U, D])
            tabs = acc_tab[0]

            def later(i):
                return not isinstance(i, int)

            def pairs_of(eng, body):
                body(0)
                with eng.Fori(1, EGROUPS // 2) as i:
                    body(i)

            def fours_of(eng, body):
                body(0)
                with eng.Fori(1, EGROUPS // 4) as i:
                    body(i)

            @block.sync
            def _(sp):
                with sp.If(sp.value_load(apart[:, :], min_val=0, max_val=1) == 0):
                    def body(i):
                        for b in range(2):
                            g = i * 2 + b
                            if later(i):
                                wait_apart(sp, s_count, g * U - U)
                            sp.dma_start(row[b][:, :], src[bass.ds(g * (U * P), U * P)]
                                         .partition_broadcast(P)).then_inc(s_row[b], 16)
                            start = sp.value_load(win_i[0:1, bass.ds(g, 1)], min_val=0, max_val=N_NODES - 1)
                            if later(i):
                                wait_apart(sp, s_sum, g * U - U)
                            sp.dma_start(hwin[b][:, :], h_tab[0][bass.ds(start, SPAN), :]).then_inc(s_hwin[b], 16)
                    pairs_of(sp, body)

            @block.vector
            def _(dve):
                with dve.If(dve.value_load(apart[:, :], min_val=0, max_val=1) == 0):
                    def body(i):
                        for b4 in range(4):
                            g = i * 4 + b4
                            b = b4 % 2
                            if later(i) or b4 >= 2:
                                dve.wait_ge(s_mix, g - 1)
                            for u in range(U):
                                nc.vector.tensor_scalar(hot[:, b, u, :], iota_w[:, :], rel_f[:, bass.ds(g * U + u, 1)],
                                                        None, ALU.is_equal).then_inc(s_hot, 1)
                            dve.wait_ge(s_row[b], i * 32 + (b4 // 2) * 16 + 16)
                            for u in range(U):
                                col = g * U + u
                                nc.vector.tensor_scalar(wmat[:, b, u, :], row[b][:, u * P:(u + 1) * P],
                                                        src_f[:, bass.ds(col, 1)], wgt_f[:, bass.ds(col, 1)],
                                                        ALU.is_equal, ALU.mult).then_inc(s_weights, 1)
                            dve.wait_ge(s_count, g * U)
                            for u in range(U):
                                nc.vector.scalar_tensor_tensor(
                                    junk[:, u, :], row[b][:, u * P:(u + 1) * P], src_f[:, bass.ds(g * U + u, 1)],
                                    lower[:, :], ALU.is_equal, ALU.mult,
                                    accum_out=count[:, b, u:u + 1]).then_inc(s_count, 1)
                            cols = src_f[:, bass.ds(g * U, U)]
                            dve.wait_ge(s_stage, g * 3)
                            nc.vector.tensor_scalar(t_idx[:, :], cols, -1.0, dump_row[:, 0:1],
                                                    ALU.mult, ALU.add).then_inc(s_stage, 1)
                            dve.wait_ge(s_count, g * U + U)
                            dve.wait_ge(s_stage, g * 3 + 1)
                            nc.vector.scalar_tensor_tensor(t_idx[:, :], count[:, b, :], 0.0, t_idx[:, :],
                                                           ALU.is_gt, ALU.mult).then_inc(s_stage, 1)
                            dve.wait_ge(s_stage, g * 3 + 2)
                            if later(i):
                                for u in range(U):
                                    dve.wait_ge(s_scatter[u], g * 16 - 48)
                            nc.vector.tensor_tensor(sidx[b4][:, :], t_idx[:, :], cols, ALU.add).then_inc(s_stage, 1)
                    fours_of(dve, body)

            @block.gpsimd
            def _(pool):
                with pool.If(pool.value_load(apart[:, :], min_val=0, max_val=1) == 0):
                    def body(i):
                        for b4 in range(4):
                            g = i * 4 + b4
                            pool.wait_ge(s_stage, g * 3 + 3)
                            for u in range(U):
                                pool.wait_ge(s_copy, g * U + u + 1)
                                wait_apart(pool, s_scatter[u], g * 16)
                                nc.gpsimd.indirect_dma_start(
                                    tabs[u], bass.IndirectOffsetOnAxis(sidx[b4][:, u:u + 1], 0), summed[:, b4 % 2, u, :],
                                    None, bounds_check=TABLE_ROWS - 1, oob_is_err=True,
                                    compute_op=ALU.add).then_inc(s_scatter[u], 16)
                    fours_of(pool, body)
                    for u in range(U):
                        pool.wait_ge(s_scatter[u], EGROUPS * 16)

            @block.tensor
            def _(pe):
                with pe.If(pe.value_load(apart[:, :], min_val=0, max_val=1) == 0):
                    def mixes(g, b, first=False):
                        if not first:
                            pe.wait_ge(s_mixc, g - 1)
                        for u in range(U):
                            pe.wait_ge(s_hot, g * U + u + 1)
                            pe.wait_ge(s_weights, g * U + u + 1)
                            last = nc.tensor.matmul(bank[b][0:SPAN, u * P:(u + 1) * P], hot[:, b, u, :],
                                                    wmat[:, b, u, :], start=True, stop=True)
                        last.then_inc(s_mix, 1)

                    def sums(g, b, visit, first=False):
                        pe.wait_ge(s_mixc, g + 1)
                        pe.wait_ge(s_hwin[b], visit * 16 + 16)
                        for u in range(U):
                            if not first:
                                pe.wait_ge(s_copy, g * U - U + u + 1)
                            nc.tensor.matmul(bank[2 + u][:, 0:D], mix[b][:, u * P:(u + 1) * P], hwin[b][:, :],
                                             start=True, stop=True).then_inc(s_sum, 1)

                    mixes(0, 0, first=True)
                    mixes(1, 1, first=True)
                    sums(0, 0, 0, first=True)
                    with pe.Fori(1, EGROUPS // 2) as i:
                        mixes(i * 2, 0)
                        sums(i * 2 - 1, 1, i - 1)
                        mixes(i * 2 + 1, 1)
                        sums(i * 2, 0, i)
                    sums(EGROUPS - 1, 1, EGROUPS // 2 - 1)

            @block.scalar
            def _(act):
                with act.If(act.value_load(apart[:, :], min_val=0, max_val=1) == 0):
                    def mix_copy(g, b):
                        act.wait_ge(s_mix, g + 1)
                        nc.scalar.activation(mix[b][:, :], bank[b][0:SPAN, :], ACT.Copy).then_inc(s_mixc, 1)

                    def sum_copy(g, b, early=False):
                        for u in range(U):
                            act.wait_ge(s_sum, g * U + u + 1)
                            if not early:
                                act.wait_ge(s_scatter[u], g * 16 - 16)
                            nc.scalar.activation(summed[:, b, u, :], bank[2 + u][:, 0:D], ACT.Copy).then_inc(s_copy, 1)

                    mix_copy(0, 0)
                    mix_copy(1, 1)
                    sum_copy(0, 0, early=True)
                    mix_copy(2, 0)
                    sum_copy(1, 1, early=True)
                    mix_copy(3, 1)
                    sum_copy(2, 0)
                    with act.Fori(2, EGROUPS // 2) as i:
                        mix_copy(i * 2, 0)
                        sum_copy(i * 2 - 1, 1)
                        mix_copy(i * 2 + 1, 1)
                        sum_copy(i * 2, 0)
                    sum_copy(EGROUPS - 1, 1)


        with borrowed(pair0):
            edge_block(0, dst_f, src_f, src)

        class Tables:
            def __init__(s, n):
                s.load = sem(f"{n}_tload")
                s.used = sem(f"{n}_tused")

        def tables_load(sp, g, s, layer, acc_free):
            n = TABLES[layer]
            acc_free()
            sp.dma_start(acc[:, :, :], node_rows(acc_tab[layer][0], g)).then_inc(s.load, 16)
            for u in range(1, n):
                wait_apart(sp, s.load, g * (16 * n) + 16 * u)
                wait_apart(sp, s.used, g * (n - 1) + u - 1)
                sp.dma_start(part[:, :, :], node_rows(acc_tab[layer][u], g)).then_inc(s.load, 16)

        def tables_add(dve, g, s, layer):
            n = TABLES[layer]
            for u in range(1, n):
                dve.wait_ge(s.load, g * (16 * n) + 16 * u + 16)
                if u > 1:
                    dve.wait_ge(s.used, g * (n - 1) + u - 1)
                nc.vector.tensor_tensor(acc[:, :, :], acc[:, :, :], part[:, :, :], ALU.add).then_inc(s.used, 1)
            dve.wait_ge(s.used, g * (n - 1) + n - 1)

        with ExitStack() as c3, nc.Block() as block:
            def sb3(name, shape, dt=F32):
                return c3.enter_context(nc.sbuf_tensor(name, shape, dt))
            s_whi = sem("f_whi")
            s_wlo = sem("f_wlo")
            s_small = sem("f_small")
            s_bn = sem("f_bn")
            s_bnroot = sem("f_bnroot")
            ln3 = LN("ln3")
            ln4 = LN("ln4")
            tb3 = Tables("f")
            s_glog = sem("f_glog")
            s_gate = sem("f_gate")
            s_gexp = sem("f_gexp")
            s_gtr = sem("f_gtr")
            s_gt = sem("f_gt")
            s_gbo = sem("f_gbo")
            s_acc0 = sem("f_acc0")
            s_xhi = sem("f_xhi")
            s_xlo = sem("f_xlo")
            s_mm = [sem(f"f_mm{i}") for i in range(3)]
            s_relu = [sem(f"f_relu{i}") for i in range(2)]
            s_hi = [sem(f"f_hi{i}") for i in range(2)]
            s_lo = [sem(f"f_lo{i}") for i in range(2)]
            s_out = sem("f_out")
            s_hmm = sem("f_hmm")
            s_hcopy = sem("f_hcopy")
            s_hst = sem("f_hst")
            s_base = sem("f_base")
            s_bst = sem("f_bst")

            pre = sb3("pre", [P, GT, D])
            raws = sb3("raws", [P, F, GT * P])
            raw = [raws[:, :, b * D:(b + 1) * D] for b in range(3)]
            x4 = raws
            s_wraw = [sem(f"f_wraw{b}") for b in range(3)]
            wsrc = (w1, w2, wo)
            whi = [sb3(f"whi{l}", [P, EXPERTS0, F, D], F32R) for l in range(3)]
            wlo = [sb3(f"wlo{l}", [P, EXPERTS0, F, D], F32R) for l in range(3)]
            bnp = acc[:, 0, 0:10 * EXPERTS0 * F].rearrange("p (l a e f) -> p l a e f", l=2, a=5, e=EXPERTS0)
            scl = sb3("scl", [P, 2, EXPERTS0, F])
            shf = sb3("shf", [P, 2, EXPERTS0, F])
            bnt = sb3("bnt", [P, 2, EXPERTS0, F])
            gws = sb3("gws", [P, F, EXPERTS0])
            gbs = sb3("gbs", [P, EXPERTS0])
            bos = sb3("bos", [EXPERTS0, D])
            lws = sb3("lws", [P, F, D])
            lbs = sb3("lbs", [P, D])
            glog = sb3("glog", [P, GT, EXPERTS0])
            gate = sb3("gate", [P, GT, EXPERTS0])
            gm = sb3("gm", [P, GT])
            gateT = sb3("gateT", [EXPERTS0, GT * P])
            xhi = sb3("xhi", [P, F, GT * P], F32R)
            xlo = sb3("xlo", [P, F, GT * P], F32R)
            xraw = sb3("xraw", [P, F, GT * P])
            rl = sb3("rl", [P, 2, F, W4])
            xn4 = rl[:, :, :, :].rearrange("p l f n -> p (l f n)")[:, 0:GT * D].rearrange("p (k d) -> p k d", k=GT)
            hhi = [[sb3(f"hhi{i}{b}", [P, F, W4], F32R) for b in range(2 - i)] for i in range(2)]
            hlo = [[sb3(f"hlo{i}{b}", [P, F, W4], F32R) for b in range(2 - i)] for i in range(2)]
            NPIECE = 3 * EXPERTS0
            STEPS = [(si, e) for si in range(len(SUBS)) for e in range(EXPERTS0)]
            NS = len(STEPS)
            AHEAD = 10
            OUTS = sum(w for _, w in SUBS) * EXPERTS0

            def tiles_before(j):
                return sum(SUBS[si][1] for si, _ in STEPS[:j])

            def three(pe, outp, hi_l, lo_l, hi_r, lo_r, first, last):
                nc.tensor.matmul(outp, hi_l, hi_r, start=first, stop=False)
                nc.tensor.matmul(outp, lo_l, hi_r, start=False, stop=False)
                return nc.tensor.matmul(outp, hi_l, lo_r, start=False, stop=last)

            @block.sync
            def _(sp):
                for l in range(3):
                    for e in range(EXPERTS0):
                        i = l * EXPERTS0 + e
                        if i >= 3:
                            sp.wait_ge(s_wlo, i - 2)
                        sp.dma_start(raw[i % 3],
                                     wsrc[l][e].rearrange("(f p) d -> p f d", p=P)).then_inc(s_wraw[i % 3], 16)
                N = TABLES[0]

                def load(g, before=None):
                    if before is not None:
                        wait_apart(sp, s_acc0, g * GT)
                    sp.dma_start(pre[:, :, :], node_rows(acc_tab[0][0], g)).then_inc(tb3.load, 16)
                    if before is not None:
                        wait_apart(sp, s_hst, before * 16)
                    for u in range(1, N):
                        wait_apart(sp, tb3.load, g * (16 * N) + 16 * u)
                        wait_apart(sp, tb3.used, g * (N - 1) + u - 1)
                        sp.dma_start(part[:, :, :], node_rows(acc_tab[0][u], g)).then_inc(tb3.load, 16)

                def group(g, last):
                    if not last:
                        load(g + 1, g)
                    wait_apart(sp, s_base, g + 1)
                    sp.dma_start(node_rows(acc_tab[1][0], g), acc[:, :, :]).then_inc(s_bst, 16)
                    wait_apart(sp, s_hcopy, g * GT + GT)
                    sp.dma_start(node_rows(h_tab[1], g), part[:, :, :]).then_inc(s_hst, 16)

                load(0)
                with sp.Fori(0, GROUPS - 1) as g:
                    group(g, False)
                group(GROUPS - 1, True)
                sp.wait_ge(s_bst, 16 * GROUPS)
                sp.wait_ge(s_hst, 16 * GROUPS)

            @block.gpsimd
            def _(pool):
                for l, arrs in enumerate(((b1, g1, be1, m1, v1), (b2, g2, be2, m2, v2))):
                    for a, arr in enumerate(arrs):
                        pool.dma_start(bnp[:, l, a], arr).then_inc(s_small, 16)
                pool.dma_start(gws[:, :, :], gw.rearrange("(f p) e -> p f e", p=P)).then_inc(s_small, 16)
                pool.dma_start(gbs[:, :], gbr.partition_broadcast(P)).then_inc(s_small, 16)
                pool.dma_start(bos[:, :], bo).then_inc(s_small, 16)
                pool.dma_start(lws[:, :, :], lw.rearrange("(f p) d -> p f d", p=P)).then_inc(s_small, 16)
                pool.dma_start(lbs[:, :], lb.partition_broadcast(P)).then_inc(s_small, 16)

            @block.scalar
            def _(act):
                act.wait_ge(s_bn, 1)
                nc.scalar.activation(scl[:, :, :, :], bnt[:, :, :, :], ACT.Sqrt).then_inc(s_bnroot, 1)
                for i in range(NPIECE):
                    act.wait_ge(s_wraw[i % 3], i // 3 * 16 + 16)
                    nc.scalar.activation(whi[i // EXPERTS0][:, i % EXPERTS0], raw[i % 3], ACT.Copy).then_inc(s_whi, 1)
                act.wait_ge(s_bn, 10)

                def operand(g):
                    act.wait_ge(s_xlo, g * GT)
                    for k in range(GT):
                        act.wait_ge(ln3.tr, g * GT + k + 1)
                        nc.scalar.activation(xraw[:, :, k * P:(k + 1) * P], transposed(k), ACT.Copy).then_inc(ln3.xt, 1)

                def upper_parts(g):
                    act.wait_ge(s_mm[0], g * (NS * F))
                    for k in range(GT):
                        act.wait_ge(ln3.xt, g * GT + k + 1)
                        nc.scalar.activation(xhi[:, :, k * P:(k + 1) * P], xraw[:, :, k * P:(k + 1) * P],
                                             ACT.Copy).then_inc(s_xhi, 1)

                def exponentials(g):
                    act.wait_ge(s_gate, g * 7 + 3)
                    nc.scalar.activation(gate[:, :, :], glog[:, :, :], ACT.Exp).then_inc(s_gexp, 1)

                def gates(g):
                    for k in range(GT):
                        act.wait_ge(s_gtr, g * GT + k + 1)
                        act.wait_ge(s_gbo, g * GT)
                        nc.scalar.activation(gateT[:, k * P:(k + 1) * P], bank[k % 2][0:EXPERTS0, 0:P],
                                             ACT.Copy).then_inc(s_gt, 1)

                def group(g, last):
                    def relus(l, j):
                        si, e = STEPS[j]
                        n = SUBS[si][1] * P
                        for m in range(F):
                            act.wait_ge(s_mm[l], g * (NS * F) + j * F + m + 1)
                            if j:
                                act.wait_ge(s_lo[l], g * NS + j)
                            nc.scalar.activation(rl[:, l, m, 0:n], bank[2 + 2 * l + m][:, 0:n], ACT.Relu,
                                                 bias=shf[:, l, e, m:m + 1],
                                                 scale=scl[:, l, e, m:m + 1]).then_inc(s_relu[l], 1)
                        act.wait_ge(s_relu[l], g * (NS * F) + j * F + F)
                        if l == 0:
                            if j >= 2:
                                act.wait_ge(s_mm[1], g * (NS * F) + (j - 1) * F)
                        else:
                            if j:
                                act.wait_ge(s_mm[2], g * OUTS + tiles_before(j))
                        nc.scalar.activation(hhi[l][j % (2 - l)][:, :, 0:n], rl[:, l, :, 0:n], ACT.Copy).then_inc(s_hi[l], 1)

                    for j in range(NS + 1):
                        if j < NS:
                            relus(0, j)
                        if j == 0:
                            gates(g)
                        if j >= 1:
                            relus(1, j - 1)
                        if j == AHEAD + 2 and not last:
                            ln_root(act, g + 1, ln3)
                    if not last:
                        operand(g + 1)
                    ln_root(act, g, ln4)
                    if not last:
                        upper_parts(g + 1)
                    act.wait_ge(s_hmm, g * GT)
                    for k in range(GT):
                        act.wait_ge(ln4.tr, g * GT + k + 1)
                        nc.scalar.activation(x4[:, :, k * P:(k + 1) * P], transposed(k), ACT.Copy).then_inc(ln4.xt, 1)
                    if not last:
                        exponentials(g + 1)
                        act.wait_ge(tb3.used, (g + 2) * (TABLES[0] - 1))
                    act.wait_ge(s_hst, g * 16)
                    for k in range(GT):
                        act.wait_ge(s_hmm, g * GT + k + 1)
                        nc.scalar.activation(part[:, k, :], bank[2 + k % 2][:, 0:D], ACT.Copy).then_inc(s_hcopy, 1)

                ln_root(act, 0, ln3)
                operand(0)
                upper_parts(0)
                exponentials(0)
                with act.Fori(0, GROUPS - 1) as g:
                    group(g, False)
                group(GROUPS - 1, True)

            @block.tensor
            def _(pe):
                pe.wait_ge(s_small, 16 * 15)
                pe.wait_ge(s_wlo, NPIECE)

                def head(g, n):
                    ln_transpose(pe, g, ln3, xn)
                    pe.wait_ge(ln3.xt, g * GT + GT)
                    pe.wait_ge(s_out, n * OUTS)
                    for k in range(GT):
                        for f in range(F):
                            last = nc.tensor.matmul(bank[6][:, k * EXPERTS0:(k + 1) * EXPERTS0],
                                                    xraw[:, f, k * P:(k + 1) * P], gws[:, f, :],
                                                    start=(f == 0), stop=(f == F - 1))
                    last.then_inc(s_glog, 1)

                def gate_products(g):
                    for k in range(GT):
                        if k == 0:
                            pe.wait_ge(s_gate, g * 7 + 7)
                        else:
                            if k >= 2:
                                pe.wait_ge(s_gt, g * GT + k - 1)
                        nc.tensor.transpose(bank[k % 2][0:EXPERTS0, 0:P], gate[:, k, :], ident[:, :]).then_inc(s_gtr, 1)
                    for k in range(GT):
                        pe.wait_ge(s_gt, g * GT + k + 1)
                        if k >= 2:
                            pe.wait_ge(s_acc0, g * GT + k - 1)
                        nc.tensor.matmul(bank[6 + k % 2][:, 0:D], gateT[:, k * P:(k + 1) * P], bos[:, :],
                                         start=True, stop=True).then_inc(s_gbo, 1)

                def group(g, last_group):
                    pe.wait_ge(s_hcopy, g * GT)
                    pe.wait_ge(s_xhi, g * GT + GT)
                    pe.wait_ge(s_xlo, g * GT + GT)

                    def layer(l, j):
                        si, e = STEPS[j]
                        k0, w = SUBS[si]
                        n = w * P
                        if l == 0:
                            rh, rlo = (xhi[:, :, k0 * P:k0 * P + n], xlo[:, :, k0 * P:k0 * P + n])
                        else:
                            pe.wait_ge(s_hi[0], g * NS + j + 1)
                            pe.wait_ge(s_lo[0], g * NS + j + 1)
                            rh, rlo = hhi[0][j % 2][:, :, 0:n], hlo[0][j % 2][:, :, 0:n]
                        for m in range(F):
                            if j:
                                pe.wait_ge(s_relu[l], g * (NS * F) + (j - 1) * F + m + 1)
                            for f in range(F):
                                last = three(pe, bank[2 + 2 * l + m][:, 0:n],
                                             whi[l][:, e, f, m * P:(m + 1) * P], wlo[l][:, e, f, m * P:(m + 1) * P],
                                             rh[:, f, :], rlo[:, f, :], f == 0, f == F - 1)
                            last.then_inc(s_mm[l], 1)

                    def output(j):
                        si, e = STEPS[j]
                        w = SUBS[si][1]
                        pe.wait_ge(s_hi[1], g * NS + j + 1)
                        pe.wait_ge(s_lo[1], g * NS + j + 1)
                        for k in range(w):
                            i = tiles_before(j) + k
                            if i >= 2:
                                pe.wait_ge(s_out, g * OUTS + i - 1)
                            elif i < 2:
                                pe.wait_ge(s_acc0, g * GT + GT)
                            for f in range(F):
                                last = three(pe, bank[6 + i % 2][:, 0:D],
                                             hhi[1][0][:, f, k * P:(k + 1) * P], hlo[1][0][:, f, k * P:(k + 1) * P],
                                             whi[2][:, e, f, :], wlo[2][:, e, f, :], f == 0, f == F - 1)
                            last.then_inc(s_mm[2], 1)

                    for j in range(NS + 2):
                        if j < NS:
                            layer(0, j)
                        if j == 0:
                            gate_products(g)
                        if 1 <= j <= NS:
                            layer(1, j - 1)
                        if j >= 2:
                            output(j - 2)
                    if not last_group:
                        head(g + 1, g + 1)
                    ln_transpose(pe, g, ln4, xn4)
                    for k in range(GT):
                        pe.wait_ge(ln4.xt, g * GT + k + 1)
                        if k >= 2:
                            pe.wait_ge(s_hcopy, g * GT + k - 1)
                        for f in range(F):
                            last = nc.tensor.matmul(bank[2 + k % 2][:, 0:D], x4[:, f, k * P:(k + 1) * P],
                                                    lws[:, f, :], start=(f == 0), stop=(f == F - 1))
                        last.then_inc(s_hmm, 1)

                head(0, 0)
                with pe.Fori(0, GROUPS - 1) as g:
                    group(g, False)
                group(GROUPS - 1, True)

            @block.vector
            def _(dve):
                dve.wait_ge(s_small, 16 * 15)
                nc.vector.tensor_scalar(bnt[:, :, :, :], bnp[:, :, 4], BN_EPS, None, ALU.add).then_inc(s_bn, 1)
                dve.wait_ge(s_bnroot, 1)
                steps = [
                    lambda: nc.vector.reciprocal(scl[:, :, :, :], scl[:, :, :, :]),
                    lambda: nc.vector.tensor_tensor(shf[:, :, :, :], scl[:, :, :, :], scl[:, :, :, :], ALU.mult),
                    lambda: nc.vector.tensor_tensor(shf[:, :, :, :], shf[:, :, :, :], bnt[:, :, :, :], ALU.mult),
                    lambda: nc.vector.tensor_scalar(shf[:, :, :, :], shf[:, :, :, :], -0.5, 1.5, ALU.mult, ALU.add),
                    lambda: nc.vector.tensor_tensor(scl[:, :, :, :], scl[:, :, :, :], shf[:, :, :, :], ALU.mult),
                    lambda: nc.vector.tensor_tensor(scl[:, :, :, :], scl[:, :, :, :], bnp[:, :, 1], ALU.mult),
                    lambda: nc.vector.tensor_tensor(shf[:, :, :, :], bnp[:, :, 0], bnp[:, :, 3], ALU.subtract),
                    lambda: nc.vector.tensor_tensor(shf[:, :, :, :], shf[:, :, :, :], scl[:, :, :, :], ALU.mult),
                    lambda: nc.vector.tensor_tensor(shf[:, :, :, :], shf[:, :, :, :], bnp[:, :, 2], ALU.add),
                ]
                for n, step in enumerate(steps):
                    step().then_inc(s_bn, 1)
                    dve.wait_ge(s_bn, n + 2)
                for i in range(NPIECE):
                    dve.wait_ge(s_whi, i + 1)
                    nc.vector.tensor_tensor(wlo[i // EXPERTS0][:, i % EXPERTS0], raw[i % 3],
                                            whi[i // EXPERTS0][:, i % EXPERTS0].bitcast(F32),
                                            ALU.subtract).then_inc(s_wlo, 1)
                N = TABLES[0]

                def add_table(g, u):
                    dve.wait_ge(tb3.load, g * (16 * N) + 16 * u + 16)
                    dve.wait_ge(tb3.used, g * (N - 1) + u - 1)
                    nc.vector.tensor_tensor(pre[:, :, :], pre[:, :, :], part[:, :, :], ALU.add).then_inc(tb3.used, 1)

                for u in range(1, N):
                    add_table(0, u)

                def logits(g):
                    dve.wait_ge(s_glog, g + 1)
                    base = g * 7
                    nc.vector.tensor_tensor(glog[:, :, :], bank[6][:, 0:GT * EXPERTS0].rearrange("p (k e) -> p k e", k=GT),
                                            gbs[:, :].unsqueeze(1).broadcast_to([P, GT, EXPERTS0]),
                                            ALU.add).then_inc(s_gate, 1)
                    dve.wait_ge(s_gate, base + 1)
                    nc.vector.tensor_reduce(gm[:, :], glog[:, :, :], AX.X, ALU.max).then_inc(s_gate, 1)
                    dve.wait_ge(s_gate, base + 2)
                    nc.vector.tensor_tensor(glog[:, :, :], glog[:, :, :],
                                            gm[:, :].unsqueeze(2).broadcast_to([P, GT, EXPERTS0]),
                                            ALU.subtract).then_inc(s_gate, 1)

                def lower_parts(g):
                    for k in range(GT):
                        dve.wait_ge(s_xhi, g * GT + k + 1)
                        nc.vector.tensor_tensor(xlo[:, :, k * P:(k + 1) * P], xraw[:, :, k * P:(k + 1) * P],
                                                xhi[:, :, k * P:(k + 1) * P].bitcast(F32), ALU.subtract).then_inc(s_xlo, 1)

                def gates(g):
                    base = g * 7
                    dve.wait_ge(s_gexp, g + 1)
                    nc.vector.tensor_reduce(gm[:, :], gate[:, :, :], AX.X, ALU.add).then_inc(s_gate, 1)
                    dve.wait_ge(s_gate, base + 4)
                    nc.vector.reciprocal(gm[:, :], gm[:, :]).then_inc(s_gate, 1)
                    dve.wait_ge(s_gate, base + 5)
                    nc.vector.tensor_tensor(glog[:, :, :], gate[:, :, :],
                                            gm[:, :].unsqueeze(2).broadcast_to([P, GT, EXPERTS0]),
                                            ALU.mult).then_inc(s_gate, 1)
                    dve.wait_ge(s_gate, base + 6)
                    nc.vector.tensor_copy(gate[:, :, :], glog[:, :, :]).then_inc(s_gate, 1)

                def first_rows(g):
                    dve.wait_ge(s_bst, g * 16)
                    for k in range(GT):
                        dve.wait_ge(s_gbo, g * GT + k + 1)
                        nc.vector.tensor_tensor(acc[:, k, :], bank[6 + k % 2][:, 0:D], pre[:, k, :],
                                                ALU.add).then_inc(s_acc0, 1)
                    dve.wait_ge(s_acc0, g * GT + GT)
                    dve.wait_ge(s_gate, g * 7 + 7)

                def group(g, last):

                    def lower_half(l, j):
                        n = SUBS[STEPS[j][0]][1] * P
                        dve.wait_ge(s_hi[l], g * NS + j + 1)
                        nc.vector.tensor_tensor(hlo[l][j % (2 - l)][:, :, 0:n], rl[:, l, :, 0:n],
                                                hhi[l][j % (2 - l)][:, :, 0:n].bitcast(F32),
                                                ALU.subtract).then_inc(s_lo[l], 1)

                    def add_out(j):
                        si, e = STEPS[j]
                        k0, w = SUBS[si]
                        for k in range(w):
                            i = tiles_before(j) + k
                            dve.wait_ge(s_mm[2], g * OUTS + i + 1)
                            if e:
                                dve.wait_ge(s_out, g * OUTS + i - w + 1)
                            nc.vector.scalar_tensor_tensor(acc[:, k0 + k, :], bank[6 + i % 2][:, 0:D],
                                                           gate[:, k0 + k, e:e + 1], acc[:, k0 + k, :],
                                                           ALU.mult, ALU.add).then_inc(s_out, 1)

                    for j in range(NS + 2):
                        if j < NS:
                            lower_half(0, j)
                        if j == 0:
                            first_rows(g)
                        if j >= 2:
                            add_out(j - 2)
                        if 1 <= j <= NS:
                            lower_half(1, j - 1)
                        if not last and j % 3 == 2 and j // 3 + 1 < N:
                            add_table(g + 1, j // 3 + 1)
                        if not last:
                            if j == AHEAD:
                                dve.wait_ge(ln4.xn, g * GT)
                                dve.wait_ge(tb3.used, (g + 1) * (N - 1) + N - 1)
                                ln_stats(g + 1, ln3, pre)
                            if j == AHEAD + 1:
                                ln_variance(dve, g + 1, ln3)
                            if j == AHEAD + 3:
                                ln_newton(dve, g + 1, ln3)
                                ln_normalise(ln3, pre, xn, range(0, 2))
                            if j == AHEAD + 4:
                                ln_normalise(ln3, pre, xn, range(2, 5))
                            if j == AHEAD + 5:
                                ln_normalise(ln3, pre, xn, range(5, GT))
                    if not last:
                        dve.wait_ge(ln3.xn, (g + 2) * GT)
                    dve.wait_ge(s_out, g * OUTS + OUTS)
                    dve.wait_ge(s_lo[1], g * NS + NS)
                    ln_vector(dve, g, ln4, acc, xn4)
                    dve.wait_ge(ln4.xn, g * GT + GT)
                    nc.vector.tensor_tensor(acc[:, :, :], acc[:, :, :],
                                            lbs[:, :].unsqueeze(1).broadcast_to([P, GT, D]), ALU.add).then_inc(s_base, 1)
                    if not last:
                        logits(g + 1)
                        lower_parts(g + 1)
                        gates(g + 1)

                dve.wait_ge(tb3.used, N - 1)
                ln_vector(dve, 0, ln3, pre, xn)
                logits(0)
                lower_parts(0)
                gates(0)
                with dve.Fori(0, GROUPS - 1) as g:
                    group(g, False)
                group(GROUPS - 1, True)

        pair1 = [sem(f"pair1_{j}") for j in range(48)]
        with borrowed(pair1), ExitStack() as c4, nc.Block() as block:
            def sb4(name, shape, dt=F32):
                return c4.enter_context(nc.sbuf_tensor(name, shape, dt))
            ln5 = LN("ln5n")
            s_got = [sem(f"n1_got{r}") for r in range(RING)]
            s_gidx = sem("n1_gidx")
            s_sw = sem("n1_sw")
            s_prod = sem("n1_prod")
            s_wadd = sem("n1_wadd")
            s_clear = sem("n1_clear")
            s_accin = sem("n1_accin")
            s_part = sem("n1_part")
            s_ptr = sem("n1_ptr")
            s_acc = sem("n1_acc")
            s_wt = sem("n1_wt")
            s_sel = sem("n1_sel")
            s_selc = sem("n1_selc")
            s_log = sem("n1_log")
            s_lg = sem("n1_lg")
            s_mx = sem("n1_mx")
            s_mi = sem("n1_mi")
            s_mf = sem("n1_mf")
            s_oh = sem("n1_oh")
            s_ohtr = sem("n1_ohtr")
            s_oht = sem("n1_oht")
            s_h = sem("n1_h")
            s_m = sem("n1_m")
            s_r = sem("n1_r")
            s_hm = sem("n1_hm")
            s_used = sem("n1_used")
            s_y = sem("n1_y")
            s_st = sem("n1_st")
            w1h = sb4("n1_w1h", [P, F, EXPERTS1 * HID1], F32R)
            w1l = sb4("n1_w1l", [P, F, EXPERTS1 * HID1], F32R)
            w2s = sb4("n1_w2s", [P, PAIRS, D])
            s_wup = sem("n1_wup")
            s_wsplit = sem("n1_wsplit")
            s_xup = sem("n1_xup")
            s_xsplit = sem("n1_xsplit")
            b1s = sb4("n1_b1s", [P, PAIRS])
            b2s = sb4("n1_b2s", [EXPERTS1, D])
            rws = sb4("n1_rws", [P, F, EXPERTS1])
            rbs = sb4("n1_rbs", [P, EXPERTS1])
            io_i = sb4("n1_io_i", [P, EXPERTS1], I32)
            io_f = sb4("n1_io_f", [P, EXPERTS1])
            sel_f = sb4("n1_sel_f", [EXPERTS1, PAIRS * P])
            sel = sb4("n1_sel", [EXPERTS1, PAIRS * P], BF16)
            xnl = sb4("n1_xnl", [P, F, GT * P], F32R)
            xnh = sb4("n1_xnh", [P, F, GT * P], F32R)
            lg = sb4("n1_lg", [P, GT, EXPERTS1])
            mx = sb4("n1_mx", [P, GT, 8])
            mi = sb4("n1_mi", [P, GT, 8], U32)
            mf = sb4("n1_mf", [P, GT])
            oh = sb4("n1_oh", [P, GT, EXPERTS1])
            ohT = sb4("n1_ohT", [EXPERTS1, GT * P])
            ohTb = sb4("n1_ohTb", [EXPERTS1, GT * P], BF16)
            hr = sb4("n1_hr", [P, 2, W4])
            hm = [sb4(f"n1_hm{i}", [P, W4]) for i in range(2)]
            yb = part
            sums_t = sb4("n1_sums_t", [P, F, ROWS + SPAN])
            part_t = sb4("n1_part_t", [P, F, GT * P])
            xnt = part_t
            PIECES = ((0, GT * P, part_t), (GT * P, GT * P, part[:, :, :].rearrange("p k d -> p (k d)")
                                            .rearrange("p (f n) -> p f n", f=F)),
                      (2 * GT * P, EXPERTS1 * HID1 - 2 * GT * P, hr))
            got = sb4("n1_got", [P, RING, U, D])
            sw = sb4("n1_sw", [P, 2, U, SPAN])
            gidx = [sb4(f"n1_gidx{h}", [P, HALF], I32) for h in range(2)]
            PREP_AT = {n + 1: SLACK + at for n, at in enumerate((0, 0, 0, 0, 0))}
            PREP = SLACK + 1
            STEPS5 = [(si, q) for si in range(len(SUBS)) for q in range(PAIRS)]
            NS5 = len(STEPS5)

            def steps_at(i):
                after = lambda x: max(0, x - PREP + 1) * NS5 // (PHASE - PREP)
                return range(after(i - 1), after(i))

            def phases(eng, edges, ffn, ready=lambda: None):
                for i in range(PHASE):
                    edges(0, i)
                ready()
                with eng.Fori(1, GROUPS) as k:
                    for i in range(PHASE):
                        edges(k, i)
                        ffn(k - 1, k, i)
                for i in range(PHASE):
                    ffn(GROUPS - 1, GROUPS, i)

            def output_tile(k):
                return bank[4 + k // 2][:, (k % 2) * D:(k % 2) * D + D]

            @block.gpsimd
            def _(pool):
                with pool.If(pool.value_load(apart[:, :], min_val=0, max_val=1) == 0):
                    def edges(k, i):
                        if i in (0, PHASE // 2):
                            pool.wait_ge(s_gidx, k * 2 + (1 if i == 0 else 2))
                        if i >= RING or not isinstance(k, int):
                            wait_apart(pool, s_prod, k * PHASE + (i - RING + 1))
                        half = i // (PHASE // 2)
                        for u in range(U):
                            c = i * U + u - half * HALF
                            nc.gpsimd.indirect_dma_start(
                                got[:, i % RING, u, :], None, h_tab[1],
                                bass.IndirectOffsetOnAxis(gidx[half][:, c:c + 1], 0),
                                bounds_check=ROWS - 1, oob_is_err=True).then_inc(s_got[i % RING], 16)

                    for i in range(RING):
                        edges(0, i)
                    nc.gpsimd.iota(io_i[:, :], pattern=[[1, EXPERTS1]], base=0, channel_multiplier=0).then_inc(s_sel, 1)
                    nc.gpsimd.memset(sel_f[:, :], 0.0).then_inc(s_sel, 1)
                    pool.wait_ge(s_sel, 2)
                    v = sel_f[:, :].rearrange("e (x h) -> e x h", h=HID1)
                    nc.gpsimd.affine_select(out=v, in_=v, compare_op=ALU.not_equal, fill=1.0, base=0,
                                            pattern=[[-1, EXPERTS1], [0, HID1]], channel_multiplier=1).then_inc(s_sel, 1)
                    for i in range(RING, PHASE):
                        edges(0, i)
                    with pool.Fori(1, GROUPS) as k:
                        for i in range(PHASE):
                            edges(k, i)

            @block.sync
            def _(sp):
                with sp.If(sp.value_load(apart[:, :], min_val=0, max_val=1) == 0):
                    for at, n, raw in PIECES:
                        sp.dma_start(raw[:, :, 0:n], mw1.rearrange("(f p) n -> p f n", p=P)[:, :, at:at + n]).then_inc(s_wt, 16)
                    sp.dma_start(w2s[:, :, :], mw2.rearrange("(q p) d -> p q d", p=P)).then_inc(s_wt, 16)
                    sp.dma_start(b1s[:, :], mb1).then_inc(s_wt, 16)
                    sp.dma_start(b2s[:, :], mb2).then_inc(s_wt, 16)
                    sp.dma_start(rws[:, :, :], rw.rearrange("(f p) e -> p f e", p=P)).then_inc(s_wt, 16)
                    sp.dma_start(rbs[:, :], rb.partition_broadcast(P)).then_inc(s_wt, 16)
                    with sp.Fori(0, GROUPS) as g:
                        wait_apart(sp, s_y, g * GT)
                        sp.dma_start(acc[:, :, :], node_rows(acc_tab[1][0], g)).then_inc(s_accin, 16)
                        wait_apart(sp, s_y, g * GT + GT)
                        sp.dma_start(node_rows(out, g), yb[:, :, :]).then_inc(s_st, 16)
                    sp.wait_ge(s_st, 16 * GROUPS)

            @block.scalar
            def _(act):
                with act.If(act.value_load(apart[:, :], min_val=0, max_val=1) == 0):
                    act.wait_ge(s_wt, 128)
                    for at, n, raw in PIECES:
                        nc.scalar.activation(w1h[:, :, at:at + n], raw[:, :, 0:n], ACT.Copy).then_inc(s_wup, 1)
                    def ffn(g, k_next, i):
                        if i == SLACK:
                            act.wait_ge(s_wadd, k_next * PHASE + (0 if isinstance(k_next, int) else SLACK))
                            act.wait_ge(s_ptr, g * GT)
                            act.wait_ge(s_xsplit, g)
                            nc.scalar.activation(part_t[:, :, :], sums_t[:, :, bass.ds(g * (GT * P), GT * P)],
                                                 ACT.Copy).then_inc(s_part, 1)
                        if i == PREP_AT[1]:
                            ln_root(act, g, ln5)
                            act.wait_ge(s_h, g * NS5)
                            for k in range(GT):
                                act.wait_ge(ln5.tr, g * GT + k + 1)
                                nc.scalar.activation(xnt[:, :, k * P:(k + 1) * P], transposed(k),
                                                     ACT.Copy).then_inc(ln5.xt, 1)
                            act.wait_ge(ln5.xt, g * GT + GT)
                            nc.scalar.activation(xnh[:, :, :], xnt[:, :, :], ACT.Copy).then_inc(s_xup, 1)
                        if i == PREP_AT[4]:
                            act.wait_ge(s_used, g * NS5)
                            for k in range(GT):
                                act.wait_ge(s_ohtr, g * GT + k + 1)
                                nc.scalar.activation(ohT[:, k * P:(k + 1) * P], bank[k % 2][0:EXPERTS1, 0:P],
                                                     ACT.Copy)
                                nc.scalar.activation(ohTb[:, k * P:(k + 1) * P], bank[k % 2][0:EXPERTS1, 0:P],
                                                     ACT.Copy).then_inc(s_oht, 1)
                        for j in steps_at(i):
                            si, q = STEPS5[j]
                            n = SUBS[si][1] * P
                            act.wait_ge(s_h, g * NS5 + j + 1)
                            if j >= 2:
                                act.wait_ge(s_hm, g * NS5 + j - 1)
                            nc.scalar.activation(hr[:, j % 2, 0:n], bank[0 + j % 2][:, 0:n], ACT.Relu,
                                                 bias=b1s[:, q:q + 1]).then_inc(s_r, 1)

                    phases(act, lambda k, i: None, ffn)

            @block.tensor
            def _(pe):
                with pe.If(pe.value_load(apart[:, :], min_val=0, max_val=1) == 0):
                    def ready():
                        pe.wait_ge(s_wt, 128)
                        pe.wait_ge(s_selc, 2)
                        pe.wait_ge(s_wsplit, 3)

                    def edges(k, i):
                        g = k * PHASE + i
                        pe.wait_ge(s_got[i % RING], (k * (PHASE // RING) + i // RING + 1) * (16 * U))
                        pe.wait_ge(s_sw, g * U + U)
                        if i >= 2 or not isinstance(k, int):
                            pe.wait_ge(s_wadd, g - 1)
                        for f in range(F):
                            for u in range(U):
                                last = nc.tensor.matmul(bank[6 + i % 2][:, f * SPAN:(f + 1) * SPAN],
                                                        got[:, i % RING, u, f * P:(f + 1) * P], sw[:, i % 2, u, :],
                                                        start=(u == 0), stop=(u == U - 1))
                        last.then_inc(s_prod, 1)

                    def exact(outp, hi_l, lo_l, hi_r, lo_r, first, last):
                        nc.tensor.matmul(outp, hi_l, hi_r, start=first, stop=False)
                        nc.tensor.matmul(outp, lo_l, hi_r, start=False, stop=False)
                        return nc.tensor.matmul(outp, hi_l, lo_r, start=False, stop=last)

                    def hidden(g, j):
                        si, q = STEPS5[j]
                        k0, w = SUBS[si]
                        n = w * P
                        if j >= 2:
                            pe.wait_ge(s_r, g * NS5 + j - 1)
                        for f in range(F):
                            last = exact(bank[j % 2][:, 0:n], w1h[:, f, q * P:(q + 1) * P],
                                         w1l[:, f, q * P:(q + 1) * P], xnh[:, f, k0 * P:k0 * P + n],
                                         xnl[:, f, k0 * P:k0 * P + n], f == 0, f == F - 1)
                        last.then_inc(s_h, 1)
                        if j >= 2:
                            pe.wait_ge(s_hm, g * NS5 + j - 1)
                        nc.tensor.matmul(bank[2 + j % 2][:, 0:n], sel[:, q * P:(q + 1) * P],
                                         ohTb[:, k0 * P:k0 * P + n], start=True, stop=True).then_inc(s_m, 1)

                    def outputs(g, j):
                        si, q = STEPS5[j]
                        k0, w = SUBS[si]
                        if q == 0:
                            pe.wait_ge(s_y, g * GT + k0)
                            for k in range(w):
                                nc.tensor.matmul(output_tile(k), ohT[:, (k0 + k) * P:(k0 + k + 1) * P], b2s[:, :],
                                                 start=(k % 2 == 0), stop=False, skip_group_check=True)
                        pe.wait_ge(s_hm, g * NS5 + j + 1)
                        for k in range(w):
                            last = nc.tensor.matmul(output_tile(k), hm[j % 2][:, k * P:(k + 1) * P], w2s[:, q, :],
                                                    start=False, stop=(q == PAIRS - 1), skip_group_check=True)
                        last.then_inc(s_used, 1)

                    def ffn(g, k_next, i):
                        if i == PREP_AT[1]:
                            pe.wait_ge(s_r, g * NS5)
                            pe.wait_ge(s_part, g + 1)
                            for k in range(GT):
                                if k >= 2:
                                    pe.wait_ge(s_acc, g * GT + k - 1)
                                for f in range(F):
                                    last = nc.tensor.transpose(bank[k % 2][:, f * P:(f + 1) * P],
                                                               part_t[:, f, k * P:(k + 1) * P], ident[:, :])
                                last.then_inc(s_ptr, 1)
                        if i == PREP_AT[3]:
                            pe.wait_ge(s_acc, g * GT + GT)
                            ln_transpose(pe, g, ln5)
                            pe.wait_ge(s_hm, g * NS5)
                            for k in range(GT):
                                pe.wait_ge(ln5.xt, g * GT + k + 1)
                                for f in range(F):
                                    last = nc.tensor.matmul(bank[2][:, k * EXPERTS1:(k + 1) * EXPERTS1],
                                                            xnt[:, f, k * P:(k + 1) * P], rws[:, f, :],
                                                            start=(f == 0), stop=(f == F - 1))
                            last.then_inc(s_log, 1)
                        if i == PREP_AT[5]:
                            for k in range(GT):
                                pe.wait_ge(s_oh, g * GT + k + 1)
                                if k >= 2:
                                    pe.wait_ge(s_oht, g * GT + k - 1)
                                nc.tensor.transpose(bank[k % 2][0:EXPERTS1, 0:P], oh[:, k, :],
                                                    ident[:, :]).then_inc(s_ohtr, 1)
                            pe.wait_ge(s_oht, g * GT + GT)
                            pe.wait_ge(s_xsplit, g + 1)
                            hidden(g, 0)
                        for j in steps_at(i):
                            if j + 1 < NS5:
                                hidden(g, j + 1)
                            outputs(g, j)

                    phases(pe, edges, ffn, ready)

            @block.vector
            def _(dve):
                with dve.If(dve.value_load(apart[:, :], min_val=0, max_val=1) == 0):
                    nc.vector.tensor_copy(gidx[0][:, :], src_f[:, 0:HALF]).then_inc(s_gidx, 1)
                    nc.vector.memset(sums_t[:, :, :], 0.0).then_inc(s_clear, 1)

                    def ready():
                        dve.wait_ge(s_wt, 128)
                        dve.wait_ge(s_sel, 3)
                        nc.vector.tensor_copy(sel[:, :], sel_f[:, :]).then_inc(s_selc, 1)
                        nc.vector.tensor_copy(io_f[:, :], io_i[:, :]).then_inc(s_selc, 1)
                        dve.wait_ge(s_wup, 3)
                        for at, n, raw in PIECES:
                            nc.vector.tensor_tensor(w1l[:, :, at:at + n], raw[:, :, 0:n],
                                                    w1h[:, :, at:at + n].bitcast(F32), ALU.subtract).then_inc(s_wsplit, 1)
                        dve.wait_ge(s_selc, 2)

                    def add_window(g, static_first=False):
                        start = dve.value_load(win_i[0:1, bass.ds(g, 1)], min_val=0, max_val=N_NODES - 1)
                        window = sums_t[:, :, bass.ds(start, SPAN)]
                        if static_first:
                            dve.wait_ge(s_clear, 1)
                        else:
                            dve.wait_ge(s_wadd, g)
                        dve.wait_ge(s_prod, g + 1)
                        nc.vector.tensor_tensor(window, bank[6 + g_parity[0]][:, 0:F * SPAN].rearrange("p (f n) -> p f n", f=F),
                                                window, ALU.add).then_inc(s_wadd, 1)

                    g_parity = [0]

                    def edges(k, i):
                        g = k * PHASE + i
                        if i >= 2 or not isinstance(k, int):
                            dve.wait_ge(s_prod, g - 1)
                        for u in range(U):
                            col = g * U + u
                            nc.vector.tensor_scalar(sw[:, i % 2, u, :], iota_w[:, :], rel_f[:, bass.ds(col, 1)],
                                                    wgt_f[:, bass.ds(col, 1)], ALU.is_equal, ALU.mult).then_inc(s_sw, 1)
                        if i >= 1 or not isinstance(k, int):
                            g_parity[0] = (i - 1) % 2
                            add_window(g - 1, static_first=isinstance(k, int) and i == 1)
                        if i == 2:
                            nc.vector.tensor_copy(gidx[1][:, :], src_f[:, bass.ds(k * (2 * HALF) + HALF, HALF)]).then_inc(s_gidx, 1)
                        if i == PHASE // 2 + 2:
                            nc.vector.tensor_copy(gidx[0][:, :], src_f[:, bass.ds(k * (2 * HALF) + 2 * HALF, HALF)]).then_inc(s_gidx, 1)

                    def finish(g, si):
                        k0, w = SUBS[si]
                        for k in range(w):
                            if k == 0:
                                dve.wait_ge(s_used, g * NS5 + PAIRS * (si + 1))
                            nc.vector.scalar_tensor_tensor(yb[:, k0 + k, :], output_tile(k), 0.0,
                                                           acc[:, k0 + k, :], ALU.max, ALU.add).then_inc(s_y, 1)

                    def ffn(g, k_next, i):
                        if i == 0 and isinstance(g, int):
                            g_parity[0] = 1
                            add_window(EGROUPS - 1)
                        if i == PREP_AT[1]:
                            dve.wait_ge(s_accin, g * 16 + 16)
                            for k in range(GT):
                                dve.wait_ge(s_ptr, g * GT + k + 1)
                                nc.vector.tensor_tensor(acc[:, k, :], bank[k % 2][:, 0:D], acc[:, k, :],
                                                        ALU.add).then_inc(s_acc, 1)
                        if i == PREP_AT[2]:
                            dve.wait_ge(s_acc, g * GT + GT)
                            ln_vector(dve, g, ln5)
                        if i == PREP_AT[4]:
                            dve.wait_ge(s_log, g + 1)
                            nc.vector.tensor_tensor(lg[:, :, :],
                                                    bank[2][:, 0:GT * EXPERTS1].rearrange("p (k e) -> p k e", k=GT),
                                                    rbs[:, :].unsqueeze(1).broadcast_to([P, GT, EXPERTS1]),
                                                    ALU.add).then_inc(s_lg, 1)
                            wait_apart(dve, s_lg, g + 1)
                            for k in range(GT):
                                nc.vector.max(mx[:, k, :], lg[:, k, :]).then_inc(s_mx, 1)
                            for k in range(GT):
                                wait_apart(dve, s_mx, g * GT + k + 1)
                                nc.vector.max_index(mi[:, k, :], mx[:, k, :], lg[:, k, :]).then_inc(s_mi, 1)
                            dve.wait_ge(s_mi, g * GT + GT)
                            nc.vector.tensor_copy(mf[:, :], mi[:, :, 0]).then_inc(s_mf, 1)
                            dve.wait_ge(s_mf, g + 1)
                            for k in range(GT):
                                nc.vector.tensor_scalar(oh[:, k, :], io_f[:, :], mf[:, k:k + 1], None,
                                                        ALU.is_equal).then_inc(s_oh, 1)
                            dve.wait_ge(s_xup, g + 1)
                            nc.vector.tensor_tensor(xnl[:, :, :], xnt[:, :, :], xnh[:, :, :].bitcast(F32),
                                                    ALU.subtract).then_inc(s_xsplit, 1)
                            dve.wait_ge(s_st, g * 16)
                        for j in steps_at(i):
                            si, q = STEPS5[j]
                            if q == 1 and si:
                                finish(g, si - 1)
                            n = SUBS[si][1] * P
                            dve.wait_ge(s_r, g * NS5 + j + 1)
                            dve.wait_ge(s_m, g * NS5 + j + 1)
                            if j >= 2:
                                dve.wait_ge(s_used, g * NS5 + j - 1)
                            nc.vector.tensor_tensor(hm[j % 2][:, 0:n], bank[2 + j % 2][:, 0:n], hr[:, j % 2, 0:n],
                                                    ALU.mult).then_inc(s_hm, 1)
                        if i == PHASE - 1:
                            finish(g, len(SUBS) - 1)

                    phases(dve, edges, ffn, ready)

        both = borrowed(pair1)
        both.__enter__()
        edge_block(1, src_f, dst_f, dst)

        with ExitStack() as c5, nc.Block() as block:
            def sb5(name, shape, dt=F32):
                return c5.enter_context(nc.sbuf_tensor(name, shape, dt))
            ln5 = LN("ln5")
            tb5 = Tables("m")
            s_wt = sem("m_wt")
            s_sel = sem("m_sel")
            s_selc = sem("m_selc")
            s_log = sem("m_log")
            s_lg = sem("m_lg")
            s_mx = sem("m_mx")
            s_mi = sem("m_mi")
            s_mf = sem("m_mf")
            s_oh = sem("m_oh")
            s_ohtr = sem("m_ohtr")
            s_oht = sem("m_oht")
            s_h = sem("m_h")
            s_m = sem("m_m")
            s_r = sem("m_r")
            s_hm = sem("m_hm")
            s_used = sem("m_used")
            s_y = sem("m_y")
            s_st = sem("m_st")
            w1s = sb5("w1s", [P, F, EXPERTS1 * HID1])
            w2s = sb5("w2s", [P, PAIRS, D])
            b1s = sb5("b1s", [P, PAIRS])
            b2s = sb5("b2s", [EXPERTS1, D])
            b2u = sb5("b2u", [EXPERTS1, D])
            rws = sb5("rws", [P, F, EXPERTS1])
            rbs = sb5("rbs", [P, EXPERTS1])
            io_i = sb5("io_i", [P, EXPERTS1], I32)
            io_f = sb5("io_f", [P, EXPERTS1])
            sel_f = sb5("sel_f", [EXPERTS1, PAIRS * P])
            sel = sb5("sel", [EXPERTS1, PAIRS * P], BF16)
            xnt = sb5("xnt5", [P, F, GT * P])
            lg = sb5("lg", [P, GT, EXPERTS1])
            mx = sb5("mx", [P, GT, 8])
            mi = sb5("mi", [P, GT, 8], U32)
            mf = sb5("mf", [P, GT])
            oh = sb5("oh", [P, GT, EXPERTS1])
            ohT = sb5("ohT", [EXPERTS1, GT * P])
            ohTb = sb5("ohTb", [EXPERTS1, GT * P], BF16)
            hr = sb5("hr", [P, 2, W4])
            hm = [sb5(f"hm{i}", [P, W4]) for i in range(2)]
            yb = sb5("yb", [P, GT, D])
            STEPS5 = [(si, q) for si in range(len(SUBS)) for q in range(PAIRS)]
            NS5 = len(STEPS5)

            @block.gpsimd
            def _(pool):
                with pool.If(pool.value_load(apart[:, :], min_val=0, max_val=1) == 1):
                    nc.gpsimd.iota(io_i[:, :], pattern=[[1, EXPERTS1]], base=0, channel_multiplier=0).then_inc(s_sel, 1)
                    nc.gpsimd.memset(sel_f[:, :], 0.0).then_inc(s_sel, 1)
                    pool.wait_ge(s_sel, 2)
                    v = sel_f[:, :].rearrange("e (x h) -> e x h", h=HID1)
                    nc.gpsimd.affine_select(out=v, in_=v, compare_op=ALU.not_equal, fill=1.0, base=0,
                                            pattern=[[-1, EXPERTS1], [0, HID1]], channel_multiplier=1).then_inc(s_sel, 1)

            @block.sync
            def _(sp):
                with sp.If(sp.value_load(apart[:, :], min_val=0, max_val=1) == 1):
                    sp.dma_start(w1s[:, :, :], mw1.rearrange("(f p) n -> p f n", p=P)).then_inc(s_wt, 16)
                    sp.dma_start(w2s[:, :, :], mw2.rearrange("(q p) d -> p q d", p=P)).then_inc(s_wt, 16)
                    sp.dma_start(b1s[:, :], mb1).then_inc(s_wt, 16)
                    sp.dma_start(b2s[:, :], mb2).then_inc(s_wt, 16)
                    sp.dma_start(rws[:, :, :], rw.rearrange("(f p) e -> p f e", p=P)).then_inc(s_wt, 16)
                    sp.dma_start(rbs[:, :], rb.partition_broadcast(P)).then_inc(s_wt, 16)
                    with sp.Fori(0, GROUPS) as g:
                        def acc_free():
                            wait_apart(sp, s_y, g * GT)
                        tables_load(sp, g, tb5, 1, acc_free)
                        wait_apart(sp, s_y, g * GT + GT)
                        sp.dma_start(node_rows(out, g), yb[:, :, :]).then_inc(s_st, 16)
                    sp.wait_ge(s_st, 16 * GROUPS)

            @block.scalar
            def _(act):
                with act.If(act.value_load(apart[:, :], min_val=0, max_val=1) == 1):
                    act.wait_ge(s_wt, 96)
                    with act.Fori(0, GROUPS) as g:
                        ln_root(act, g, ln5)
                        act.wait_ge(s_h, g * NS5)
                        for k in range(GT):
                            act.wait_ge(ln5.tr, g * GT + k + 1)
                            nc.scalar.activation(xnt[:, :, k * P:(k + 1) * P], transposed(k), ACT.Copy).then_inc(ln5.xt, 1)
                        act.wait_ge(s_used, g * NS5)
                        for k in range(GT):
                            act.wait_ge(s_ohtr, g * GT + k + 1)
                            nc.scalar.activation(ohT[:, k * P:(k + 1) * P], bank[k % 2][0:EXPERTS1, 0:P],
                                                 ACT.Copy)
                            nc.scalar.activation(ohTb[:, k * P:(k + 1) * P], bank[k % 2][0:EXPERTS1, 0:P],
                                                 ACT.Copy).then_inc(s_oht, 1)
                        for j, (si, q) in enumerate(STEPS5):
                            n = SUBS[si][1] * P
                            act.wait_ge(s_h, g * NS5 + j + 1)
                            if j >= 2:
                                act.wait_ge(s_hm, g * NS5 + j - 1)
                            nc.scalar.activation(hr[:, j % 2, 0:n], bank[0 + j % 2][:, 0:n], ACT.Relu,
                                                 bias=b1s[:, q:q + 1]).then_inc(s_r, 1)

            @block.tensor
            def _(pe):
                with pe.If(pe.value_load(apart[:, :], min_val=0, max_val=1) == 1):
                    pe.wait_ge(s_wt, 96)
                    pe.wait_ge(s_selc, 2)
                    with pe.Fori(0, GROUPS) as g:
                        pe.wait_ge(s_r, g * NS5)
                        ln_transpose(pe, g, ln5)
                        pe.wait_ge(s_hm, g * NS5)
                        for k in range(GT):
                            pe.wait_ge(ln5.xt, g * GT + k + 1)
                            for f in range(F):
                                last = nc.tensor.matmul(bank[2][:, k * EXPERTS1:(k + 1) * EXPERTS1],
                                                        xnt[:, f, k * P:(k + 1) * P], rws[:, f, :],
                                                        start=(f == 0), stop=(f == F - 1))
                        last.then_inc(s_log, 1)
                        for k in range(GT):
                            pe.wait_ge(s_oh, g * GT + k + 1)
                            if k >= 2:
                                pe.wait_ge(s_oht, g * GT + k - 1)
                            nc.tensor.transpose(bank[k % 2][0:EXPERTS1, 0:P], oh[:, k, :], ident[:, :]).then_inc(s_ohtr, 1)
                        pe.wait_ge(s_oht, g * GT + GT)

                        def hidden(j):
                            si, q = STEPS5[j]
                            k0, w = SUBS[si]
                            n = w * P
                            if j >= 2:
                                pe.wait_ge(s_r, g * NS5 + j - 1)
                            for f in range(F):
                                last = nc.tensor.matmul(bank[j % 2][:, 0:n], w1s[:, f, q * P:(q + 1) * P],
                                                        xnt[:, f, k0 * P:k0 * P + n], start=(f == 0), stop=(f == F - 1))
                            last.then_inc(s_h, 1)
                            if j >= 2:
                                pe.wait_ge(s_hm, g * NS5 + j - 1)
                            nc.tensor.matmul(bank[2 + j % 2][:, 0:n], sel[:, q * P:(q + 1) * P],
                                             ohTb[:, k0 * P:k0 * P + n], start=True, stop=True).then_inc(s_m, 1)

                        def outputs(j):
                            si, q = STEPS5[j]
                            k0, w = SUBS[si]
                            if q == 0:
                                pe.wait_ge(s_y, g * GT + k0)
                                for k in range(w):
                                    nc.tensor.matmul(bank[4 + k][:, 0:D], ohT[:, (k0 + k) * P:(k0 + k + 1) * P], b2s[:, :],
                                                     start=True, stop=False)
                            pe.wait_ge(s_hm, g * NS5 + j + 1)
                            for k in range(w):
                                last = nc.tensor.matmul(bank[4 + k][:, 0:D], hm[j % 2][:, k * P:(k + 1) * P], w2s[:, q, :],
                                                        start=False, stop=(q == PAIRS - 1))
                            last.then_inc(s_used, 1)

                        hidden(0)
                        for j in range(NS5):
                            if j + 1 < NS5:
                                hidden(j + 1)
                            outputs(j)

            @block.vector
            def _(dve):
                with dve.If(dve.value_load(apart[:, :], min_val=0, max_val=1) == 1):
                    dve.wait_ge(s_wt, 96)
                    dve.wait_ge(s_sel, 3)
                    nc.vector.tensor_copy(sel[:, :], sel_f[:, :]).then_inc(s_selc, 1)
                    nc.vector.tensor_copy(io_f[:, :], io_i[:, :]).then_inc(s_selc, 1)
                    dve.wait_ge(s_selc, 2)
                    with dve.Fori(0, GROUPS) as g:
                        tables_add(dve, g, tb5, 1)
                        ln_vector(dve, g, ln5)
                        dve.wait_ge(s_log, g + 1)
                        nc.vector.tensor_tensor(lg[:, :, :], bank[2][:, 0:GT * EXPERTS1].rearrange("p (k e) -> p k e", k=GT),
                                                rbs[:, :].unsqueeze(1).broadcast_to([P, GT, EXPERTS1]),
                                                ALU.add).then_inc(s_lg, 1)
                        wait_apart(dve, s_lg, g + 1)
                        for k in range(GT):
                            nc.vector.max(mx[:, k, :], lg[:, k, :]).then_inc(s_mx, 1)
                        for k in range(GT):
                            wait_apart(dve, s_mx, g * GT + k + 1)
                            nc.vector.max_index(mi[:, k, :], mx[:, k, :], lg[:, k, :]).then_inc(s_mi, 1)
                        dve.wait_ge(s_mi, g * GT + GT)
                        nc.vector.tensor_copy(mf[:, :], mi[:, :, 0]).then_inc(s_mf, 1)
                        dve.wait_ge(s_mf, g + 1)
                        for k in range(GT):
                            nc.vector.tensor_scalar(oh[:, k, :], io_f[:, :], mf[:, k:k + 1], None,
                                                    ALU.is_equal).then_inc(s_oh, 1)

                        def finish(si):
                            k0, w = SUBS[si]
                            for k in range(w):
                                if k == 0:
                                    dve.wait_ge(s_used, g * NS5 + PAIRS * (si + 1))
                                nc.vector.scalar_tensor_tensor(yb[:, k0 + k, :], bank[4 + k][:, 0:D], 0.0,
                                                               acc[:, k0 + k, :], ALU.max, ALU.add).then_inc(s_y, 1)

                        dve.wait_ge(s_st, g * 16)
                        for j, (si, q) in enumerate(STEPS5):
                            if q == 1 and si:
                                finish(si - 1)
                            n = SUBS[si][1] * P
                            dve.wait_ge(s_r, g * NS5 + j + 1)
                            dve.wait_ge(s_m, g * NS5 + j + 1)
                            if j >= 2:
                                dve.wait_ge(s_used, g * NS5 + j - 1)
                            nc.vector.tensor_tensor(hm[j % 2][:, 0:n], bank[2 + j % 2][:, 0:n], hr[:, j % 2, 0:n],
                                                    ALU.mult).then_inc(s_hm, 1)
                        finish(len(SUBS) - 1)
        both.__exit__(None, None, None)


INS = ["x", "src", "dst", "wgt", "wl", "wr", "bl", "br", "gw", "gbr",
       "w1", "b1", "g1", "be1", "m1", "v1", "w2", "b2", "g2", "be2", "m2", "v2", "wo", "bo",
       "lw", "lb", "rw", "rb", "mw1", "mb1", "mw2", "mb2"]


def kernel(x, src, dst, edge_weight, L0_gnn_weight_l, L0_gnn_bias_l, L0_gnn_weight_r, L0_gnn_bias_r,
           L0_ffn_Wr, L0_ffn_br, L0_ffn_W1, L0_ffn_b1, L0_ffn_g1, L0_ffn_be1, L0_ffn_m1, L0_ffn_v1,
           L0_ffn_W2, L0_ffn_b2, L0_ffn_g2, L0_ffn_be2, L0_ffn_m2, L0_ffn_v2, L0_ffn_Wo, L0_ffn_bo,
           L1_gnn_weight, L1_gnn_bias, L1_ffn_router_w, L1_ffn_router_b, L1_ffn_W1, L1_ffn_b1,
           L1_ffn_W2, L1_ffn_b2):
    import concourse.bacc as bacc
    from concourse.bass_utils import run_bass_kernel_spmd

    def padded(a, rows):
        a = np.asarray(a)
        return np.concatenate([a, np.zeros((rows - a.shape[0],) + a.shape[1:], a.dtype)])

    def repeated(a, rows):
        a = np.asarray(a)
        return np.concatenate([a, np.repeat(a[-1:], rows - a.shape[0])])

    def features_first(a):
        return np.asarray(a).reshape(EXPERTS0, F, P).transpose(2, 0, 1)

    arrays = [
        padded(x, ROWS), padded(src, E_PAD), repeated(dst, E_PAD), padded(edge_weight, E_PAD),
        L0_gnn_weight_l, L0_gnn_weight_r, L0_gnn_bias_l, L0_gnn_bias_r, L0_ffn_Wr, L0_ffn_br,
        L0_ffn_W1, *(features_first(a) for a in (L0_ffn_b1, L0_ffn_g1, L0_ffn_be1, L0_ffn_m1, L0_ffn_v1)),
        L0_ffn_W2, *(features_first(a) for a in (L0_ffn_b2, L0_ffn_g2, L0_ffn_be2, L0_ffn_m2, L0_ffn_v2)),
        L0_ffn_Wo, L0_ffn_bo, L1_gnn_weight, L1_gnn_bias,
        np.asarray(L1_ffn_router_w).transpose(1, 0), L1_ffn_router_b,
        np.asarray(L1_ffn_W1).transpose(1, 0, 2).reshape(D, EXPERTS1 * HID1),
        np.asarray(L1_ffn_b1).reshape(PAIRS, P).transpose(1, 0),
        np.asarray(L1_ffn_W2).reshape(EXPERTS1 * HID1, D), L1_ffn_b2,
    ]
    nc = bacc.Bacc("TRN2", target_bir_lowering=False, num_devices=1)
    feeds, args = {}, []
    for name, a in zip(INS, arrays):
        a = np.ascontiguousarray(a)
        feeds[f"in_{name}"] = a
        args.append(nc.dram_tensor(f"in_{name}", a.shape, mybir.dt.from_np(a.dtype), kind="ExternalInput").ap())
    out = nc.dram_tensor("out_rows", (ROWS, D), F32, kind="ExternalOutput").ap()
    build(nc, *args, out)
    r = run_bass_kernel_spmd(nc, [feeds], core_ids=[0])
    return r.results[0]["out_rows"][:N_NODES]
```
